# Optimizing a Trainium2 kernel written in Bass

```python
import numpy as np
import jax
import jax.numpy as jnp

def _softmax(x, axis=-1):
    return jax.nn.softmax(x, axis=axis)

def _gelu(x):
    return jax.nn.gelu(x, approximate=True)

def _silu(x):
    return jax.nn.silu(x)

def _sigmoid(x):
    return jax.nn.sigmoid(x)

def _layernorm(x, axis=-1, eps=1e-05):
    m = jnp.mean(x, axis=axis, keepdims=True)
    v = jnp.var(x, axis=axis, keepdims=True)
    return (x - m) / jnp.sqrt(v + eps)

def _scatter_add(tgt, idx, src, axis=0):
    return tgt.at[idx].add(src)

def _segment_sum(src, seg, n):
    return jax.ops.segment_sum(src, seg, n)
kernel_name = 'mk_flamingo_gated_d2_seqx_r4_119c44'

def setup_inputs(seed: int=0):
    np.random.seed(seed)
    _w = jnp.asarray

    def _rec_inputs():
        import jax
        import jax.numpy as jnp
        _rk = jax.random.key(seed)
        x = -0.0003929 + 0.9999 * jax.random.normal(jax.random.fold_in(_rk, 1), (4, 512, 256), jnp.float32)
        _lenS = 512 - jax.random.randint(jax.random.fold_in(_rk, 7), (4,), 0, max(1, 512 // 4) + 1, jnp.int32)
        _lenS2 = 1601 - jax.random.randint(jax.random.fold_in(_rk, 8), (4,), 0, max(1, 1601 // 4) + 1, jnp.int32)
        _ctx_1024P = jax.random.normal(jax.random.fold_in(_rk, 11), (4, 16, 256), jnp.float32)
        _ctx_1024c = jax.random.dirichlet(jax.random.fold_in(_rk, 511), 0.3 * jnp.ones((16,), jnp.float32), (4, 1601))
        _ctx_1024t = jnp.einsum('bsk,bkd->bsd', _ctx_1024c, _ctx_1024P)
        _ctx_1024t = _ctx_1024t * jax.lax.rsqrt(jnp.mean(jnp.square(_ctx_1024t)) + 1e-12) * 0.953939
        ctx_1024 = 4.13588e-05 + 0.999923 * (_ctx_1024t + 0.3 * jax.random.normal(jax.random.fold_in(_rk, 611), (4, 1601, 256), jnp.float32))
        _g = jax.random.normal(jax.random.fold_in(_rk, 9001), (2, 2), jnp.float32)
        _g = jnp.sign(_g) * jnp.maximum(jnp.abs(_g), 1.0) + (_g == 0) * 1.0
        g_xattn = _g[0]
        g_ffn = _g[1]
        return (x, ctx_1024, g_xattn, g_ffn)
    x, ctx_1024, g_xattn, g_ffn = _rec_inputs()

    def _L0_xattn_setup():
        import jax, jax.numpy as jnp
        import numpy as np
        H = 256
        B = 8
        L_CHAR = 512
        L_SUB = 256

        def _linear(x, W, b):
            return jnp.einsum('blh,oh->blo', x, W) + b

        def _interp_linear(x, out_len):
            L_in = x.shape[1]
            pos = (jnp.arange(out_len, dtype=x.dtype) + 0.5) * (L_in / out_len) - 0.5
            pos = jnp.clip(pos, 0.0, L_in - 1)
            lo = jnp.floor(pos).astype(jnp.int32)
            hi = jnp.minimum(lo + 1, L_in - 1)
            w = (pos - lo.astype(x.dtype))[None, :, None]
            return x[:, lo] * (1 - w) + x[:, hi] * w
        key = jax.random.key(seed)
        ks = jax.random.split(key, 18)
        s = 0.02
        inp = {'char_emb': jax.random.normal(ks[0], (B, L_CHAR, H), jnp.float32), 'subword_emb': jax.random.normal(ks[1], (B, L_SUB, H), jnp.float32)}
        names = ['Wq_c', 'Wk_s', 'Wv_s', 'Wq_s', 'Wk_c', 'Wv_c']
        for i, n in enumerate(names):
            inp[n] = jax.random.normal(ks[2 + 2 * i], (H, H), jnp.float32) * s
            inp['b' + n[1:]] = jax.random.normal(ks[3 + 2 * i], (H,), jnp.float32) * s
        inp['Wg'] = jax.random.normal(ks[14], (H, 2 * H), jnp.float32) * s
        inp['bg'] = jax.random.normal(ks[15], (H,), jnp.float32) * s
        return inp
    _L0_xattn_all = _L0_xattn_setup()
    _L0_xattn_in = {k: v for k, v in _L0_xattn_all.items() if k in ('Wq_c', 'bq_c', 'Wk_s', 'bk_s', 'Wv_s', 'bv_s', 'Wq_s', 'bq_s', 'Wk_c', 'bk_c', 'Wv_c', 'bv_c', 'Wg', 'bg')}
    del _L0_xattn_all

    def _L0_ffn_setup():
        import jax, jax.numpy as jnp
        import numpy as np
        B, S, D = (2, 1024, 256)
        H = 1024
        E = 8
        K = 4
        key = jax.random.key(seed)
        kx, kr, ku, kd = jax.random.split(key, 4)
        x = jax.random.normal(kx, (B, S, D), dtype=jnp.float32)
        router_w = jax.random.normal(kr, (D, E), dtype=jnp.float32) / np.sqrt(D)
        up_w = jax.random.normal(ku, (E, D, H), dtype=jnp.float32) / np.sqrt(D)
        down_w = jax.random.normal(kd, (E, H, D), dtype=jnp.float32) / np.sqrt(H)
        return {'x': x, 'router_w': router_w, 'up_w': up_w, 'down_w': down_w}
    _L0_ffn_all = _L0_ffn_setup()
    _L0_ffn_in = {k: v for k, v in _L0_ffn_all.items() if k in ('router_w', 'up_w', 'down_w')}
    del _L0_ffn_all

    def _L1_xattn_setup():
        import jax, jax.numpy as jnp
        import numpy as np
        C = 256
        B, SQ, SKV = (4, 512, 512)
        key = jax.random.key(seed)
        ks = jax.random.split(key, 10)
        s = 1.0 / np.sqrt(C)
        return {'x': jax.random.normal(ks[0], (B, SQ, C), jnp.float32), 'content_embeddings': jax.random.normal(ks[1], (B, SKV, C), jnp.float32), 'Wq': jax.random.normal(ks[2], (C, C), jnp.float32) * s, 'bq': jnp.zeros((C,), jnp.float32), 'Wk': jax.random.normal(ks[3], (C, C), jnp.float32) * s, 'bk': jnp.zeros((C,), jnp.float32), 'Wv': jax.random.normal(ks[4], (C, C), jnp.float32) * s, 'bv': jnp.zeros((C,), jnp.float32), 'Wo': jax.random.normal(ks[5], (C, C), jnp.float32) * s, 'bo': jnp.zeros((C,), jnp.float32)}
    _L1_xattn_all = _L1_xattn_setup()
    _L1_xattn_in = {k: v for k, v in _L1_xattn_all.items() if k in ('Wq', 'bq', 'Wk', 'bk', 'Wv', 'bv', 'Wo', 'bo')}
    del _L1_xattn_all

    def _L1_ffn_setup():
        import jax, jax.numpy as jnp
        import numpy as np
        B, T, D = (2, 512, 256)
        E, K, FF = (8, 2, 1024)

        def _reference_tuple_inner(x, gate_w, gate_b, w1, b1, w2, b2):
            n_experts = w1.shape[0]
            gate_logits = x @ gate_w + gate_b
            topk_vals, topk_idx = jax.lax.top_k(gate_logits, K)
            topk_w = jax.nn.softmax(topk_vals, axis=-1)
            onehot = jax.nn.one_hot(topk_idx, n_experts, dtype=x.dtype)
            comb = jnp.sum(onehot * topk_w[..., None], axis=2)
            h = jax.nn.gelu(jnp.einsum('btd,edf->ebtf', x, w1) + b1[:, None, None, :], approximate=False)
            y = jnp.einsum('ebtf,efd->ebtd', h, w2) + b2[:, None, None, :]
            output = jnp.einsum('ebtd,bte->btd', y, comb)
            expert_counts = jnp.sum(onehot, axis=(0, 1, 2)).astype(jnp.float32)
            return (output, gate_logits, topk_idx, expert_counts)
        key = jax.random.key(seed)
        ks = jax.random.split(key, 4)
        scale = 0.02
        return {'x': jax.random.normal(ks[0], (B, T, D), jnp.float32), 'gate_w': jax.random.normal(ks[1], (D, E), jnp.float32) * scale, 'gate_b': jnp.zeros((E,), jnp.float32), 'w1': jax.random.normal(ks[2], (E, D, FF), jnp.float32) * scale, 'b1': jnp.zeros((E, FF), jnp.float32), 'w2': jax.random.normal(ks[3], (E, FF, D), jnp.float32) * scale, 'b2': jnp.zeros((E, D), jnp.float32)}
    _L1_ffn_all = _L1_ffn_setup()
    _L1_ffn_in = {k: v for k, v in _L1_ffn_all.items() if k in ('gate_w', 'gate_b', 'w1', 'b1', 'w2', 'b2')}
    del _L1_ffn_all
    return {'x': x, 'ctx_1024': ctx_1024, 'g_xattn': g_xattn, 'g_ffn': g_ffn, 'L0_xattn_Wq_c': _L0_xattn_in['Wq_c'], 'L0_xattn_bq_c': _L0_xattn_in['bq_c'], 'L0_xattn_Wk_s': _L0_xattn_in['Wk_s'], 'L0_xattn_bk_s': _L0_xattn_in['bk_s'], 'L0_xattn_Wv_s': _L0_xattn_in['Wv_s'], 'L0_xattn_bv_s': _L0_xattn_in['bv_s'], 'L0_xattn_Wq_s': _L0_xattn_in['Wq_s'], 'L0_xattn_bq_s': _L0_xattn_in['bq_s'], 'L0_xattn_Wk_c': _L0_xattn_in['Wk_c'], 'L0_xattn_bk_c': _L0_xattn_in['bk_c'], 'L0_xattn_Wv_c': _L0_xattn_in['Wv_c'], 'L0_xattn_bv_c': _L0_xattn_in['bv_c'], 'L0_xattn_Wg': _L0_xattn_in['Wg'], 'L0_xattn_bg': _L0_xattn_in['bg'], 'L0_ffn_router_w': _L0_ffn_in['router_w'], 'L0_ffn_up_w': _L0_ffn_in['up_w'], 'L0_ffn_down_w': _L0_ffn_in['down_w'], 'L1_xattn_Wq': _L1_xattn_in['Wq'], 'L1_xattn_bq': _L1_xattn_in['bq'], 'L1_xattn_Wk': _L1_xattn_in['Wk'], 'L1_xattn_bk': _L1_xattn_in['bk'], 'L1_xattn_Wv': _L1_xattn_in['Wv'], 'L1_xattn_bv': _L1_xattn_in['bv'], 'L1_xattn_Wo': _L1_xattn_in['Wo'], 'L1_xattn_bo': _L1_xattn_in['bo'], 'L1_ffn_gate_w': _L1_ffn_in['gate_w'], 'L1_ffn_gate_b': _L1_ffn_in['gate_b'], 'L1_ffn_w1': _L1_ffn_in['w1'], 'L1_ffn_b1': _L1_ffn_in['b1'], 'L1_ffn_w2': _L1_ffn_in['w2'], 'L1_ffn_b2': _L1_ffn_in['b2']}

def reference(x, ctx_1024, g_xattn, g_ffn, L0_xattn_Wq_c, L0_xattn_bq_c, L0_xattn_Wk_s, L0_xattn_bk_s, L0_xattn_Wv_s, L0_xattn_bv_s, L0_xattn_Wq_s, L0_xattn_bq_s, L0_xattn_Wk_c, L0_xattn_bk_c, L0_xattn_Wv_c, L0_xattn_bv_c, L0_xattn_Wg, L0_xattn_bg, L0_ffn_router_w, L0_ffn_up_w, L0_ffn_down_w, L1_xattn_Wq, L1_xattn_bq, L1_xattn_Wk, L1_xattn_bk, L1_xattn_Wv, L1_xattn_bv, L1_xattn_Wo, L1_xattn_bo, L1_ffn_gate_w, L1_ffn_gate_b, L1_ffn_w1, L1_ffn_b1, L1_ffn_w2, L1_ffn_b2):
    import jax
    import jax.numpy as jnp

    def _L0_xattn_ref(char_emb, subword_emb, Wq_c, bq_c, Wk_s, bk_s, Wv_s, bv_s, Wq_s, bq_s, Wk_c, bk_c, Wv_c, bv_c, Wg, bg):
        import jax, jax.numpy as jnp
        import numpy as np
        H = 256
        B = 8
        L_CHAR = 512
        L_SUB = 256

        def _linear(x, W, b):
            return jnp.einsum('blh,oh->blo', x, W) + b

        def _interp_linear(x, out_len):
            L_in = x.shape[1]
            pos = (jnp.arange(out_len, dtype=x.dtype) + 0.5) * (L_in / out_len) - 0.5
            pos = jnp.clip(pos, 0.0, L_in - 1)
            lo = jnp.floor(pos).astype(jnp.int32)
            hi = jnp.minimum(lo + 1, L_in - 1)
            w = (pos - lo.astype(x.dtype))[None, :, None]
            return x[:, lo] * (1 - w) + x[:, hi] * w
        h = char_emb.shape[-1]
        scale = 1.0 / jnp.sqrt(jnp.asarray(h, char_emb.dtype))
        Q_char = _linear(char_emb, Wq_c, bq_c)
        K_sub = _linear(subword_emb, Wk_s, bk_s)
        V_sub = _linear(subword_emb, Wv_s, bv_s)
        scores = jnp.einsum('bqh,bkh->bqk', Q_char, K_sub) * scale
        char2sub = jnp.einsum('bqk,bkh->bqh', jax.nn.softmax(scores, axis=-1), V_sub)
        Q_sub = _linear(subword_emb, Wq_s, bq_s)
        K_char = _linear(char_emb, Wk_c, bk_c)
        V_char = _linear(char_emb, Wv_c, bv_c)
        scores2 = jnp.einsum('bqh,bkh->bqk', Q_sub, K_char) * scale
        sub2char = jnp.einsum('bqk,bkh->bqh', jax.nn.softmax(scores2, axis=-1), V_char)
        L_char = char_emb.shape[1]
        if sub2char.shape[1] != L_char:
            sub2char = _interp_linear(sub2char, L_char)
        gate_in = jnp.concatenate([char2sub, sub2char], axis=-1)
        gate = jax.nn.sigmoid(jnp.einsum('blh,oh->blo', gate_in, Wg) + bg)
        return gate * char2sub + (1 - gate) * sub2char

    def _L0_ffn_ref(x, router_w, up_w, down_w):
        import jax, jax.numpy as jnp
        import numpy as np
        B, S, D = (2, 1024, 256)
        H = 1024
        E = 8
        K = 4
        router_logits = jnp.einsum('bsd,de->bse', x, router_w)
        routing_weights = jax.nn.softmax(router_logits, axis=-1)
        topk_weights, topk_indices = jax.lax.top_k(routing_weights, K)
        topk_weights = topk_weights / jnp.sum(topk_weights, axis=-1, keepdims=True)
        h = jnp.einsum('bsd,edh->bseh', x, up_w)
        h = jax.nn.gelu(h)
        expert_outputs = jnp.einsum('bseh,ehd->bsed', h, down_w)
        gathered = jnp.take_along_axis(expert_outputs, topk_indices[:, :, :, None], axis=2)
        output = jnp.sum(topk_weights[:, :, :, None] * gathered, axis=2)
        return output

    def _L1_xattn_ref(x, content_embeddings, Wq, bq, Wk, bk, Wv, bv, Wo, bo):
        import jax, jax.numpy as jnp
        import numpy as np
        C = 256
        B, SQ, SKV = (4, 512, 512)
        queries = x @ Wq.T + bq
        keys = content_embeddings @ Wk.T + bk
        values = content_embeddings @ Wv.T + bv
        scale = 1.0 / jnp.sqrt(jnp.asarray(C, x.dtype))
        scores = jnp.einsum('bqc,bkc->bqk', queries, keys) * scale
        attn = jax.nn.softmax(scores, axis=-1)
        attended = jnp.einsum('bqk,bkc->bqc', attn, values)
        out = x + attended
        return out @ Wo.T + bo

    def _L1_ffn_ref(x, gate_w, gate_b, w1, b1, w2, b2):
        import jax, jax.numpy as jnp
        import numpy as np
        B, T, D = (2, 512, 256)
        E, K, FF = (8, 2, 1024)

        def _reference_tuple_inner(x, gate_w, gate_b, w1, b1, w2, b2):
            n_experts = w1.shape[0]
            gate_logits = x @ gate_w + gate_b
            topk_vals, topk_idx = jax.lax.top_k(gate_logits, K)
            topk_w = jax.nn.softmax(topk_vals, axis=-1)
            onehot = jax.nn.one_hot(topk_idx, n_experts, dtype=x.dtype)
            comb = jnp.sum(onehot * topk_w[..., None], axis=2)
            h = jax.nn.gelu(jnp.einsum('btd,edf->ebtf', x, w1) + b1[:, None, None, :], approximate=False)
            y = jnp.einsum('ebtf,efd->ebtd', h, w2) + b2[:, None, None, :]
            output = jnp.einsum('ebtd,bte->btd', y, comb)
            expert_counts = jnp.sum(onehot, axis=(0, 1, 2)).astype(jnp.float32)
            return (output, gate_logits, topk_idx, expert_counts)
        return _reference_tuple_inner(x, gate_w, gate_b, w1, b1, w2, b2)[0]
    x = x + jnp.tanh(g_xattn[0]) * _L0_xattn_ref(_layernorm(x, axis=-1), ctx_1024, L0_xattn_Wq_c, L0_xattn_bq_c, L0_xattn_Wk_s, L0_xattn_bk_s, L0_xattn_Wv_s, L0_xattn_bv_s, L0_xattn_Wq_s, L0_xattn_bq_s, L0_xattn_Wk_c, L0_xattn_bk_c, L0_xattn_Wv_c, L0_xattn_bv_c, L0_xattn_Wg, L0_xattn_bg)
    x = x + jnp.tanh(g_ffn[0]) * _L0_ffn_ref(_layernorm(x, axis=-1), L0_ffn_router_w, L0_ffn_up_w, L0_ffn_down_w)
    x = x + jnp.tanh(g_xattn[1]) * _L1_xattn_ref(_layernorm(x, axis=-1), ctx_1024, L1_xattn_Wq, L1_xattn_bq, L1_xattn_Wk, L1_xattn_bk, L1_xattn_Wv, L1_xattn_bv, L1_xattn_Wo, L1_xattn_bo)
    x = x + jnp.tanh(g_ffn[1]) * _L1_ffn_ref(_layernorm(x, axis=-1), L1_ffn_gate_w, L1_ffn_gate_b, L1_ffn_w1, L1_ffn_b1, L1_ffn_w2, L1_ffn_b2)
    return x

_drawn_inputs = setup_inputs


def setup_inputs(seed=0):
    import zlib

    import numpy as np

    out = dict(_drawn_inputs(seed))
    spreads = {'g_ffn': (-1.0, 0.6),
     'L1_xattn_bq': (0.0, 0.58),
     'L1_xattn_bk': (0.0, 0.8),
     'L1_xattn_bv': (0.0, 0.1),
     'L1_xattn_bo': (0.0, 0.1),
     'L1_ffn_gate_b': (0.0, 0.29),
     'L1_ffn_b1': (0.0, 0.574),
     'L1_ffn_b2': (0.0, 0.1)}
    factors = {'L0_xattn_Wq_c': 8.0,
     'L0_xattn_bq_c': 8.0,
     'L0_xattn_Wk_s': 8.0,
     'L0_xattn_bk_s': 8.0,
     'L0_xattn_bv_s': 4.874,
     'L0_xattn_Wq_s': 8.0,
     'L0_xattn_bq_s': 8.0,
     'L0_xattn_Wk_c': 8.0,
     'L0_xattn_bk_c': 8.0,
     'L0_xattn_Wv_c': 6.549,
     'L0_xattn_bv_c': 4.949,
     'L0_xattn_Wg': 8.0,
     'L0_xattn_bg': 8.0}
    for name, (base, spread) in spreads.items():
        noise = np.random.default_rng([zlib.crc32(name.encode()), seed]).standard_normal(out[name].shape)
        drawn = base * np.exp(spread * noise) if base else spread * noise
        out[name] = jnp.asarray(drawn.astype(out[name].dtype))
    for name, factor in factors.items():
        out[name] = (out[name] * factor).astype(out[name].dtype)
    return out
```

```python
from contextlib import ExitStack

import numpy as np

import concourse.bass as bass
from concourse import mybir

F32 = mybir.dt.float32
F32R = mybir.dt.float32r
ALU = mybir.AluOpType
ACT = mybir.ActivationFunctionType
AX = mybir.AxisListType

P = 128
BATCH, TOK, D = 4, 512, 256
CTX = 1601
KD = D // P
TT = TOK // P
NT = BATCH * TT
CHUNKS = 4
CW = 2 * -(-CTX // (2 * CHUNKS))
CTXP = CHUNKS * CW
CLAST = CTX - (CHUNKS - 1) * CW
CT = -(-CTX // P)
CREM = CTX - (CT - 1) * P
E, H = 8, 1024
HT = H // P
TOP = (4, 2)
EPS = 1e-5
SCALE = 1.0 / float(np.sqrt(np.float32(D)))
STAGE = 1024
NSTAGE = 3

_COLS = [
    ("bq_c", KD), ("bv_s", KD), ("bq_s", KD), ("bk_c", KD), ("bv_c", KD), ("bg", KD),
    ("bq1", KD), ("bv1", KD), ("b1", E * HT), ("mixing", 2 * TT), ("gates", 4),
    ("lower", E * E), ("gate_b", E), ("bk_s", KD), ("bk1", KD), ("router0", KD * E), ("router1", KD * E),
    ("bo", D), ("ident", P),
]
COL = {}
_at = 0
for _n, _w in _COLS:
    COL[_n] = (_at, _at + _w)
    _at += _w
NCOL = _at
PAIRED = COL["bk_s"][0], COL["router1"][1]


def f32(ap):
    return ap.bitcast(F32)


class Queue:

    def __init__(self, sem):
        self.sem, self.steps, self.count = sem, [], 0

    def do(self, step, after=()):
        need = {}
        for sem, value in after:
            if value > need.get(sem.name, (None, 0))[1]:
                need[sem.name] = (sem, value)
        self.steps.append((step, list(need.values())))
        self.count += 1
        return (self.sem, self.count)

    def last(self):
        return (self.sem, self.count)

    def emit(self, engine):
        passed = {}
        for step, need in self.steps:
            for sem, value in need:
                if passed.get(sem.name, 0) < value:
                    engine.wait_ge(sem, value)
                    passed[sem.name] = value
            step(engine).then_inc(self.sem, 1)


class Loads:

    def __init__(self):
        self.steps, self.total = [], {}

    def do(self, dst, src, sem, after=()):
        self.total[sem.name] = self.total.get(sem.name, 0) + 16
        self.steps.append((dst, src, sem, list(after)))
        return (sem, self.total[sem.name])

    def emit(self, engine):
        passed = {}
        for dst, src, sem, after in self.steps:
            for s, value in after:
                if passed.get(s.name, 0) < value:
                    engine.wait_ge(s, value)
                    passed[s.name] = value
            engine.dma_start(dst, src).then_inc(sem, 16)


class Buf:

    def __init__(self, *aps):
        self.aps = aps
        self.ready, self.free = [], []

    @property
    def hi(self):
        return self.aps[0]

    @property
    def lo(self):
        return self.aps[1]

    @property
    def ap(self):
        return self.aps[0]


class Ring:
    def __init__(self, bufs):
        self.bufs, self.n = bufs, 0

    def take(self):
        b = self.bufs[self.n % len(self.bufs)]
        self.n += 1
        return b


def build(nc, t, out):
    ctx = ExitStack()
    with ctx:
        def sem(name):
            return ctx.enter_context(nc.semaphore(name))

        pe, act, dve, pool = (Queue(sem(f"{n}_steps")) for n in ("pe", "act", "dve", "pool"))
        loads = Loads()
        engines = (pe, act, dve, pool)

        def sb(name, shape, dtype=F32, stack=ctx):
            return stack.enter_context(nc.sbuf_tensor(name, shape, dtype))

        def pair(name, shape, stack=ctx):
            hi, lo = sb(name + "_hi", shape, F32R, stack), sb(name + "_lo", shape, F32R, stack)
            whole = tuple(slice(None) for _ in shape)
            return Buf(hi[whole], lo[whole])

        ps = ctx.enter_context(nc.psum_tensor("banks", [P, 8, 512], F32))

        x = sb("x", [P, NT, D])
        small = sb("small", [P, NCOL])
        small_p = pair("small_pair", [P, PAIRED[1] - PAIRED[0]])
        b2 = sb("b2", [E, D])
        stage = sb("stage", [P, NSTAGE, STAGE])
        tanh_g = sb("tanh_g", [P, 4])
        half_bg = sb("half_bg", [P, KD])
        bo_g = sb("bo_g", [P, D])
        stats = sb("stats", [P, NT, 6])
        moments = sb("moments", [P, NT, 2])
        rstd = sb("rstd", [P, NT])
        minus_half = sb("minus_half", [P, TT])
        s_small, s_b2 = sem("small_in"), sem("b2_in")
        s_x = [sem(f"x_in{b}") for b in range(BATCH)]
        s_out = sem("out_done")
        slots = Ring([Buf(stage[:, i, :]) for i in range(NSTAGE)])
        for i, s in enumerate(slots.bufs):
            s.sem = sem(f"stage{i}_in")

        def col(name, i=None, n=1):
            a, b = COL[name]
            return small[:, a:b] if i is None else small[:, a + i:a + i + n]

        ident = col("ident")

        t_small = loads.do(small[:, :], t["small"], s_small)
        t_b2 = loads.do(b2[:, :], t["b2"], s_b2)
        x_in = []
        for b in range(BATCH):
            x_in.append(loads.do(x[:, b * TT:(b + 1) * TT, :],
                                 t["x"].rearrange("(t p) d -> p t d", p=P)[:, b * TT:(b + 1) * TT, :], s_x[b]))
            if b == 0:
                x_first = len(loads.steps)

        x_ready = [[x_in[i // TT]] for i in range(NT)]

        t_mh = pool.do(lambda e: e.memset(minus_half[:, :], -0.5))
        t_tanh = act.do(lambda e: e.activation(tanh_g[:, :], col("gates"), ACT.Tanh), [t_small])
        t_bg = dve.do(lambda e: e.tensor_scalar(half_bg[:, :], col("bg"), 0.5, None, ALU.mult), [t_small])
        t_bo = dve.do(lambda e: e.tensor_scalar(bo_g[:, :], col("bo"), tanh_g[:, 1:2], None, ALU.mult), [t_tanh])
        t_sp = dve.do(lambda e: e.tensor_copy(small_p.hi, small[:, PAIRED[0]:PAIRED[1]]), [t_small])
        t_sp = dve.do(lambda e: e.tensor_tensor(small_p.lo, small[:, PAIRED[0]:PAIRED[1]], f32(small_p.hi),
                                                ALU.subtract), [t_sp])
        small_p.ready = [t_sp]

        def pcol(name, i, n):
            a = COL[name][0] - PAIRED[0] + i
            return small_p.hi[:, a:a + n], small_p.lo[:, a:a + n]

        def bring(src, n, hi, lo, after):
            slot = slots.take()
            landed = loads.do(slot.ap[:, :n], src, slot.sem, slot.free)
            view = slot.ap[:, :n]
            if len(hi.shape) == 3:
                view = view.rearrange("p (a b) -> p a b", a=hi.shape[1])
            made = dve.do(lambda e: e.tensor_copy(hi, view), [landed, *after])
            made = pool.do(lambda e: e.tensor_tensor(lo, view, f32(hi), ALU.subtract), [made, *after])
            slot.free = [made]
            return made

        def three(e, dst, lhs, rhs, first, last):
            for n, (a, b) in enumerate(((lhs[0], rhs[0]), (lhs[0], rhs[1]), (lhs[1], rhs[0]))):
                mm = e.matmul(dst, a, b, start=first and n == 0, stop=last and n == 2, skip_group_check=True)
            return mm

        def split(src, hi, lo, after, bias=None):
            if bias is None:
                a = act.do(lambda e: e.activation(hi, src, ACT.Copy), after)
                return dve.do(lambda e: e.tensor_tensor(lo, src, f32(hi), ALU.subtract), [a, *after])
            a = act.do(lambda e: e.activation(hi, src, ACT.Identity, bias=bias), after)
            return dve.do(lambda e: e.scalar_tensor_tensor(lo, src, bias, f32(hi), ALU.add, ALU.subtract), [a, *after])

        def norm_stats(tiles, xn, after):
            for i in tiles:
                s = dve.do(lambda e, i=i: e.bn_stats(stats[:, i, :], x[:, i, :]), x_ready[i])
                s = dve.do(lambda e, i=i: e.bn_aggr(moments[:, i, :], stats[:, i, :]), [s])
            a, n = tiles[0], len(tiles)
            s = dve.do(lambda e: e.tensor_scalar(rstd[:, a:a + n], moments[:, a:a + n, 1], EPS, None, ALU.add), [s])
            s = pool.do(lambda e: e.tensor_tensor(rstd[:, a:a + n], rstd[:, a:a + n], minus_half[:, :n], ALU.pow),
                        [s, t_mh])
            for i in tiles:
                v = dve.do(lambda e, i=i: e.tensor_scalar(xn.ap[:, i - a, :], x[:, i, :], moments[:, i, 0:1],
                                                          rstd[:, i:i + 1], ALU.subtract, ALU.mult),
                           [s, *after, *xn.free])
            xn.ready, xn.free = [v], []

        def norm_turn(xn, hi, lo, banks, after):
            made = []
            for k in range(KD):
                bank = banks.take()

                def turn(e, k=k, bank=bank):
                    for i in range(TT):
                        mm = e.transpose(bank.ap[:, i * P:(i + 1) * P], xn.ap[:, i, k * P:(k + 1) * P], ident)
                    return mm
                m = pe.do(turn, [*xn.ready, *bank.free])
                bank.free = [split(bank.ap, hi[:, k, :], lo[:, k, :], [m, *after])]
                made += bank.free
            xn.free = [m]
            return made

        def barrier():
            return [q.last() for q in engines]

        def attention(layer, start):
            st = ExitStack()
            two_way = layer == 0
            n = f"a{layer}_"
            gate_col = tanh_g[:, 2 * 0 + layer:2 * 0 + layer + 1]
            weights = pair(n + "weights", [P, t[f"aw{layer}"].shape[1]], st)
            ctx_c = pair(n + "ctx_cols", [P, KD, CTXP], st)
            ctx_r = pair(n + "ctx_rows", [P, CT, D], st)
            xl = pair(n + "xl", [P, KD, TOK], st)
            s0, s1, s2, s3, s4 = (pair(n + f"cols{i}", [P, KD, TOK], st) for i in range(5))
            xn = Buf(sb(n + "xn", [P, TT, D], F32, st)[:, :, :])
            probs = Ring([Buf(sb(n + f"probs{i}", [P, CTXP], F32, st)[:, :]) for i in range(2)])
            pt = Ring([pair(n + f"probs_t{i}", [P, TOK], st) for i in range(3)])
            mixed = Ring([Buf(sb(n + f"mixed{i}", [P, D], F32, st)[:, :]) for i in range(2)])
            work = Buf(sb(n + "work", [P, KD, TOK], F32, st)[:, :, :])
            pc = Buf(sb(n + "pc", [P, TT, TOK], F32, st)[:, :, :]) if two_way else None
            rrow = work.ap[0:1, 0, :]
            rcol = Buf(sb(n + "rcol", [P, TT], F32, st)[:, :])
            NS = 4
            cells = [[Buf(sb(n + f"cell{i}_{j}", [P, 2], F32, st)[:, :]) for j in range(NS)] for i in range(4)]
            top, nbias, sums, rinv = (Ring(c) for c in cells)
            everything = [xl, s0, s1, s2, s3, s4, xn, work, rcol, *probs.bufs, *pt.bufs, *mixed.bufs]
            everything += [b for c in cells for b in c] + ([pc] if pc else [])
            for b in everything:
                b.free = list(start)
            weights.free = ctx_c.free = ctx_r.free = list(start)

            bank = [Buf(ps[:, i, :]) for i in range(8)]
            for b in bank:
                b.free = list(start)
            banks = Ring(bank[4:7])
            mix_bank = bank[7]
            score_banks = bank[:4]

            def load_weights(i):
                a, b = i * STAGE, (i + 1) * STAGE
                weights.ready = [bring(t[f"aw{layer}"][:, a:b], STAGE, weights.hi[:, a:b], weights.lo[:, a:b], weights.free)]
                w_ready.append(weights.ready)

            w_ready = []

            def wt(i, k, a=0, n=P):
                o = (i * KD + k) * D + a
                return weights.hi[:, o:o + n], weights.lo[:, o:o + n]

            def load_ctx_c(b):
                half = CTXP // 2
                ready = []
                for k in range(KD):
                    for h in range(2):
                        c = slice(h * half, (h + 1) * half)
                        ready = [bring(t["ctx_cols"][b, :, k, c], half, ctx_c.hi[:, k, c], ctx_c.lo[:, k, c], ctx_c.free)]
                ctx_c.ready = ready

            def load_ctx_r(b):
                for a in range(0, CT, 4):
                    m = min(4, CT - a)
                    ready = [bring(t["ctx_rows"][b, :, a:a + m, :], m * D, ctx_r.hi[:, a:a + m, :],
                                   ctx_r.lo[:, a:a + m, :], ctx_r.free)]
                ctx_r.ready = ready

            def load_sel(b, which):
                s4.ready = [bring(t["ctx_picked"][b, which], KD * TOK, s4.hi, s4.lo, s4.free)]

            def project(w, src, dst, bias, ready=None):
                made = []
                for m in range(KD):
                    bk = banks.take()

                    def mms(e, m=m, bk=bk):
                        for k in range(KD):
                            mm = three(e, bk.ap, wt(w, k, m * P), (src.hi[:, k, :], src.lo[:, k, :]), k == 0, k == KD - 1)
                        return mm
                    p = pe.do(mms, [*w_ready[w // 2], *src.ready, *bk.free])
                    bk.free = [split(bk.ap, dst.hi[:, m, :], dst.lo[:, m, :], [p, *dst.free], bias and bias(m))]
                    made += bk.free
                src.free = [p]
                dst.ready, dst.free = made, []
                return p

            def query_bias(q, name):
                bk = banks.take()

                def mms(e):
                    for k in range(KD):
                        mm = three(e, bk.ap[0:1, :], pcol(name, k, 1), (q.hi[:, k, :], q.lo[:, k, :]), k == 0, k == KD - 1)
                    return mm
                p = pe.do(mms, [*small_p.ready, *q.ready, *bk.free])
                a = act.do(lambda e: e.activation(rrow, bk.ap[0:1, :], ACT.Copy), [p, *work.free])
                bk.free = [a]
                bk2 = banks.take()

                def turn(e):
                    for i in range(TT):
                        mm = e.transpose(bk2.ap[:, i:i + 1], rrow[:, i * P:(i + 1) * P], ident[0:1, 0:1])
                    return mm
                p2 = pe.do(turn, [a, *bk2.free])
                work.free = [p2]
                v = dve.do(lambda e: e.tensor_copy(rcol.ap, bk2.ap[:, 0:TT]), [p2, *rcol.free])
                bk2.free = [v]
                rcol.ready, rcol.free = [v], []
                return p

            class Tile:
                pass

            def scores(i, g):
                o = Tile()
                sb_free = [z for bk in score_banks for z in bk.free]

                def mms(e):
                    for c in range(CHUNKS):
                        for k in range(KD):
                            mm = three(e, ps[:, c, 0:CW], (g.hi[:, k, i * P:(i + 1) * P], g.lo[:, k, i * P:(i + 1) * P]),
                                       (ctx_c.hi[:, k, c * CW:(c + 1) * CW], ctx_c.lo[:, k, c * CW:(c + 1) * CW]),
                                       k == 0, k == KD - 1)
                    return mm
                p = pe.do(mms, [*g.ready, *ctx_c.ready, *sb_free])
                mx, nb, sm, ri = top.take(), nbias.take(), sums.take(), rinv.take()
                o.p, o.rinv = probs.take(), ri
                v = dve.do(lambda e: e.tensor_reduce(mx.ap[:, 0:1], ps[:, 0:CHUNKS, 0:CW], AX.XY, ALU.max), [p, *mx.free])
                r = rcol.ap[:, i:i + 1]
                v2 = dve.do(lambda e: e.tensor_tensor(mx.ap[:, 1:2], mx.ap[:, 0:1], r, ALU.add), [v, *rcol.ready])
                v3 = dve.do(lambda e: e.tensor_scalar(nb.ap[:, 0:1], r, mx.ap[:, 1:2], SCALE, ALU.subtract, ALU.mult),
                            [v2, *nb.free])
                full = (CHUNKS - 1) * CW
                a1 = act.do(lambda e: e.activation(o.p.ap[:, 0:full].rearrange("p (c w) -> p c w", w=CW),
                                                   ps[:, 0:CHUNKS - 1, 0:CW], ACT.Exp, bias=nb.ap[:, 0:1], scale=SCALE,
                                                   accum_out=sm.ap[:, 0:1]), [v3, *o.p.free, *sm.free])
                a2 = act.do(lambda e: e.activation(o.p.ap[:, full:CTX], ps[:, CHUNKS - 1, 0:CLAST], ACT.Exp,
                                                   bias=nb.ap[:, 0:1], scale=SCALE, accum_out=sm.ap[:, 1:2]), [v3])
                v4 = dve.do(lambda e: e.tensor_tensor(ri.ap[:, 1:2], sm.ap[:, 0:1], sm.ap[:, 1:2], ALU.add), [a2, *ri.free])
                v5 = dve.do(lambda e: e.reciprocal(ri.ap[:, 0:1], ri.ap[:, 1:2]), [v4])
                mx.free, nb.free, sm.free = [v3], [a2], [v4]
                rcol.free = [v3]
                for bk in score_banks:
                    bk.free = [v, a2]
                o.p.ready, ri.ready = [a1, a2], [v5]
                o.scored = p
                return o

            def mix(o):
                groups = [list(range(a, min(a + 4, CT))) for a in range(0, CT, 4)]

                def turn(kts):
                    bk, dst = banks.take(), pt.take()
                    w = CREM if kts[-1] == CT - 1 else P

                    def mms(e):
                        for j, kt in enumerate(kts):
                            mm = e.transpose(bk.ap[0:w, j * P:(j + 1) * P], o.p.ap[:, kt * P:kt * P + w], ident)
                        return mm
                    p = pe.do(mms, [*o.p.ready, *bk.free])
                    c = len(kts) * P
                    s = split(bk.ap[0:w, 0:c], dst.hi[0:w, 0:c], dst.lo[0:w, 0:c], [p, *dst.free])
                    bk.free, dst.ready, dst.free = [s], [s], []
                    return dst, w, p

                def multiply(kts, dst, w):
                    def mms(e):
                        for j, kt in enumerate(kts):
                            c = slice(j * P, (j + 1) * P)
                            mm = three(e, mix_bank.ap[:, 0:D], (dst.hi[0:w, c], dst.lo[0:w, c]),
                                       (ctx_r.hi[0:w, kt, :], ctx_r.lo[0:w, kt, :]), kt == 0, kt == CT - 1)
                        return mm
                    p = pe.do(mms, [*dst.ready, *ctx_r.ready, *mix_bank.free])
                    dst.free = [p]
                    return p

                turned = [turn(groups[0]), turn(groups[1])]
                for gi, kts in enumerate(groups):
                    p = multiply(kts, *turned[gi][:2])
                    if gi + 2 < len(groups):
                        turned.append(turn(groups[gi + 2]))
                o.p.free = [turned[-1][2]]
                o.mixed = mixed.take()
                a = act.do(lambda e: e.activation(o.mixed.ap, mix_bank.ap[:, 0:D], ACT.Copy, scale=o.rinv.ap[:, 0:1]),
                           [p, *o.rinv.ready, *o.mixed.free])
                mix_bank.free = [a]
                o.rinv.free = [a]
                o.mixed.ready = [a]
                o.multiplied = p

            def turn_mixed(i, o, dst):
                bk = banks.take()

                def mms(e):
                    for k in range(KD):
                        mm = e.transpose(bk.ap[:, k * P:(k + 1) * P], o.mixed.ap[:, k * P:(k + 1) * P], ident)
                    return mm
                p = pe.do(mms, [*o.mixed.ready, *bk.free])
                c = slice(i * P, (i + 1) * P)
                s = split(bk.ap[:, 0:KD * P].rearrange("p (k q) -> p k q", k=KD), dst.hi[:, :, c], dst.lo[:, :, c],
                          [p, *(dst.free if i == 0 else [])])
                bk.free, o.mixed.free = [s], [p]
                dst.ready = [s]

            def attend(g, dst, fill):
                tiles = []
                for i in range(TT + 2):
                    if i < TT:
                        tiles.append(scores(i, g))
                    if i == 0:
                        fill()
                    if i >= 2:
                        turn_mixed(i - 2, tiles[i - 2], dst)
                    if 1 <= i <= TT:
                        mix(tiles[i - 1])
                ctx_c.free = [tiles[-1].scored]
                ctx_r.free = [tiles[-1].multiplied]
                g.free = [tiles[-1].scored]
                dst.free = []

            def residual(b, pairs, src, gate, extra=None):
                pass

            norm_stats(range(0, TT), xn, start)
            for i in range(1):
                load_weights(i)
            xl.ready = norm_turn(xn, xl.hi, xl.lo, banks, xl.free)
            load_ctx_c(0)
            for i in range(1, t[f"aw{layer}"].shape[1] // STAGE):
                load_weights(i)
            load_ctx_r(0)

            for b in range(BATCH):
                more = b + 1 < BATCH
                if two_way:
                    WQ, WK, WV, WQS, WKC, WVC, WG = range(7)
                    names = ("bq_c", "bk_s", "bv_s")
                else:
                    WQ, WK, WV, WO = range(4)
                    names = ("bq1", "bk1", "bv1")
                project(WQ, xl, s0, lambda m: col(names[0], m))
                project(WK, s0, s1, None)
                s0.free = [query_bias(s0, names[1])]

                def back_keys():
                    project(WKC, xl, s3, lambda m: col("bk_c", m))
                    made = []
                    for h in range(2):
                        bk = banks.take()

                        def mms(e, h=h, bk=bk):
                            for j in range(2):
                                c = slice((2 * h + j) * P, (2 * h + j + 1) * P)
                                for k in range(KD):
                                    mm = three(e, bk.ap[:, j * D:(j + 1) * D], (xl.hi[:, k, c], xl.lo[:, k, c]),
                                               wt(WVC, k, 0, D), k == 0 and j == 0, k == KD - 1)
                            return mm
                        p = pe.do(mms, [*w_ready[WVC // 2], *xl.ready, *bk.free])
                        bk.free = [split(bk.ap, s0.hi[:, h, :], s0.lo[:, h, :], [p, *s0.free])]
                        made += bk.free
                    s0.ready, s0.free, xl.free = made, [], [p]

                if two_way:
                    load_sel(b, 0)
                attend(s1, s2, back_keys if two_way else (lambda: None))
                if more:
                    load_ctx_c(b + 1)
                    load_ctx_r(b + 1)
                    norm_stats(range((b + 1) * TT, (b + 2) * TT), xn, [])

                if two_way:
                    project(WV, s2, s1, lambda m: col(names[2], m))
                    for which in range(2):
                        project(WQS, s4, s2, lambda m: col("bq_s", m))
                        if which == 0:
                            load_sel(b, 1)
                            if more:
                                xl.ready = norm_turn(xn, xl.hi, xl.lo, banks, xl.free)
                        for i in range(TT):
                            bk = score_banks[i]

                            def mms(e, i=i, bk=bk):
                                c = slice(i * P, (i + 1) * P)
                                for k in range(KD):
                                    mm = three(e, bk.ap, (s2.hi[:, k, c], s2.lo[:, k, c]),
                                               (s3.hi[:, k, :], s3.lo[:, k, :]), k == 0, k == KD - 1)
                                return mm
                            p = pe.do(mms, [*s2.ready, *s3.ready, *bk.free])
                            mx, nb, sm, ri = top.take(), nbias.take(), sums.take(), rinv.take()
                            pr = probs.take()
                            v = dve.do(lambda e, bk=bk, mx=mx: e.tensor_reduce(mx.ap[:, 0:1], bk.ap, AX.X, ALU.max),
                                       [p, *mx.free])
                            v = dve.do(lambda e, nb=nb, mx=mx: e.tensor_scalar(nb.ap[:, 0:1], mx.ap[:, 0:1], -SCALE, None,
                                                                               ALU.mult), [v, *nb.free])
                            a = act.do(lambda e, bk=bk, nb=nb, sm=sm, pr=pr: e.activation(
                                pr.ap[:, 0:TOK], bk.ap, ACT.Exp, bias=nb.ap[:, 0:1], scale=SCALE,
                                accum_out=sm.ap[:, 0:1]), [v, *pr.free, *sm.free])
                            mx.free, nb.free, bk.free = [v], [a], [a]
                            v = dve.do(lambda e, ri=ri, sm=sm: e.reciprocal(ri.ap[:, 1:2], sm.ap[:, 0:1]), [a, *ri.free])
                            sm.free = [v]
                            w = col("mixing", which * TT + i)
                            v = dve.do(lambda e, ri=ri, w=w: e.tensor_tensor(ri.ap[:, 0:1], ri.ap[:, 1:2], w, ALU.mult), [v])
                            if which == 0:
                                v = act.do(lambda e, i=i, pr=pr, ri=ri: e.activation(
                                    pc.ap[:, i, :], pr.ap[:, 0:TOK], ACT.Copy, scale=ri.ap[:, 0:1]), [v, *pc.free])
                                pc.ready = [v]
                            else:
                                v = dve.do(lambda e, i=i, pr=pr, ri=ri: e.scalar_tensor_tensor(
                                    pc.ap[:, i, :], pr.ap[:, 0:TOK], ri.ap[:, 0:1], pc.ap[:, i, :], ALU.mult, ALU.add),
                                    [v, *pc.ready])
                            ri.free = pr.free = [v]
                        s2.free = [p]
                        s2.ready = []
                    s3.free = [p]
                    pc.ready = [v]
                    acc = score_banks[0:KD]
                    turned = []

                    def turn_pc(j):
                        bk, dst = banks.take(), pt.take()

                        def mms(e):
                            for i in range(TT):
                                mm = e.transpose(bk.ap[:, i * P:(i + 1) * P], pc.ap[:, i, j * P:(j + 1) * P], ident)
                            return mm
                        p = pe.do(mms, [*pc.ready, *bk.free])
                        s = split(bk.ap, dst.hi, dst.lo, [p, *dst.free])
                        bk.free, dst.ready = [s], [s]
                        turned.append((dst, p))

                    turn_pc(0)
                    turn_pc(1)
                    for j in range(TT):
                        dst = turned[j][0]

                        def mms(e, j=j, dst=dst):
                            for m in range(KD):
                                o = (j % 2) * D + m * P
                                mm = three(e, acc[m].ap, (s0.hi[:, j // 2, o:o + P], s0.lo[:, j // 2, o:o + P]),
                                           (dst.hi, dst.lo), j == 0, j == TT - 1)
                            return mm
                        p = pe.do(mms, [*dst.ready, *s0.ready, *[z for q in acc for z in q.free]])
                        dst.free = [p]
                        if j + 2 < TT:
                            turn_pc(j + 2)
                    pc.free = [turned[-1][1]]
                    s0.free = [p]
                    made = []
                    for m in range(KD):
                        acc[m].free = [split(acc[m].ap, s3.hi[:, m, :], s3.lo[:, m, :], [p, *s3.free], col("bv_c", m))]
                        made += acc[m].free
                    s3.ready, s3.free = made, []
                    diff = pc.ap[:, 0:KD, :]
                    v = pool.do(lambda e: e.tensor_tensor(diff, f32(s1.hi), f32(s3.hi), ALU.subtract),
                                [*s1.ready, *s3.ready, *pc.free])
                    part = pc.ap[:, KD:2 * KD, :]
                    v = pool.do(lambda e: e.tensor_tensor(part, f32(s1.lo), f32(s3.lo), ALU.subtract), [v])
                    t_diff = pool.do(lambda e: e.tensor_tensor(diff, diff, part, ALU.add), [v])
                    made = []
                    for m in range(KD):
                        bk = banks.take()

                        def mms(e, m=m, bk=bk):
                            for f in range(2 * KD):
                                src, k = (s1, f) if f < KD else (s3, f - KD)
                                o = (WG * KD + f) * D + m * P
                                mm = three(e, bk.ap, (weights.hi[:, o:o + P], weights.lo[:, o:o + P]),
                                           (src.hi[:, k, :], src.lo[:, k, :]), f == 0, f == 2 * KD - 1)
                            return mm
                        p = pe.do(mms, [*w_ready[WG // 2], *s1.ready, *s3.ready, *bk.free])
                        a = act.do(lambda e, m=m, bk=bk: e.activation(work.ap[:, m, :], bk.ap, ACT.Tanh,
                                                                      bias=half_bg[:, m:m + 1], scale=0.5),
                                   [p, *work.free, t_bg])
                        bk.free = [a]
                        made.append(a)
                    v = dve.do(lambda e: e.scalar_tensor_tensor(diff, work.ap, 1.0, diff, ALU.add, ALU.mult),
                               [*made, t_diff])
                    v = dve.do(lambda e: e.scalar_tensor_tensor(work.ap, diff, 0.5, f32(s3.hi), ALU.mult, ALU.add), [v])
                    v = dve.do(lambda e: e.tensor_tensor(work.ap, work.ap, f32(s3.lo), ALU.add), [v])
                    pc.free = [v]
                    s1.free = [p, t_diff]
                    s3.free = [p, v]
                    work.ready = [v]
                    for h in range(2):
                        bk = banks.take()

                        def turn(e, h=h, bk=bk):
                            for j in range(2):
                                c = slice((2 * h + j) * P, (2 * h + j + 1) * P)
                                for k in range(KD):
                                    o = j * D + k * P
                                    mm = e.transpose(bk.ap[:, o:o + P], work.ap[:, k, c], ident)
                            return mm
                        p = pe.do(turn, [*work.ready, *bk.free])
                        i = b * TT + 2 * h
                        xs = x[:, i:i + 2, :].rearrange("p t d -> p (t d)")
                        v = dve.do(lambda e, bk=bk, xs=xs: e.scalar_tensor_tensor(xs, bk.ap, gate_col, xs, ALU.mult, ALU.add),
                                   [p, t_tanh, *x_ready[i], *x_ready[i + 1]])
                        bk.free = [v]
                        x_ready[i] = x_ready[i + 1] = [v]
                    work.free = [p]
                else:
                    made = []
                    for m in range(KD):
                        bk = banks.take()

                        def mms(e, m=m, bk=bk):
                            for k in range(KD):
                                mm = three(e, bk.ap, wt(WV, k, m * P), (s2.hi[:, k, :], s2.lo[:, k, :]), k == 0, k == KD - 1)
                            return mm
                        p = pe.do(mms, [*w_ready[WV // 2], *s2.ready, *bk.free])
                        v = dve.do(lambda e, m=m, bk=bk: e.scalar_tensor_tensor(
                            work.ap[:, m, :], bk.ap, col(names[2], m), f32(xl.hi)[:, m, :], ALU.add, ALU.add),
                            [p, *work.free])
                        bk.free = [v]
                        v = dve.do(lambda e, m=m: e.tensor_tensor(work.ap[:, m, :], work.ap[:, m, :], f32(xl.lo)[:, m, :],
                                                                  ALU.add), [v])
                        made.append(split(work.ap[:, m, :], s1.hi[:, m, :], s1.lo[:, m, :], [v, *s1.free]))
                    s2.free = [p]
                    xl.free = [*xl.free, v]
                    work.free = made
                    s1.ready, s1.free = made, []
                    for h in range(2):
                        bk = banks.take()

                        def mms(e, h=h, bk=bk):
                            for j in range(2):
                                c = slice((2 * h + j) * P, (2 * h + j + 1) * P)
                                for k in range(KD):
                                    mm = three(e, bk.ap[:, j * D:(j + 1) * D], (s1.hi[:, k, c], s1.lo[:, k, c]),
                                               wt(WO, k, 0, D), k == 0 and j == 0, k == KD - 1)
                            return mm
                        p = pe.do(mms, [*w_ready[WO // 2], *s1.ready, *bk.free])
                        i = b * TT + 2 * h
                        xs = x[:, i:i + 2, :].rearrange("p t d -> p (t d)")
                        v = dve.do(lambda e, bk=bk, xs=xs: e.scalar_tensor_tensor(xs, bk.ap, gate_col, xs, ALU.mult, ALU.add),
                                   [p, t_tanh, *x_ready[i], *x_ready[i + 1]])
                        bk.free = [v]
                        for j in range(2):
                            v = dve.do(lambda e, q=i + j: e.tensor_tensor(x[:, q, :], x[:, q, :], bo_g[:, :], ALU.add),
                                       [v, t_bo])
                            x_ready[i + j] = [v]
                    s1.free = [p]
                    if more:
                        xl.ready = norm_turn(xn, xl.hi, xl.lo, banks, xl.free)
            st.close()

        def experts(layer, start):
            st = ExitStack()
            n = f"m{layer}_"
            gelu = (ACT.Gelu_apprx_tanh, ACT.Gelu)[layer]
            up_d, down_d = t[f"up{layer}"], t[f"down{layer}"]
            xl = pair(n + "xl", [P, KD, BATCH * TOK], st)
            ups = [pair(n + f"up{i}", [P, KD, H], st) for i in range(2)]
            downs = [pair(n + f"down{i}", [P, HT, D], st) for i in range(2)]
            xns = Ring([Buf(sb(n + f"xn{i}", [P, TT, D], F32, st)[:, :, :]) for i in range(2)])
            hidden = Ring([Buf(sb(n + f"hidden{i}", [P, TOK], F32, st)[:, :]) for i in range(3)])
            hp = Ring([pair(n + f"hidden_pair{i}", [P, TOK], st) for i in range(4)])
            comb = sb(n + "comb", [P, NT, E], F32, st)
            logits = sb(n + "logits", [P, TT, E], F32, st)
            lrow = Buf(sb(n + "logits_row", [E, TOK], F32, st)[:, :])
            above = sb(n + "above", [P, TT, E, E], F32, st)
            same = sb(n + "same", [P, TT, E, E], F32, st)
            rank = sb(n + "rank", [P, TT, E], F32, st)
            peak = sb(n + "peak", [P, TT], F32, st)
            total = sb(n + "total", [P, TT], F32, st)
            combt = sb(n + "combt", [E, NT, P], F32, st)
            every = [*ups, *downs, *xns.bufs, *hidden.bufs, *hp.bufs, lrow]
            for b in every:
                b.free = list(start)
            bank = [Buf(ps[:, i, :]) for i in range(8)]
            for b in bank:
                b.free = list(start)
            up_banks = Ring(bank[0:3])
            out_banks = Ring([bank[3:5], bank[5:7]])
            side = Ring([bank[7]])
            gate_col = tanh_g[:, 2 + layer:3 + layer]

            def load_expert(e_, piece):
                u, d = ups[e_ % 2], downs[e_ % 2]
                if piece < KD:
                    src = up_d[e_].rearrange("(k p) f -> p k f", p=P)[:, piece, :]
                    u.ready = [bring(src, H, u.hi[:, piece, :], u.lo[:, piece, :], u.free)]
                else:
                    h = HT // 2
                    a = (piece - KD) * h
                    src = down_d[e_].rearrange("(f p) d -> p f d", p=P)[:, a:a + h, :]
                    d.ready = [bring(src, h * D, d.hi[:, a:a + h, :], d.lo[:, a:a + h, :], d.free)]

            def route(c):
                cs = slice(c * TOK, (c + 1) * TOK)
                bk = side.take()

                def mms(e):
                    for k in range(KD):
                        mm = three(e, bk.ap[0:E, :], pcol(f"router{layer}", k * E, E), (xl.hi[:, k, cs], xl.lo[:, k, cs]),
                                   k == 0, k == KD - 1)
                    return mm
                p = pe.do(mms, [*small_p.ready, *xl_ready[c], *bk.free])
                a = act.do(lambda e: e.activation(lrow.ap, bk.ap[0:E, :], ACT.Copy), [p, *lrow.free])
                bk.free = [a]
                bk2 = up_banks.take()

                def turn(e):
                    for i in range(TT):
                        mm = e.transpose(bk2.ap[:, i * E:(i + 1) * E], lrow.ap[:, i * P:(i + 1) * P], ident[0:E, 0:E])
                    return mm
                p = pe.do(turn, [a, *bk2.free])
                lrow.free = [p]
                lg = bk2.ap[:, 0:TT * E].rearrange("p (t e) -> p t e", e=E)
                last = prev_route[0]
                if layer == 0:
                    v = dve.do(lambda e: e.tensor_copy(logits[:, :, :], lg), [p, *last])
                else:
                    gb = col("gate_b").unsqueeze(1).to_broadcast([P, TT, E])
                    v = dve.do(lambda e: e.tensor_tensor(logits[:, :, :], lg, gb, ALU.add), [p, *last])
                bk2.free = [v]
                other = logits[:, :, :].unsqueeze(2).to_broadcast([P, TT, E, E])
                own = logits[:, :, :].unsqueeze(3).to_broadcast([P, TT, E, E])
                low = col("lower").rearrange("p (a b) -> p a b", a=E)
                v0 = dve.do(lambda e: e.tensor_reduce(peak[:, :], logits[:, :, :], AX.X, ALU.max), [v])
                v1 = dve.do(lambda e: e.tensor_tensor(above[:, :, :, :], other, own, ALU.is_gt), [v])
                v2 = dve.do(lambda e: e.tensor_tensor(same[:, :, :, :], other, own, ALU.is_equal), [v])
                for i in range(TT):
                    v3 = dve.do(lambda e, i=i: e.tensor_tensor(same[:, i, :, :], same[:, i, :, :], low, ALU.mult), [v2])
                v4 = dve.do(lambda e: e.tensor_tensor(above[:, :, :, :], above[:, :, :, :], same[:, :, :, :], ALU.add), [v1, v3])
                v5 = dve.do(lambda e: e.tensor_reduce(rank[:, :, :], above[:, :, :, :], AX.X, ALU.add), [v4])
                cb = comb[:, c * TT:(c + 1) * TT, :]
                v6 = dve.do(lambda e: e.tensor_tensor(logits[:, :, :], logits[:, :, :],
                                                      peak[:, :].unsqueeze(2).to_broadcast([P, TT, E]), ALU.subtract),
                            [v0, v1, v2])
                a = act.do(lambda e: e.activation(cb, logits[:, :, :], ACT.Exp), [v6])
                v7 = dve.do(lambda e: e.scalar_tensor_tensor(cb, rank[:, :, :], float(TOP[layer]), cb, ALU.is_lt, ALU.mult),
                            [v5, a])
                v8 = dve.do(lambda e: e.tensor_reduce(total[:, :], cb, AX.X, ALU.add), [v7])
                v9 = dve.do(lambda e: e.reciprocal(total[:, :], total[:, :]), [v8])
                v10 = dve.do(lambda e: e.scalar_tensor_tensor(cb, cb, gate_col,
                                                              total[:, :].unsqueeze(2).to_broadcast([P, TT, E]),
                                                              ALU.mult, ALU.mult), [v9, t_tanh])
                prev_route[0] = [v10]
                comb_ready.append([v10])

            def output_bias(c):
                bk = side.take()

                def turn(e):
                    for i in range(TT):
                        mm = e.transpose(bk.ap[0:E, i * P:(i + 1) * P], comb[:, c * TT + i, :], ident)
                    return mm
                p = pe.do(turn, [*comb_ready[c], *bk.free])
                a = act.do(lambda e: e.activation(combt[:, c * TT:(c + 1) * TT, :],
                                                  bk.ap[0:E, :].rearrange("e (t p) -> e t p", p=P), ACT.Copy), [p])
                bk.free = [a]
                for h in range(2):
                    bk = side.take()

                    def mms(e, h=h, bk=bk):
                        for j in range(2):
                            mm = e.matmul(bk.ap[:, j * D:(j + 1) * D], combt[:, c * TT + 2 * h + j, :], b2[:, :],
                                          start=j == 0, stop=True, skip_group_check=True)
                        return mm
                    p = pe.do(mms, [a, t_b2, *bk.free])
                    i = c * TT + 2 * h
                    xs = x[:, i:i + 2, :].rearrange("p t d -> p (t d)")
                    v = dve.do(lambda e, bk=bk, xs=xs: e.tensor_tensor(xs, xs, bk.ap, ALU.add),
                               [p, *x_ready[i], *x_ready[i + 1]])
                    bk.free = [v]
                    x_ready[i] = x_ready[i + 1] = [v]

            xl_ready, comb_ready, prev_route = [], [], [list(start)]
            load_expert(0, 0)
            for c in range(BATCH):
                xn = xns.take()
                norm_stats(range(c * TT, (c + 1) * TT), xn, start)
                cs = slice(c * TOK, (c + 1) * TOK)
                xl_ready.append(norm_turn(xn, xl.hi[:, :, cs], xl.lo[:, :, cs], up_banks, start))
                if c < 3:
                    load_expert(0, c + 1)
            for c in range(BATCH):
                route(c)
            if layer == 1:
                for c in range(BATCH):
                    output_bias(c)

            def up(e_, c, f):
                u, bk, hf, hb = ups[e_ % 2], up_banks.take(), hidden.take(), hp.take()
                cs, fs = slice(c * TOK, (c + 1) * TOK), slice(f * P, (f + 1) * P)

                def mms(e):
                    for k in range(KD):
                        mm = three(e, bk.ap, (u.hi[:, k, fs], u.lo[:, k, fs]), (xl.hi[:, k, cs], xl.lo[:, k, cs]),
                                   k == 0, k == KD - 1)
                    return mm
                p = pe.do(mms, [*u.ready, *xl_ready[c], *bk.free])
                bias = {} if layer == 0 else {"bias": col("b1", e_ * HT + f)}
                a = act.do(lambda e: e.activation(hf.ap, bk.ap, gelu, **bias), [p, *hf.free])
                bk.free = [a]
                a2 = act.do(lambda e: e.activation(hb.hi, hf.ap, ACT.Copy), [a, *hb.free])
                v = dve.do(lambda e: e.tensor_tensor(hb.lo, hf.ap, f32(hb.hi), ALU.subtract), [a2])
                hf.free, hb.ready = [v], [v]
                if c == BATCH - 1 and f == HT - 1:
                    u.free = [p]
                return hb

            def down(e_, c, f, hb, banks2):
                d = downs[e_ % 2]

                def mms(e):
                    for i in range(TT):
                        mm = three(e, banks2[i // 2].ap[:, (i % 2) * D:(i % 2 + 1) * D],
                                   (hb.hi[:, i * P:(i + 1) * P], hb.lo[:, i * P:(i + 1) * P]),
                                   (d.hi[:, f, :], d.lo[:, f, :]), f == 0 and i % 2 == 0, f == HT - 1)
                    return mm
                p = pe.do(mms, [*d.ready, *hb.ready, *[z for q in banks2 for z in q.free]])
                hb.free = [p]
                if c == BATCH - 1 and f == HT - 1:
                    d.free = [p]
                if f == HT - 1:
                    for i in range(TT):
                        ti = c * TT + i
                        v = dve.do(lambda e, i=i, ti=ti: e.scalar_tensor_tensor(
                            x[:, ti, :], banks2[i // 2].ap[:, (i % 2) * D:(i % 2 + 1) * D],
                            comb[:, ti, e_:e_ + 1], x[:, ti, :], ALU.mult, ALU.add),
                            [p, *comb_ready[c], *x_ready[ti]])
                        x_ready[ti] = [v]
                        banks2[i // 2].free = [v]
                    if layer == 1 and e_ == E - 1:
                        loads.do(out.rearrange("(t p) d -> p t d", p=P)[:, c * TT:(c + 1) * TT, :],
                                 x[:, c * TT:(c + 1) * TT, :], s_out, [v])

            steps = [(e_, c, f) for e_ in range(E) for c in range(BATCH) for f in range(HT)]
            made, outs = {}, {}
            AHEAD = 2
            for q in range(len(steps) + AHEAD):
                if q < len(steps):
                    e_, c, f = steps[q]
                    if f == 2 and e_ + 1 < E:
                        load_expert(e_ + 1, c)
                    made[q] = up(e_, c, f)
                if q >= AHEAD:
                    e_, c, f = steps[q - AHEAD]
                    if f == 0:
                        outs[c] = out_banks.take()
                    down(e_, c, f, made.pop(q - AHEAD), outs[c])
            st.close()

        attention(0, [])
        experts(0, barrier())
        attention(1, barrier())
        experts(1, barrier())

        block = ctx.enter_context(nc.Block())

        @block.sync
        def _(e):
            loads.emit(e)
            e.wait_ge(s_out, loads.total[s_out.name])

        @block.tensor
        def _(e):
            pe.emit(e)

        @block.scalar
        def _(e):
            act.emit(e)

        @block.vector
        def _(e):
            dve.emit(e)

        @block.gpsimd
        def _(e):
            pool.emit(e)


def columns(w):
    a, b = w.shape
    return w.reshape(a // P, P, b).transpose(1, 0, 2).reshape(P, -1)


def kernel(**inputs):
    import concourse.bacc as _bacc
    from concourse.bass_utils import run_bass_kernel_spmd as _run

    g = {k: np.asarray(v) for k, v in inputs.items()}
    a = {}
    a["x"] = g["x"].reshape(BATCH * TOK, D)
    ctx = g["ctx_1024"]
    padded = np.concatenate([ctx, np.repeat(ctx[:, -1:], CTXP - CTX, axis=1)], axis=1)
    a["ctx_cols"] = padded.transpose(0, 2, 1).reshape(BATCH, KD, P, CTXP).transpose(0, 2, 1, 3)
    rows = np.concatenate([ctx, np.repeat(ctx[:, -1:], CT * P - CTX, axis=1)], axis=1)
    a["ctx_rows"] = rows.reshape(BATCH, CT, P, D).transpose(0, 2, 1, 3)
    one = np.float32(1)
    pos = (np.arange(TOK, dtype=np.float32) + np.float32(0.5)) * np.float32(CTX / TOK) - np.float32(0.5)
    pos = np.clip(pos, np.float32(0), np.float32(CTX - 1))
    lo = np.floor(pos).astype(np.int32)
    hi = np.minimum(lo + 1, CTX - 1)
    share = pos - lo.astype(np.float32)
    picked = np.stack([ctx[:, lo], ctx[:, hi]], axis=1)
    a["ctx_picked"] = picked.transpose(0, 1, 3, 2).reshape(BATCH, 2, KD, P, TOK).transpose(0, 1, 3, 2, 4).reshape(
        BATCH, 2, P, KD * TOK)
    L0, L1 = "L0_xattn_", "L1_xattn_"
    a["aw0"] = np.concatenate([columns(w) for w in (
        g[L0 + "Wq_c"].T, g[L0 + "Wk_s"], g[L0 + "Wv_s"].T, g[L0 + "Wq_s"].T, g[L0 + "Wk_c"].T, g[L0 + "Wv_c"].T,
        g[L0 + "Wg"].T)], axis=1)
    a["aw1"] = np.concatenate([columns(w) for w in (
        g[L1 + "Wq"].T, g[L1 + "Wk"], g[L1 + "Wv"].T, g[L1 + "Wo"].T)], axis=1)
    a["up0"], a["down0"] = g["L0_ffn_up_w"], g["L0_ffn_down_w"]
    a["up1"], a["down1"] = g["L1_ffn_w1"], g["L1_ffn_w2"]
    a["b2"] = g["L1_ffn_b2"]

    def vec(v):
        return v.reshape(-1, P).T

    def rows_of(v):
        return np.broadcast_to(v.reshape(1, -1), (P, v.size))
    parts = {
        "bq_c": vec(g[L0 + "bq_c"]), "bv_s": vec(g[L0 + "bv_s"]), "bq_s": vec(g[L0 + "bq_s"]), "bk_c": vec(g[L0 + "bk_c"]),
        "bv_c": vec(g[L0 + "bv_c"]), "bg": vec(g[L0 + "bg"]), "bq1": vec(g[L1 + "bq"]), "bv1": vec(g[L1 + "bv"]),
        "b1": vec(g["L1_ffn_b1"]), "mixing": np.concatenate([vec(one - share), vec(share)], axis=1),
        "gates": rows_of(np.concatenate([g["g_xattn"], g["g_ffn"]])),
        "lower": rows_of(np.tril(np.ones((E, E), np.float32), -1)), "gate_b": rows_of(g["L1_ffn_gate_b"]),
        "bk_s": vec(g[L0 + "bk_s"]), "bk1": vec(g[L1 + "bk"]), "router0": columns(g["L0_ffn_router_w"]),
        "router1": columns(g["L1_ffn_gate_w"]), "bo": rows_of(g[L1 + "bo"]), "ident": np.eye(P, dtype=np.float32),
    }
    a["small"] = np.concatenate([parts[n] for n, _ in _COLS], axis=1)

    nc = _bacc.Bacc("TRN2", target_bir_lowering=False, num_devices=1)
    arrays, handles = {}, {}
    for name, v in a.items():
        v = np.ascontiguousarray(v)
        arrays[f"in_{name}"] = v
        handles[name] = nc.dram_tensor(f"in_{name}", v.shape, mybir.dt.from_np(v.dtype), kind="ExternalInput").ap()
    out = nc.dram_tensor("out_x", (BATCH * TOK, D), F32, kind="ExternalOutput").ap()
    build(nc, handles, out)
    r = _run(nc, [arrays], core_ids=[0])
    return r.results[0]["out_x"].reshape(BATCH, TOK, D)
```

```python
from contextlib import ExitStack

import numpy as np

import concourse.bass as bass
from concourse import mybir

F32 = mybir.dt.float32
F16 = mybir.dt.float16
I32 = mybir.dt.int32
F32R = mybir.dt.float32r
ALU = mybir.AluOpType
ACT = mybir.ActivationFunctionType
AX = mybir.AxisListType

P = 128
BATCH, TOK, D = 4, 512, 256
CTX = 1601
KD = D // P
TT = TOK // P
NT = BATCH * TT
CHUNKS = 4
CW = 2 * -(-CTX // (2 * CHUNKS))
CTXP = CHUNKS * CW
CLAST = CTX - (CHUNKS - 1) * CW
CT = -(-CTX // P)
CTX_C, CTX_R = 2 * KD, -(-CT // TT)
SLOTS = TT + 2
CREM = CTX - (CT - 1) * P
E, H = 8, 1024
HT = H // P
TOP = (4, 2)
EPS = 1e-5
SCALE = 1.0 / float(np.sqrt(np.float32(D)))
BLOCK = 256
BT = BLOCK // P
NB = BATCH * TOK // BLOCK
M = NB * BT
SPARE = BATCH * TOK
ROWS = SPARE + BLOCK
ROW = D + E
STAGE = 1024
NSTAGE = 3

_COLS = [
    ("bq_c", KD), ("bv_s", KD), ("bq_s", KD), ("bk_c", KD), ("bv_c", KD), ("bg", KD),
    ("bq1", KD), ("bv1", KD), ("b1", E * HT), ("mixing", 2 * TT), ("gates", 4),
    ("lower", E * E), ("token", NT), ("spare", BT), ("gate_b", E), ("bk_s", KD), ("bk1", KD), ("router0", KD * E), ("router1", KD * E),
    ("bo", D), ("ident", P),
]
COL = {}
_at = 0
for _n, _w in _COLS:
    COL[_n] = (_at, _at + _w)
    _at += _w
NCOL = _at
PAIRED = COL["bk_s"][0], COL["router1"][1]


def f32(ap):
    return ap.bitcast(F32)


class Queue:

    def __init__(self, sem):
        self.sem, self.steps, self.count = sem, [], 0

    def do(self, step, after=()):
        need = {}
        for sem, value in after:
            if value > need.get(sem.name, (None, 0))[1]:
                need[sem.name] = (sem, value)
        self.steps.append((step, list(need.values())))
        self.count += 1
        return (self.sem, self.count)

    def plain(self, step):
        self.steps.append(("plain", step))

    def only_if(self, register, above):
        self.steps.append(("if", register, above, self.count))

    def end_ifs(self):
        self.steps.append(("end", self.count))

    def last(self):
        return (self.sem, self.count)

    def emit(self, engine):
        self.at, self.registers = 0, {}
        self._emit(engine, {}, 0)

    def _emit(self, engine, passed, depth):
        while self.at < len(self.steps):
            entry = self.steps[self.at]
            if entry[0] == "end":
                return
            self.at += 1
            if entry[0] == "plain":
                entry[1](engine, self.registers)
            elif entry[0] == "if":
                _, register, above, count = entry
                with engine.If(self.registers[register] > above):
                    self._emit(engine, dict(passed), depth + 1)
                end = self.steps[self.at][1]
                if end > count:
                    with engine.Else():
                        if count:
                            engine.wait_ge(self.sem, count)
                        engine.nop().then_inc(self.sem, end - count)
                if depth:
                    return
                self.at += 1
            else:
                step, need = entry
                for sem, value in need:
                    if passed.get(sem.name, 0) < value:
                        engine.wait_ge(sem, value)
                        passed[sem.name] = value
                step(engine).then_inc(self.sem, 1)


class Loads:

    def __init__(self):
        self.steps, self.total = [], {}

    def do(self, dst, src, sem, after=()):
        self.total[sem.name] = self.total.get(sem.name, 0) + 16
        self.steps.append((dst, src, sem, list(after)))
        return (sem, self.total[sem.name])

    def emit(self, engine):
        passed = {}
        for dst, src, sem, after in self.steps:
            for s, value in after:
                if passed.get(s.name, 0) < value:
                    engine.wait_ge(s, value)
                    passed[s.name] = value
            engine.dma_start(dst, src).then_inc(sem, 16)


class Buf:

    def __init__(self, *aps):
        self.aps = aps
        self.ready, self.free = [], []

    @property
    def hi(self):
        return self.aps[0]

    @property
    def lo(self):
        return self.aps[1]

    @property
    def ap(self):
        return self.aps[0]


class Ring:
    def __init__(self, bufs):
        self.bufs, self.n = bufs, 0

    def take(self):
        b = self.bufs[self.n % len(self.bufs)]
        self.n += 1
        return b


def build(nc, t, out):
    ctx = ExitStack()
    with ctx:
        def sem(name):
            return ctx.enter_context(nc.semaphore(name))

        pe, act, dve, pool = (Queue(sem(f"{n}_steps")) for n in ("pe", "act", "dve", "pool"))
        loads = Loads()
        engines = (pe, act, dve, pool)

        def sb(name, shape, dtype=F32, stack=ctx):
            return stack.enter_context(nc.sbuf_tensor(name, shape, dtype))

        def pair(name, shape, stack=ctx):
            hi, lo = sb(name + "_hi", shape, F32R, stack), sb(name + "_lo", shape, F32R, stack)
            whole = tuple(slice(None) for _ in shape)
            return Buf(hi[whole], lo[whole])

        ps = ctx.enter_context(nc.psum_tensor("banks", [P, 8, 512], F32))

        small = sb("small", [P, NCOL])
        small_p = pair("small_pair", [P, PAIRED[1] - PAIRED[0]])
        b2 = sb("b2", [E, D])
        stage = sb("stage", [P, NSTAGE, STAGE])
        tanh_g = sb("tanh_g", [P, 4])
        half_bg = sb("half_bg", [P, KD])
        minus_half = sb("minus_half", [P, TT])
        half = sb("half_consts", [P, 3 * P + M], F16)
        before, ones, places, tiles_m = (half[:, i * P:i * P + n] for i, n in enumerate((P, P, P, M)))
        xn = Buf(sb("xn", [P, TT, ROW])[:, :, :])
        turned = pair("turned", [P, KD, TOK])
        chosen = sb("chosen", [P, NT, E], F16)
        earlier = sb("earlier", [P, NT + 1, E], F16)
        lists = sb("lists", [P, E * M])
        shared = [sb(f"onehot{i}", [P, E * P], F16) for i in range(2)]
        onehot = Ring([Buf(s[:, :].rearrange("p (e q) -> p e q", e=E)) for s in shared])
        pairwise = shared[0][:, :].bitcast(F32)
        above, same = (pairwise[:, i * TT * E * E:(i + 1) * TT * E * E].rearrange("p (t a b) -> p t a b", t=TT, a=E)
                       for i in range(2))
        logits_row = shared[1][0:E, :].bitcast(F32)
        place = sb("place", [P, TT * E])
        place3 = pairwise[:, 0:E * M]
        place_i, part_i, tile_i = (sb(f"place_i{i}", [P, TT * E], I32) for i in range(3))
        part_h, tile_h = (sb(f"place_h{i}", [P, TT, E], F16) for i in range(2))
        tokens_at = sb("tokens_at", [P, TT, E, M], F16)
        list_i = sb("list_i", [P, E * M], I32)
        counts_i = sb("counts_i", [1, E], I32)
        logits = sb("logits", [P, TT, E])
        rank = sb("rank", [P, TT, E])
        peak = sb("peak", [P, TT])
        total = sb("total", [P, TT])

        class Norm:

            def __init__(self, name):
                self.stats = sb(name + "_stats", [P, TT, 6])
                self.moments = sb(name + "_moments", [P, TT, 2])
                self.rstd = sb(name + "_rstd", [P, TT])
                self.free = []

        norm_in, norm_out = Norm("norm_in"), Norm("norm_out")
        s_small, s_b2 = sem("small_in"), sem("b2_in")
        s_half = sem("half_in")
        s_x = [sem(f"x_in{b}") for b in range(3)]
        s_rows = [sem(f"rows_out{i}") for i in range(2)]
        s_acc = [sem(f"residual_out{i}") for i in range(2)]
        slots = Ring([Buf(stage[:, i, :]) for i in range(NSTAGE)])
        for i, s in enumerate(slots.bufs):
            s.sem = sem(f"stage{i}_in")

        def col(name, i=None, n=1):
            a, b = COL[name]
            return small[:, a:b] if i is None else small[:, a + i:a + i + n]

        ident = col("ident")

        t_small = loads.do(small[:, :], t["small"], s_small)
        t_half = loads.do(half[:, :], t["half"], s_half)
        t_b2 = loads.do(b2[:, :], t["b2"], s_b2)
        rows_d = [nc.dram_tensor(f"rows{i}", (ROWS, ROW), F32, kind="Internal").ap() for i in range(2)]
        acc_d = [nc.dram_tensor("residual0", (ROWS, D), F32, kind="Internal").ap(), out]
        t_zero = dve.do(lambda e: e.memset(xn.ap, 0.0))
        for i in range(2):
            for d, w, q in ((rows_d[i], ROW, s_rows[i]), (acc_d[i], D, s_acc[i])):
                z = loads.do(d[SPARE:ROWS, :].rearrange("(t p) d -> p t d", p=P), xn.ap[:, 0:BT, 0:w], q, [t_zero])
                xn.free.append(z)

        t_mh = pool.do(lambda e: e.memset(minus_half[:, :], -0.5))
        t_tanh = act.do(lambda e: e.activation(tanh_g[:, :], col("gates"), ACT.Tanh), [t_small])
        t_bg = dve.do(lambda e: e.tensor_scalar(half_bg[:, :], col("bg"), 0.5, None, ALU.mult), [t_small])
        t_bo = dve.do(lambda e: e.tensor_scalar(col("bo"), col("bo"), tanh_g[:, 1:2], None, ALU.mult), [t_tanh])
        t_sp = dve.do(lambda e: e.tensor_copy(small_p.hi, small[:, PAIRED[0]:PAIRED[1]]), [t_small])
        t_sp = dve.do(lambda e: e.tensor_tensor(small_p.lo, small[:, PAIRED[0]:PAIRED[1]], f32(small_p.hi),
                                                ALU.subtract), [t_sp])
        small_p.ready = [t_sp]

        def pcol(name, i, n):
            a = COL[name][0] - PAIRED[0] + i
            return small_p.hi[:, a:a + n], small_p.lo[:, a:a + n]

        def bring(src, n, hi, lo, after, first=dve, second=pool):
            slot = slots.take()
            landed = loads.do(slot.ap[:, :n], src, slot.sem, slot.free)
            view = slot.ap[:, :n]
            if len(hi.shape) == 3:
                view = view.rearrange("p (a b) -> p a b", a=hi.shape[1])
            copy = (lambda e: e.activation(hi, view, ACT.Copy)) if first is act else (lambda e: e.tensor_copy(hi, view))
            made = first.do(copy, [landed, *after])
            made = second.do(lambda e: e.tensor_tensor(lo, view, f32(hi), ALU.subtract), [made, *after])
            slot.free = [made]
            return made

        def three(e, dst, lhs, rhs, first, last):
            for n, (a, b) in enumerate(((lhs[0], rhs[0]), (lhs[0], rhs[1]), (lhs[1], rhs[0]))):
                mm = e.matmul(dst, a, b, start=first and n == 0, stop=last and n == 2, skip_group_check=True)
            return mm

        def split(src, hi, lo, after, bias=None):
            if bias is None:
                a = act.do(lambda e: e.activation(hi, src, ACT.Copy), after)
                return dve.do(lambda e: e.tensor_tensor(lo, src, f32(hi), ALU.subtract), [a, *after])
            a = act.do(lambda e: e.activation(hi, src, ACT.Identity, bias=bias), after)
            return dve.do(lambda e: e.scalar_tensor_tensor(lo, src, bias, f32(hi), ALU.add, ALU.subtract), [a, *after])

        def norm_stats(nb, x, ready):
            for i in range(TT):
                v = dve.do(lambda e, i=i: e.bn_stats(nb.stats[:, i, :], x.ap[:, i, :]), [*ready, *nb.free])
            for i in range(TT):
                v = dve.do(lambda e, i=i: e.bn_aggr(nb.moments[:, i, :], nb.stats[:, i, :]), [v])
            v = dve.do(lambda e: e.tensor_scalar(nb.rstd[:, :], nb.moments[:, :, 1], EPS, None, ALU.add), [v])
            v = pool.do(lambda e: e.tensor_tensor(nb.rstd[:, :], nb.rstd[:, :], minus_half[:, :], ALU.pow), [v, t_mh])
            for i in range(TT):
                v1 = dve.do(lambda e, i=i: e.tensor_scalar(xn.ap[:, i, 0:D], x.ap[:, i, :], nb.moments[:, i, 0:1],
                                                           nb.rstd[:, i:i + 1], ALU.subtract, ALU.mult), [v, *xn.free])
            xn.ready, xn.free, nb.free = [v1], [], [v1]

        def norm_turn(dst, banks):
            made = []
            for k in range(KD):
                bank = banks.take()

                def turn(e, k=k, bank=bank):
                    for i in range(TT):
                        mm = e.transpose(bank.ap[:, i * P:(i + 1) * P], xn.ap[:, i, k * P:(k + 1) * P], ident)
                    return mm
                m = pe.do(turn, [*xn.ready, *bank.free])
                bank.free = [split(bank.ap, dst.hi[:, k, :], dst.lo[:, k, :], [m, *dst.free])]
                made += bank.free
            xn.free = [m]
            dst.ready, dst.free = made, []

        def barrier():
            return [q.last() for q in engines]

        def attention(layer, start, x_d, x_there):
            st = ExitStack()
            two_way = layer == 0
            n = f"a{layer}_"
            gate_col = tanh_g[:, 2 * 0 + layer:2 * 0 + layer + 1]
            weights = pair(n + "weights", [P, t[f"aw{layer}"].shape[1]], st)
            ctx_c = pair(n + "ctx_cols", [P, KD, CTXP], st)
            ctx_r = pair(n + "ctx_rows", [P, CT, D], st)
            xl = pair(n + "xl", [P, KD, TOK], st)
            y = None if two_way else pair(n + "y", [P, KD, TOK], st)
            s0, s1, s3, s4 = (pair(n + f"cols{i}", [P, KD, TOK], st) for i in range(4))
            s2 = turned
            xs_ = [Buf(sb(n + f"x{i}", [P, TT, D], F32, st)[:, :, :]) for i in range(2 if two_way else 3)]
            probs = Ring([Buf(sb(n + f"probs{i}", [P, CTXP], F32, st)[:, :]) for i in range(2)])
            pt = Ring([pair(n + f"probs_t{i}", [P, TOK], st) for i in range(3)])
            pt_tail = pair(n + "probs_t_tail", [P, P], st)
            mixed = Ring([Buf(sb(n + f"mixed{i}", [P, D], F32, st)[:, :]) for i in range(2)])
            work = Buf(sb(n + "work", [P, KD, TOK], F32, st)[:, :, :])
            pc = Buf(sb(n + "pc", [P, TT, TOK], F32, st)[:, :, :]) if two_way else None
            rrow = work.ap[0:1, 0, :]
            rcol = Buf(sb(n + "rcol", [P, TT], F32, st)[:, :])
            NS = 4
            cells = [[Buf(sb(n + f"cell{i}_{j}", [P, 2], F32, st)[:, :]) for j in range(NS)] for i in range(4)]
            top, nbias, sums, rinv = (Ring(c) for c in cells)
            everything = [xl, s0, s1, s3, s4, *xs_, work, rcol, *probs.bufs, *pt.bufs, pt_tail, *mixed.bufs]
            everything += [b for c in cells for b in c] + ([pc] if two_way else [y])
            for b in everything:
                b.free = list(start)
            s2.free = [*s2.free, *start]
            weights.free = ctx_c.free = ctx_r.free = list(start)

            bank = [Buf(ps[:, i, :]) for i in range(8)]
            for b in bank:
                b.free = list(start)
            banks = Ring(bank[4:7])
            mix_bank = bank[7]
            score_banks = bank[:4]

            def load_weights(i):
                a, b = i * STAGE, (i + 1) * STAGE
                weights.ready = [bring(t[f"aw{layer}"][:, a:b], STAGE, weights.hi[:, a:b], weights.lo[:, a:b], weights.free)]
                w_ready.append(weights.ready)

            w_ready = []

            def wt(i, k, a=0, n=P):
                o = (i * KD + k) * D + a
                return weights.hi[:, o:o + n], weights.lo[:, o:o + n]

            def ctx_pieces(b):
                def some_cols(k, h):
                    half = CTXP // 2
                    c = slice(h * half, (h + 1) * half)
                    ready = bring(t["ctx_cols"][b, :, k, c], half, ctx_c.hi[:, k, c], ctx_c.lo[:, k, c], ctx_c.free, first)
                    ctx_c.ready = [*ctx_c.ready, ready] if (k, h) != (0, 0) else [ready]

                def some_rows(a):
                    m = min(TT, CT - a)
                    ready = bring(t["ctx_rows"][b, :, a:a + m, :], m * D, ctx_r.hi[:, a:a + m, :],
                                  ctx_r.lo[:, a:a + m, :], ctx_r.free, first)
                    ctx_r.ready = [*ctx_r.ready, ready] if a else [ready]
                return ([lambda k=k, h=h: some_cols(k, h) for k in range(KD) for h in range(2)]
                        + [lambda a=a: some_rows(a) for a in range(0, CT, TT)])

            first = dve if two_way else act

            def start_loads(number):
                for _ in range(number):
                    if to_load:
                        to_load.pop(0)()

            def load_sel(b, which):
                s4.ready = [bring(t["ctx_picked"][b, which], KD * TOK, s4.hi, s4.lo, s4.free)]

            def project(w, src, dst, bias, ready=None):
                made = []
                for m in range(KD):
                    bk = banks.take()

                    def mms(e, m=m, bk=bk):
                        for k in range(KD):
                            mm = three(e, bk.ap, wt(w, k, m * P), (src.hi[:, k, :], src.lo[:, k, :]), k == 0, k == KD - 1)
                        return mm
                    p = pe.do(mms, [*w_ready[w // 2], *src.ready, *bk.free])
                    bk.free = [split(bk.ap, dst.hi[:, m, :], dst.lo[:, m, :], [p, *dst.free], bias and bias(m))]
                    made += bk.free
                src.free = [p]
                dst.ready, dst.free = made, []
                return p

            def query_bias(q, name):
                bk = banks.take()

                def mms(e):
                    for k in range(KD):
                        mm = three(e, bk.ap[0:1, :], pcol(name, k, 1), (q.hi[:, k, :], q.lo[:, k, :]), k == 0, k == KD - 1)
                    return mm
                p = pe.do(mms, [*small_p.ready, *q.ready, *bk.free])
                a = act.do(lambda e: e.activation(rrow, bk.ap[0:1, :], ACT.Copy), [p, *work.free])
                bk.free = [a]
                bk2 = banks.take()

                def turn(e):
                    for i in range(TT):
                        mm = e.transpose(bk2.ap[:, i:i + 1], rrow[:, i * P:(i + 1) * P], ident[0:1, 0:1])
                    return mm
                p2 = pe.do(turn, [a, *bk2.free])
                work.free = [p2]
                v = dve.do(lambda e: e.tensor_copy(rcol.ap, bk2.ap[:, 0:TT]), [p2, *rcol.free])
                bk2.free = [v]
                rcol.ready, rcol.free = [v], []
                return p

            class Tile:
                pass

            def scores(i, g):
                o = Tile()
                sb_free = [z for bk in score_banks for z in bk.free]

                def mms(e):
                    for c in range(CHUNKS):
                        for k in range(KD):
                            mm = three(e, ps[:, c, 0:CW], (g.hi[:, k, i * P:(i + 1) * P], g.lo[:, k, i * P:(i + 1) * P]),
                                       (ctx_c.hi[:, k, c * CW:(c + 1) * CW], ctx_c.lo[:, k, c * CW:(c + 1) * CW]),
                                       k == 0, k == KD - 1)
                    return mm
                p = pe.do(mms, [*g.ready, *ctx_c.ready, *sb_free])
                mx, nb, sm, ri = top.take(), nbias.take(), sums.take(), rinv.take()
                o.p, o.rinv = probs.take(), ri
                v = dve.do(lambda e: e.tensor_reduce(mx.ap[:, 0:1], ps[:, 0:CHUNKS, 0:CW], AX.XY, ALU.max), [p, *mx.free])
                r = rcol.ap[:, i:i + 1]
                v2 = dve.do(lambda e: e.tensor_tensor(mx.ap[:, 1:2], mx.ap[:, 0:1], r, ALU.add), [v, *rcol.ready])
                v3 = dve.do(lambda e: e.tensor_scalar(nb.ap[:, 0:1], r, mx.ap[:, 1:2], SCALE, ALU.subtract, ALU.mult),
                            [v2, *nb.free])
                rcol.free = [v3]
                o.peak, o.softmax = v, (i, mx, nb, sm, v3)
                o.scored = p
                return o

            def softmax(o):
                i, mx, nb, sm, v3 = o.softmax
                full = (CHUNKS - 1) * CW
                a1 = act.do(lambda e: e.activation(o.p.ap[:, 0:full].rearrange("p (c w) -> p c w", w=CW),
                                                   ps[:, 0:CHUNKS - 1, 0:CW], ACT.Exp, bias=nb.ap[:, 0:1], scale=SCALE,
                                                   accum_out=sm.ap[:, 0:1]), [v3, *o.p.free, *sm.free])
                a2 = act.do(lambda e: e.activation(o.p.ap[:, full:CTX], ps[:, CHUNKS - 1, 0:CLAST], ACT.Exp,
                                                   bias=nb.ap[:, 0:1], scale=SCALE, accum_out=sm.ap[:, 1:2]), [v3])
                mx.free, nb.free, sm.ready = [v3], [a2], [a2]
                o.sums = sm
                for bk in score_banks:
                    bk.free = [o.peak, a2]
                o.p.ready = [a1, a2]

            groups = [list(range(a, min(a + TT, CT))) for a in range(0, CT, TT)]

            def turn_probs(o):
                o.turned = []
                for kts in groups:
                    bk, dst = banks.take(), pt_tail if kts[-1] == CT - 1 else pt.take()
                    w = CREM if kts[-1] == CT - 1 else P

                    def mms(e, kts=kts, bk=bk, w=w):
                        for j, kt in enumerate(kts):
                            mm = e.transpose(bk.ap[0:w, j * P:(j + 1) * P], o.p.ap[:, kt * P:kt * P + w], ident)
                        return mm
                    p = pe.do(mms, [*o.p.ready, *bk.free])
                    c = len(kts) * P
                    s = split(bk.ap[0:w, 0:c], dst.hi[0:w, 0:c], dst.lo[0:w, 0:c], [p, *dst.free])
                    bk.free, dst.ready, dst.free = [s], [s], []
                    o.turned.append((kts, dst, w, dst.ready))
                o.p.free = [p]

            def mix(o):
                for kts, dst, w, ready in o.turned:
                    def mms(e, kts=kts, dst=dst, w=w):
                        for j, kt in enumerate(kts):
                            c = slice(j * P, (j + 1) * P)
                            mm = three(e, mix_bank.ap[:, 0:D], (dst.hi[0:w, c], dst.lo[0:w, c]),
                                       (ctx_r.hi[0:w, kt, :], ctx_r.lo[0:w, kt, :]), kt == 0, kt == CT - 1)
                        return mm
                    p = pe.do(mms, [*ready, *ctx_r.ready, *mix_bank.free])
                    dst.free = [p]
                sm, ri = o.sums, o.rinv
                v = dve.do(lambda e: e.tensor_tensor(ri.ap[:, 1:2], sm.ap[:, 0:1], sm.ap[:, 1:2], ALU.add), [*sm.ready, *ri.free])
                ri.ready = [dve.do(lambda e: e.reciprocal(ri.ap[:, 0:1], ri.ap[:, 1:2]), [v])]
                sm.free = [v]
                o.mixed = mixed.take()
                a = act.do(lambda e: e.activation(o.mixed.ap, mix_bank.ap[:, 0:D], ACT.Copy, scale=o.rinv.ap[:, 0:1]),
                           [p, *o.rinv.ready, *o.mixed.free])
                mix_bank.free = [a]
                o.rinv.free = [a]
                o.mixed.ready = [a]
                o.multiplied = p

            def turn_mixed(i, o, dst):
                bk = banks.take()

                def mms(e):
                    for k in range(KD):
                        mm = e.transpose(bk.ap[:, k * P:(k + 1) * P], o.mixed.ap[:, k * P:(k + 1) * P], ident)
                    return mm
                p = pe.do(mms, [*o.mixed.ready, *bk.free])
                c = slice(i * P, (i + 1) * P)
                s = split(bk.ap[:, 0:KD * P].rearrange("p (k q) -> p k q", k=KD), dst.hi[:, :, c], dst.lo[:, :, c],
                          [p, *(dst.free if i == 0 else [])])
                bk.free, o.mixed.free = [s], [p]
                dst.ready = [s]

            def attend(g, dst, fill):
                tiles = []
                for i in range(TT + 2):
                    if 1 <= i <= TT:
                        turn_probs(tiles[i - 1])
                    if i < TT:
                        tiles.append(scores(i, g))
                        ctx_c.free = g.free = [tiles[i].scored]
                    if i >= 2:
                        turn_mixed(i - 2, tiles[i - 2], dst)
                    if i < TT:
                        softmax(tiles[i])
                    fill(i)
                    if 1 <= i <= TT:
                        mix(tiles[i - 1])
                        ctx_r.free = [tiles[i - 1].multiplied]
                dst.free = []

            def load_x(b):
                xb = xs_[b % len(xs_)]
                src = x_d[b * TOK:(b + 1) * TOK, :].rearrange("(t p) d -> p t d", p=P)
                xb.ready, xb.free = [loads.do(xb.ap, src, s_x[b % len(xs_)], [*xb.free, *x_there])], []
                return xb

            if two_way:
                WQ, WK, WV, WQS, WKC, WVC, WG = range(7)
                names = ("bq_c", "bk_s", "bv_s")
            else:
                WQ, WK, WV, WO = range(4)
                names = ("bq1", "bk1", "bv1")
            xls = [xl, xl] if two_way else [xl, s3]
            gs = [s1, s1] if two_way else [s1, s4]

            def project_queries(b):
                project(WQ, xls[b % 2], s0, lambda m: col(names[0], m))

            def project_keys(b):
                project(WK, s0, gs[b % 2], None)
                s0.free = [query_bias(s0, names[1])]

            xb = load_x(0)
            norm_stats(norm_in, xb, xb.ready)
            load_weights(0)
            norm_turn(xl, banks)
            to_load = ctx_pieces(0)
            start_loads(CTX_C)
            for i in range(1, t[f"aw{layer}"].shape[1] // STAGE):
                load_weights(i)
            start_loads(CTX_R)
            fills = [[] for _ in range(SLOTS)]

            x_next = None
            for b in range(BATCH):
                more = b + 1 < BATCH
                if b == 0:
                    project_queries(b)
                    project_keys(b)

                def back_keys():
                    project(WKC, xl, s3, lambda m: col("bk_c", m))
                    made = []
                    for h in range(2):
                        bk = banks.take()

                        def mms(e, h=h, bk=bk):
                            for j in range(2):
                                c = slice((2 * h + j) * P, (2 * h + j + 1) * P)
                                for k in range(KD):
                                    mm = three(e, bk.ap[:, j * D:(j + 1) * D], (xl.hi[:, k, c], xl.lo[:, k, c]),
                                               wt(WVC, k, 0, D), k == 0 and j == 0, k == KD - 1)
                            return mm
                        p = pe.do(mms, [*w_ready[WVC // 2], *xl.ready, *bk.free])
                        bk.free = [split(bk.ap, s0.hi[:, h, :], s0.lo[:, h, :], [p, *s0.free])]
                        made += bk.free
                    s0.ready, s0.free, xl.free = made, [], [p]

                def back_queries():
                    project(WQS, s4, s1, lambda m: col("bq_s", m))

                if two_way:
                    load_sel(b, 0)
                    fills[0].insert(0, back_keys)
                    fills[TT + 1] += [back_queries, lambda b=b: load_sel(b, 1)]
                if more:
                    def next_x(b=b):
                        nonlocal x_next
                        x_next = load_x(b + 1)
                    fills[TT - 1 if two_way else 0].append(next_x)
                    fills[TT].append(lambda: norm_stats(norm_in, x_next, x_next.ready))
                    if not two_way:
                        to_load += ctx_pieces(b + 1)
                        fills[TT] += [lambda: start_loads(1)]
                        fills[TT + 1] += [lambda: start_loads(1),
                                          lambda b=b: (norm_turn(xls[(b + 1) % 2], banks), project_queries(b + 1)),
                                          lambda: start_loads(1)]
                attend(gs[b % 2], s2, lambda i: [piece() for piece in fills[i]])
                fills = [[] for _ in range(SLOTS)]
                if more and two_way:
                    to_load += ctx_pieces(b + 1)
                if two_way:
                    for which in range(2):
                        if which:
                            back_queries()
                            start_loads(1)
                            if more:
                                norm_turn(xl, banks)
                        for i in range(TT):
                            bk = score_banks[i]

                            def mms(e, i=i, bk=bk):
                                c = slice(i * P, (i + 1) * P)
                                for k in range(KD):
                                    mm = three(e, bk.ap, (s1.hi[:, k, c], s1.lo[:, k, c]),
                                               (s3.hi[:, k, :], s3.lo[:, k, :]), k == 0, k == KD - 1)
                                return mm
                            p = pe.do(mms, [*s1.ready, *s3.ready, *bk.free])
                            mx, nb, sm, ri = top.take(), nbias.take(), sums.take(), rinv.take()
                            pr = probs.take()
                            v = dve.do(lambda e, bk=bk, mx=mx: e.tensor_reduce(mx.ap[:, 0:1], bk.ap, AX.X, ALU.max),
                                       [p, *mx.free])
                            v = dve.do(lambda e, nb=nb, mx=mx: e.tensor_scalar(nb.ap[:, 0:1], mx.ap[:, 0:1], -SCALE, None,
                                                                               ALU.mult), [v, *nb.free])
                            a = act.do(lambda e, bk=bk, nb=nb, sm=sm, pr=pr: e.activation(
                                pr.ap[:, 0:TOK], bk.ap, ACT.Exp, bias=nb.ap[:, 0:1], scale=SCALE,
                                accum_out=sm.ap[:, 0:1]), [v, *pr.free, *sm.free])
                            mx.free, nb.free, bk.free = [v], [a], [a]
                            v = dve.do(lambda e, ri=ri, sm=sm: e.reciprocal(ri.ap[:, 1:2], sm.ap[:, 0:1]), [a, *ri.free])
                            sm.free = [v]
                            w = col("mixing", which * TT + i)
                            v = dve.do(lambda e, ri=ri, w=w: e.tensor_tensor(ri.ap[:, 0:1], ri.ap[:, 1:2], w, ALU.mult), [v])
                            if which == 0:
                                v = act.do(lambda e, i=i, pr=pr, ri=ri: e.activation(
                                    pc.ap[:, i, :], pr.ap[:, 0:TOK], ACT.Copy, scale=ri.ap[:, 0:1]), [v, *pc.free])
                                pc.ready = [v]
                            else:
                                v = dve.do(lambda e, i=i, pr=pr, ri=ri: e.scalar_tensor_tensor(
                                    pc.ap[:, i, :], pr.ap[:, 0:TOK], ri.ap[:, 0:1], pc.ap[:, i, :], ALU.mult, ALU.add),
                                    [v, *pc.ready])
                            ri.free = pr.free = [v]
                            if i % 2:
                                start_loads(1)
                        s1.free = [p]
                    s3.free = [p]
                    pc.ready = [v]
                    project(WV, s2, s1, lambda m: col(names[2], m))
                    acc = score_banks[0:KD]
                    turned_pc = []

                    def turn_pc(j):
                        bk, dst = banks.take(), pt.take()

                        def mms(e):
                            for i in range(TT):
                                mm = e.transpose(bk.ap[:, i * P:(i + 1) * P], pc.ap[:, i, j * P:(j + 1) * P], ident)
                            return mm
                        p = pe.do(mms, [*pc.ready, *bk.free])
                        s = split(bk.ap, dst.hi, dst.lo, [p, *dst.free])
                        bk.free, dst.ready = [s], [s]
                        turned_pc.append((dst, p))

                    turn_pc(0)
                    turn_pc(1)
                    for j in range(TT):
                        dst = turned_pc[j][0]

                        def mms(e, j=j, dst=dst):
                            for m in range(KD):
                                o = (j % 2) * D + m * P
                                mm = three(e, acc[m].ap, (s0.hi[:, j // 2, o:o + P], s0.lo[:, j // 2, o:o + P]),
                                           (dst.hi, dst.lo), j == 0, j == TT - 1)
                            return mm
                        p = pe.do(mms, [*dst.ready, *s0.ready, *[z for q in acc for z in q.free]])
                        dst.free = [p]
                        if j + 2 < TT:
                            turn_pc(j + 2)
                            start_loads(1)
                    pc.free = [turned_pc[-1][1]]
                    s0.free = [p]
                    made = []
                    for m in range(KD):
                        acc[m].free = [split(acc[m].ap, s3.hi[:, m, :], s3.lo[:, m, :], [p, *s3.free], col("bv_c", m))]
                        made += acc[m].free
                    s3.ready, s3.free = made, []
                    diff, part = pc.ap[:, 0:KD, :], pc.ap[:, KD:2 * KD, :]
                    g_ = pool.do(lambda e: e.tensor_tensor(diff, f32(s1.hi), f32(s3.hi), ALU.subtract),
                                 [*s1.ready, *s3.ready, *pc.free])
                    v = dve.do(lambda e: e.tensor_tensor(part, f32(s1.lo), f32(s3.lo), ALU.subtract),
                               [*s1.ready, *s3.ready, *pc.free])
                    t_diff = dve.do(lambda e: e.tensor_tensor(diff, diff, part, ALU.add), [v, g_])
                    made = []
                    gate_banks = [banks.take() for _ in range(KD)]
                    for src, f0 in ((s1, 0), (s3, KD)):
                        for m in range(KD):
                            bk = gate_banks[m]

                            def mms(e, m=m, bk=bk, src=src, f0=f0):
                                for k in range(KD):
                                    o = (WG * KD + f0 + k) * D + m * P
                                    mm = three(e, bk.ap, (weights.hi[:, o:o + P], weights.lo[:, o:o + P]),
                                               (src.hi[:, k, :], src.lo[:, k, :]), f0 + k == 0, f0 + k == 2 * KD - 1)
                                return mm
                            p = pe.do(mms, [*w_ready[WG // 2], *src.ready, *(bk.free if f0 == 0 else [])])
                            if f0:
                                a = act.do(lambda e, m=m, bk=bk: e.activation(work.ap[:, m, :], bk.ap, ACT.Tanh,
                                                                              bias=half_bg[:, m:m + 1], scale=0.5),
                                           [p, *work.free, t_bg])
                                bk.free = [a]
                                made.append(a)
                    t_gate = p
                    v = dve.do(lambda e: e.scalar_tensor_tensor(diff, work.ap, 1.0, diff, ALU.add, ALU.mult),
                               [*made, t_diff])
                    v = dve.do(lambda e: e.scalar_tensor_tensor(work.ap, diff, 0.5, f32(s3.hi), ALU.mult, ALU.add), [v])
                    v = dve.do(lambda e: e.tensor_tensor(work.ap, work.ap, f32(s3.lo), ALU.add), [v])
                    pc.free = [v]
                    s1.free = [t_gate, t_diff]
                    s3.free = [t_gate, v]
                    work.ready = [v]
                    start_loads(1)
                    if more:
                        project_queries(b + 1)
                    for h in range(2):
                        bk = banks.take()

                        def turn(e, h=h, bk=bk):
                            for j in range(2):
                                c = slice((2 * h + j) * P, (2 * h + j + 1) * P)
                                for k in range(KD):
                                    o = j * D + k * P
                                    mm = e.transpose(bk.ap[:, o:o + P], work.ap[:, k, c], ident)
                            return mm
                        p = pe.do(turn, [*work.ready, *bk.free])
                        xs = xb.ap[:, 2 * h:2 * h + 2, :].rearrange("p t d -> p (t d)")
                        v = dve.do(lambda e, bk=bk, xs=xs: e.scalar_tensor_tensor(xs, bk.ap, gate_col, xs, ALU.mult, ALU.add),
                                   [p, t_tanh, *xb.ready])
                        bk.free = [v]
                    xb.ready = [v]
                    work.free = [p]
                    if more:
                        project_keys(b + 1)
                else:
                    xl_b = xls[b % 2]
                    start_loads(1)
                    made = []
                    for m in range(KD):
                        bk = banks.take()

                        def mms(e, m=m, bk=bk):
                            for k in range(KD):
                                mm = three(e, bk.ap, wt(WV, k, m * P), (s2.hi[:, k, :], s2.lo[:, k, :]), k == 0, k == KD - 1)
                            return mm
                        p = pe.do(mms, [*w_ready[WV // 2], *s2.ready, *bk.free])
                        v = dve.do(lambda e, m=m, bk=bk, xl_b=xl_b: e.scalar_tensor_tensor(
                            work.ap[:, m, :], bk.ap, col(names[2], m), f32(xl_b.hi)[:, m, :], ALU.add, ALU.add),
                            [p, *work.free])
                        bk.free = [v]
                        v = dve.do(lambda e, m=m, xl_b=xl_b: e.tensor_tensor(work.ap[:, m, :], work.ap[:, m, :],
                                                                             f32(xl_b.lo)[:, m, :], ALU.add), [v])
                        made.append(split(work.ap[:, m, :], y.hi[:, m, :], y.lo[:, m, :], [v, *y.free]))
                    s2.free = [p]
                    xl_b.free = [*xl_b.free, v]
                    work.free = made
                    y.ready, y.free = made, []
                    if more:
                        start_loads(1)
                        project_keys(b + 1)
                        start_loads(1)

                    def output(xb=xb):
                        for h in range(2):
                            bk = banks.take()

                            def mms(e, h=h, bk=bk):
                                for j in range(2):
                                    c = slice((2 * h + j) * P, (2 * h + j + 1) * P)
                                    for k in range(KD):
                                        mm = three(e, bk.ap[:, j * D:(j + 1) * D], (y.hi[:, k, c], y.lo[:, k, c]),
                                                   wt(WO, k, 0, D), k == 0 and j == 0, k == KD - 1)
                                return mm
                            p = pe.do(mms, [*w_ready[WO // 2], *y.ready, *bk.free])
                            xs = xb.ap[:, 2 * h:2 * h + 2, :].rearrange("p t d -> p (t d)")
                            v = dve.do(lambda e, bk=bk, xs=xs: e.scalar_tensor_tensor(xs, bk.ap, gate_col, xs, ALU.mult,
                                                                                      ALU.add), [p, t_tanh, *xb.ready])
                            bk.free = [v]
                            for j in range(2):
                                v = dve.do(lambda e, q=2 * h + j: e.tensor_tensor(xb.ap[:, q, :], xb.ap[:, q, :], col("bo"),
                                                                                  ALU.add), [v, t_bo])
                        xb.ready = [v]
                        y.free = [p]
                pieces = route(layer, b, xb, banks)
                if two_way:
                    norm_stats(norm_out, xb, xb.ready)
                else:
                    pieces = [lambda o=output, xb=xb: (o(), norm_stats(norm_out, xb, xb.ready)), *pieces[:-2],
                              lambda a=pieces[-2], z=pieces[-1]: (a(), z())]
                if more:
                    for i in range(2):
                        fills[i].append(lambda: start_loads(1))
                    for i, piece in enumerate(pieces):
                        fills[i].append(piece)
                    xb = x_next
            if not two_way:
                pieces.pop(0)()
            core_done = barrier()
            for piece in pieces:
                piece()
            lists_ready, counts_ready = finish_lists(banks)
            for b in bank:
                core_done += b.free
            st.close()
            return core_done, lists_ready, counts_ready

        routed = []

        def route(layer, b, xb, banks):
            s = {}
            tiles = range(b * TT, (b + 1) * TT)
            ch = chosen[:, b * TT:(b + 1) * TT, :]

            def find_logits():
                norm_turn(turned, banks)
                bk = banks.take()

                def mms(e):
                    for k in range(KD):
                        mm = three(e, bk.ap[0:E, :], pcol(f"router{layer}", k * E, E),
                                   (turned.hi[:, k, :], turned.lo[:, k, :]), k == 0, k == KD - 1)
                    return mm
                p = pe.do(mms, [*small_p.ready, *turned.ready, *bk.free])
                turned.free = [p]
                s["logits"] = act.do(lambda e: e.activation(logits_row, bk.ap[0:E, :], ACT.Copy), [p, *routed])
                bk.free = [s["logits"]]

            def choose():
                bk = banks.take()

                def turn(e):
                    for i in range(TT):
                        mm = e.transpose(bk.ap[:, i * E:(i + 1) * E], logits_row[:, i * P:(i + 1) * P], ident[0:E, 0:E])
                    return mm
                p = pe.do(turn, [s["logits"], *bk.free])
                lg = bk.ap[:, 0:TT * E].rearrange("p (t e) -> p t e", e=E)
                if layer == 0:
                    v = dve.do(lambda e: e.tensor_copy(logits[:, :, :], lg), [p, *routed])
                else:
                    gb = col("gate_b").unsqueeze(1).to_broadcast([P, TT, E])
                    v = dve.do(lambda e: e.tensor_tensor(logits[:, :, :], lg, gb, ALU.add), [p, *routed])
                bk.free = [v]
                other = logits[:, :, :].unsqueeze(2).to_broadcast([P, TT, E, E])
                own = logits[:, :, :].unsqueeze(3).to_broadcast([P, TT, E, E])
                low = col("lower").rearrange("p (a b) -> p a b", a=E).unsqueeze(1).to_broadcast([P, TT, E, E])
                v0 = dve.do(lambda e: e.tensor_reduce(peak[:, :], logits[:, :, :], AX.X, ALU.max), [v])
                v1 = dve.do(lambda e: e.tensor_tensor(above, other, own, ALU.is_gt), [v])
                v2 = dve.do(lambda e: e.tensor_tensor(same, other, own, ALU.is_equal), [v])
                v3 = dve.do(lambda e: e.tensor_tensor(logits[:, :, :], logits[:, :, :],
                                                      peak[:, :].unsqueeze(2).to_broadcast([P, TT, E]), ALU.subtract),
                            [v0, v1, v2])
                s["exp"] = act.do(lambda e: e.activation(logits[:, :, :], logits[:, :, :], ACT.Exp), [v3])
                v = dve.do(lambda e: e.tensor_tensor(same, same, low, ALU.mult), [v2])
                v = dve.do(lambda e: e.tensor_tensor(above, above, same, ALU.add), [v1, v])
                v = dve.do(lambda e: e.tensor_reduce(rank[:, :, :], above, AX.X, ALU.add), [v])
                s["chosen"] = v = dve.do(lambda e: e.tensor_scalar(ch, rank[:, :, :], float(TOP[layer]), None, ALU.is_lt), [v])
                if b == 0:
                    v = dve.do(lambda e: e.memset(earlier[:, 0, :], 0.0), [v])
                for i in tiles:
                    v = dve.do(lambda e, i=i: e.tensor_tensor(earlier[:, i + 1, :], earlier[:, i, :], chosen[:, i, :],
                                                              ALU.add), [v])
                s["earlier"] = v

            def weigh():
                gate_col = tanh_g[:, 2 + layer:3 + layer]
                weights = xn.ap[:, :, D:ROW]
                v = dve.do(lambda e: e.tensor_tensor(logits[:, :, :], logits[:, :, :], ch, ALU.mult), [s["chosen"], s["exp"]])
                v = dve.do(lambda e: e.tensor_reduce(total[:, :], logits[:, :, :], AX.X, ALU.add), [v])
                v = dve.do(lambda e: e.reciprocal(total[:, :], total[:, :]), [v])
                s["weights"] = dve.do(lambda e: e.scalar_tensor_tensor(
                    weights, logits[:, :, :], gate_col, total[:, :].unsqueeze(2).to_broadcast([P, TT, E]),
                    ALU.mult, ALU.mult), [v, t_tanh, *xn.ready])
                dst = rows_d[layer][b * TOK:(b + 1) * TOK, :].rearrange("(t p) d -> p t d", p=P)
                xn.free = [*xn.free, loads.do(dst, xn.ap, s_rows[layer], [s["weights"], *xn.ready])]
                if layer == 0:
                    send_residual()
                bk = banks.take()

                def mms(e):
                    i = b * TT
                    e.matmul(bk.ap[:, 0:TT * E], before, chosen[:, i:i + TT, :].rearrange("p t e -> p (t e)"), start=True,
                             stop=False, skip_group_check=True)
                    return e.matmul(bk.ap[:, 0:TT * E], ones, earlier[:, i:i + TT, :].rearrange("p t e -> p (t e)"),
                                    start=False, stop=True, skip_group_check=True)
                p = pe.do(mms, [s["earlier"], t_half, *bk.free])
                v = dve.do(lambda e: e.scalar_tensor_tensor(place[:, :], bk.ap[:, 0:TT * E], 1.0,
                                                            ch.rearrange("p t e -> p (t e)"), ALU.add, ALU.mult), [p, *routed])
                bk.free = [v]
                v = dve.do(lambda e: e.tensor_scalar(place_i[:, :], place[:, :], -1.0, None, ALU.add), [v])
                shift = P.bit_length() - 1
                v1 = dve.do(lambda e: e.tensor_scalar(tile_i[:, :], place_i[:, :], shift, None, ALU.arith_shift_right), [v])
                v2 = dve.do(lambda e: e.tensor_scalar(part_i[:, :], place_i[:, :], P - 1, None, ALU.bitwise_and), [v])
                v1 = dve.do(lambda e: e.tensor_copy(tile_h[:, :, :].rearrange("p t e -> p (t e)"), tile_i[:, :]), [v1])
                v2 = dve.do(lambda e: e.tensor_copy(part_h[:, :, :].rearrange("p t e -> p (t e)"), part_i[:, :]), [v2])
                s["part"] = v2
                v1 = dve.do(lambda e: e.tensor_tensor(
                    tokens_at[:, :, :, :].rearrange("p t e m -> p (t e) m"), tiles_m.unsqueeze(1).to_broadcast([P, TT * E, M]),
                    tile_h[:, :, :].rearrange("p t e -> p (t e)").unsqueeze(2).to_broadcast([P, TT * E, M]),
                    ALU.is_equal), [v1, t_half, *routed])
                flat = tokens_at[:, :, :, :].rearrange("p t e m -> p t (e m)")
                s["at"] = dve.do(lambda e: e.tensor_tensor(
                    flat, flat, col("token")[:, b * TT:(b + 1) * TT].unsqueeze(2).to_broadcast([P, TT, E * M]), ALU.mult), [v1])

            def send_residual():
                dst = acc_d[layer][b * TOK:(b + 1) * TOK, :].rearrange("(t p) d -> p t d", p=P)
                xb.free = [loads.do(dst, xb.ap, s_acc[layer], xb.ready)]

            def turn_weights():
                bk = banks.take()

                def turn(e):
                    for i in range(TT):
                        mm = e.transpose(bk.ap[0:E, i * P:(i + 1) * P], xn.ap[:, i, D:ROW], ident)
                    return mm
                p = pe.do(turn, [s["weights"], *bk.free])
                xn.free.append(p)
                s["turned"] = act.do(lambda e: e.activation(logits_row, bk.ap[0:E, :], ACT.Copy), [p, *routed])
                bk.free = [s["turned"]]

            def add_biases():
                for h in range(2):
                    bk = banks.take()

                    def mms(e, h=h, bk=bk):
                        for j in range(2):
                            c = slice((2 * h + j) * P, (2 * h + j + 1) * P)
                            mm = e.matmul(bk.ap[:, j * D:(j + 1) * D], logits_row[:, c], b2[:, :],
                                          start=j == 0, stop=True, skip_group_check=True)
                        return mm
                    p = pe.do(mms, [s["turned"], t_b2, *bk.free])
                    xs = xb.ap[:, 2 * h:2 * h + 2, :].rearrange("p t d -> p (t d)")
                    v = dve.do(lambda e, bk=bk, xs=xs: e.tensor_tensor(xs, xs, bk.ap, ALU.add), [p, *xb.ready])
                    bk.free = [v]
                xb.ready = [v]
                send_residual()

            def mark(i):
                oh = onehot.take()
                oh.ready = [dve.do(lambda e: e.tensor_tensor(
                    oh.ap, places.unsqueeze(1).to_broadcast([P, E, P]),
                    part_h[:, i, :].unsqueeze(2).to_broadcast([P, E, P]), ALU.is_equal), [s["part"], *xb.ready, *oh.free])]
                s[i] = oh

            def put(i):
                oh, bk = s[i], banks.take()

                def mms(e):
                    for x_ in range(E):
                        mm = e.matmul(bk.ap[:, x_ * M:(x_ + 1) * M], oh.ap[:, x_, :], tokens_at[:, i, x_, :],
                                      start=x_ == 0, stop=x_ == E - 1, skip_group_check=True)
                    return mm
                p = pe.do(mms, [s["at"], *oh.ready, *bk.free])
                before_ = [s["listed"]] if "listed" in s else routed
                if b == 0 and i == 0:
                    v = dve.do(lambda e: e.tensor_copy(lists[:, :], bk.ap[:, 0:E * M]), [p, *before_])
                else:
                    v = dve.do(lambda e: e.tensor_tensor(lists[:, :], lists[:, :], bk.ap[:, 0:E * M], ALU.add),
                               [p, *before_])
                oh.free, bk.free, s["listed"] = [p], [v], v
                if i == TT - 1:
                    routed[:] = [v, p]

            def weigh_and_place():
                weigh()
                if layer == 1:
                    turn_weights()
                mark(0)

            def put_first():
                if layer == 1:
                    add_biases()
                put(0)
                mark(1)

            def put_second():
                put(1)
                mark(2)
                mark(3)

            def put_rest():
                put(2)
                put(3)

            assert TT == 4
            return [find_logits, choose, weigh_and_place, put_first, put_second, put_rest]

        def finish_lists(banks):
            bk = banks.take()
            p = pe.do(lambda e: e.matmul(bk.ap[:, 0:E], ones, earlier[:, NT, :], start=True, stop=True,
                                         skip_group_check=True), [*routed, *bk.free])
            c = dve.do(lambda e: e.tensor_copy(counts_i[:, :], bk.ap[0:1, 0:E]), [p, *routed])
            bk.free = [c]
            spare = col("spare").unsqueeze(1).to_broadcast([P, E * NB, BT])
            ls = lists[:, :].rearrange("p (a t) -> p a t", t=BT)
            t_ = place3.rearrange("p (a t) -> p a t", t=BT)
            v = dve.do(lambda e: e.scalar_tensor_tensor(t_, ls, 0.0, spare, ALU.is_equal, ALU.mult), [*routed])
            v = dve.do(lambda e: e.scalar_tensor_tensor(list_i[:, :], lists[:, :], -1.0, place3, ALU.add, ALU.add), [v])
            return [v], [c]

        def experts(layer, start, list_ready, counts_ready):
            st = ExitStack()
            n = f"m{layer}_"
            gelu = (ACT.Gelu_apprx_tanh, ACT.Gelu)[layer]
            up_d, down_d = t[f"up{layer}"], t[f"down{layer}"]
            ups = [pair(n + f"up{i}", [P, KD, H], st) for i in range(2)]
            downs = [pair(n + f"down{i}", [P, HT, D], st) for i in range(2)]
            firsts, others = ([Buf(sb(n + f"{w}{i}", [P, BT, ROW], F32, st)[:, :, :]) for i in range(2)]
                              for w in ("first_block", "other_block"))
            for i in range(2):
                firsts[i].sem, others[i].sem = sem(n + f"first_in{i}"), sem(n + f"other_in{i}")
                firsts[i].count = 0
            xt = pair(n + "xt", [P, KD, BLOCK], st)
            act_out = Ring([Buf(sb(n + f"act_out{i}", [P, BLOCK], F32, st)[:, :]) for i in range(3)])
            hidden = [pair(n + f"hidden{f}", [P, BLOCK], st) for f in range(HT)]
            y = Buf(sb(n + "y", [P, BT, D], F32, st)[:, :, :])
            w_now, w_prev = (Buf(sb(n + f"w{i}", [P, BT], F32, st)[:, :]) for i in range(2))
            i_now, i_prev, i_out = (Buf(sb(n + f"i{i}", [P, BT], I32, st)[:, :]) for i in range(3))
            for b in (*ups, *downs, *firsts, *others, xt, *act_out.bufs, *hidden, y, w_now, w_prev, i_now, i_prev, i_out):
                b.free = list(start)
            bank = [Buf(ps[:, i, :]) for i in range(8)]
            for b in bank:
                b.free = list(start)
            up_banks = Ring(bank[0:5])
            x_bank, y_bank = bank[5], bank[6]
            s_add = sem(n + "added")
            rows_ready = (s_rows[layer], loads.total[s_rows[layer].name])
            acc_ready = (s_acc[layer], loads.total[s_acc[layer].name])

            def load_expert(e_, piece):
                u, d = ups[e_ % 2], downs[e_ % 2]
                if piece < KD:
                    src = up_d[e_].rearrange("(k p) f -> p k f", p=P)[:, piece, :]
                    u.ready = [bring(src, H, u.hi[:, piece, :], u.lo[:, piece, :], u.free)]
                else:
                    h = HT // 2
                    a = (piece - KD) * h
                    src = down_d[e_].rearrange("(f p) d -> p f d", p=P)[:, a:a + h, :]
                    d.ready = [bring(src, h * D, d.hi[:, a:a + h, :], d.lo[:, a:a + h, :], d.free, second=dve)]

            def counters(e, r):
                for key in ("adds", "others0", "others1"):
                    r[key] = e.alloc_register(n + key)
                    e.reg_mov(r[key], 0)
            pool.plain(counters)

            def others_in(i):
                def step(e):
                    e.wait_ge(others[i].sem, e.snap(pool.registers[f"others{i}"]))
                    e.wait_ge(pool.sem, before_step)
                    return e.nop()
                before_step = pool.count
                return pool.do(step)

            def gather_done(e_, j):
                g = others[j % 2] if j else firsts[e_ % 2]
                g.ready = [others_in(j % 2) if j else (g.sem, g.count)]
                return g

            def gather(e_, j):
                g = others[j % 2] if j else firsts[e_ % 2]
                rows = [list_i[:, e_ * M + j * BT + i:e_ * M + j * BT + i + 1] for i in range(BT)]

                def step(e):
                    for i in range(BT):
                        e.indirect_dma_start(out=g.ap[:, i, :], out_offset=None, in_=rows_d[layer],
                                             in_offset=bass.IndirectOffsetOnAxis(ap=rows[i], axis=0)).then_inc(g.sem, 16)
                    if j:
                        r = pool.registers[f"others{j % 2}"]
                        e.reg_add(r, r, 16 * BT)
                    e.wait_ge(pool.sem, before_step)
                    return e.nop()
                landed = []
                if j and not (e_ == 0 and j <= 2):
                    landed = [others_in(j % 2)]
                before_step = pool.count
                pool.do(step, [*list_ready, rows_ready, *landed, *g.free])
                if j == 0:
                    g.count += 16 * BT

            def add_done():
                def step(e):
                    e.wait_ge(s_add, e.snap(pool.registers["adds"]))
                    e.wait_ge(pool.sem, before_step)
                    return e.nop()
                before_step = pool.count
                return pool.do(step)

            def add():
                def step(e):
                    for i in range(BT):
                        e.indirect_dma_start(out=acc_d[layer], out_offset=bass.IndirectOffsetOnAxis(ap=i_out.ap[:, i:i + 1], axis=0),
                                             in_=y.ap[:, i, :], in_offset=None, compute_op=ALU.add).then_inc(s_add, 16)
                    e.reg_add(pool.registers["adds"], pool.registers["adds"], 16 * BT)
                    e.wait_ge(pool.sem, before_step)
                    return e.nop()
                before_step = pool.count
                pool.do(step, [acc_ready, *y.ready, *i_out.ready])

            def now_is_before():
                w_prev.ready = [dve.do(lambda e: e.tensor_copy(w_prev.ap, w_now.ap), [*w_prev.free, *w_now.ready])]
                i_prev.ready = [dve.do(lambda e: e.tensor_copy(i_prev.ap, i_now.ap), [*i_prev.free, *i_now.ready])]

            def block_in(e_, j, g):
                now_is_before()
                v = dve.do(lambda e: e.tensor_copy(w_now.ap, g.ap[:, :, D + e_]), [*w_prev.ready, *g.ready])
                w_now.ready = [v]
                o = e_ * M + j * BT
                v2 = dve.do(lambda e: e.tensor_copy(i_now.ap, list_i[:, o:o + BT]), [*i_prev.ready, *list_ready])
                i_now.ready = [v2]

                def turn(e):
                    for i in range(BT):
                        for k in range(KD):
                            c = k * BLOCK + i * P
                            mm = e.transpose(x_bank.ap[:, c:c + P], g.ap[:, i, k * P:(k + 1) * P], ident)
                    return mm
                p = pe.do(turn, [*g.ready, *x_bank.free])
                g.free = [v, p]
                src = x_bank.ap.rearrange("p (k t) -> p k t", k=KD)
                x_bank.free = [split(src, xt.hi, xt.lo, [p, *xt.free])]
                xt.ready = x_bank.free

            def up(e_, f):
                u, bk, a_, hb = ups[e_ % 2], up_banks.take(), act_out.take(), hidden[f]
                fs = slice(f * P, (f + 1) * P)
                dst = bk.ap[:, 0:BLOCK]

                def mms(e):
                    for k in range(KD):
                        mm = three(e, dst, (u.hi[:, k, fs], u.lo[:, k, fs]), (xt.hi[:, k, :], xt.lo[:, k, :]),
                                   k == 0, k == KD - 1)
                    return mm
                p = pe.do(mms, [*u.ready, *xt.ready, *bk.free])
                bias = {} if layer == 0 else {"bias": col("b1", e_ * HT + f)}
                a = act.do(lambda e: e.activation(a_.ap, dst, gelu, **bias), [p, *a_.free])
                bk.free = [a]
                a2 = act.do(lambda e: e.activation(hb.hi, a_.ap, ACT.Copy), [a, *hb.free])
                v = dve.do(lambda e: e.tensor_tensor(hb.lo, a_.ap, f32(hb.hi), ALU.subtract), [a2, *hb.free])
                a_.free, hb.ready, xt.free, u.free = [v], [v], [p], [p]

            def down(e_, f):
                d, hb = downs[e_ % 2], hidden[f]

                def mms(e):
                    for i in range(BT):
                        mm = three(e, y_bank.ap[:, i * D:(i + 1) * D], (hb.hi[:, i * P:(i + 1) * P], hb.lo[:, i * P:(i + 1) * P]),
                                   (d.hi[:, f, :], d.lo[:, f, :]), f == 0 and i == 0, f == HT - 1)
                    return mm
                p = pe.do(mms, [*d.ready, *hb.ready, *y_bank.free])
                hb.free = d.free = y_bank.ready = [p]

            def block_out():
                for i in range(BT):
                    a = act.do(lambda e, i=i: e.activation(y.ap[:, i, :], y_bank.ap[:, i * D:(i + 1) * D], ACT.Copy,
                                                           scale=w_prev.ap[:, i:i + 1]),
                               [*y_bank.ready, *w_prev.ready, *y.free])
                v = dve.do(lambda e: e.tensor_copy(i_out.ap, i_prev.ap), [*i_prev.ready, *y.free])
                y_bank.free, w_prev.free, i_prev.free, y.ready, i_out.ready = [a], [a], [v], [a], [v]

            y.ready = [pool.do(lambda e: e.memset(y.ap, 0.0), y.free)]
            spare = col("spare")
            for b in (i_out, i_now):
                b.ready = [dve.do(lambda e, b=b: e.tensor_scalar(b.ap, spare, -1.0, None, ALU.add), [t_small, *b.free])]
            w_now.ready = [dve.do(lambda e: e.memset(w_now.ap, 0.0), w_now.free)]
            for piece in range(4):
                load_expert(0, piece)

            for q in (pe, act, dve, pool):
                def get_counts(e, r, q=q):
                    for sem_, value in counts_ready:
                        e.wait_ge(sem_, value)
                    for e_ in range(E):
                        r[e_] = e.snap(e.value_load(counts_i[0:1, e_:e_ + 1], min_val=0, max_val=BATCH * TOK))
                q.plain(get_counts)
            add()
            for j in range(3):
                gather(0, j)

            for e_ in range(E):
                for j in range(NB):
                    first = e_ == 0 and j == 0
                    if j:
                        for q in engines:
                            q.only_if(e_, BLOCK * j)
                    g = gather_done(e_, j)
                    if j + 1 < NB and not (e_ == 0 and j <= 1):
                        gather(e_, j + 1)
                    if j == 0 and e_ + 1 < E:
                        gather(e_ + 1, 0)
                    y.free = [add_done()]
                    block_in(e_, j, g)
                    ups_, downs_ = list(range(HT)), list(range(HT))
                    before_e = e_ if j else e_ - 1
                    if not first:
                        for _ in range(3):
                            down(before_e, downs_.pop(0))
                    for _ in range(HT):
                        f = ups_.pop(0)
                        up(e_, f)
                        if not first and downs_:
                            down(before_e, downs_.pop(0))
                            if not downs_:
                                block_out()
                        if j == 0 and e_ + 1 < E and f in (0, 2, 4, 5):
                            load_expert(e_ + 1, (0, 2, 4, 5).index(f))
                    if not first:
                        add()
                for q in engines:
                    q.end_ifs()
            y.free = [add_done()]
            now_is_before()
            for f in range(HT):
                down(E - 1, f)
            block_out()
            add()
            t_done = add_done()
            routed[:] = [t_done, t_done]
            st.close()
            return t_done

        done = attention(0, [], t["x"], [])
        done = experts(0, *done)
        done = attention(1, barrier(), acc_d[0], [done])
        done = experts(1, *done)

        block = ctx.enter_context(nc.Block())

        @block.sync
        def _(e):
            loads.emit(e)
            e.wait_ge(*done)

        @block.tensor
        def _(e):
            pe.emit(e)

        @block.scalar
        def _(e):
            act.emit(e)

        @block.vector
        def _(e):
            dve.emit(e)

        @block.gpsimd
        def _(e):
            pool.emit(e)


def columns(w):
    a, b = w.shape
    return w.reshape(a // P, P, b).transpose(1, 0, 2).reshape(P, -1)


def kernel(**inputs):
    import concourse.bacc as _bacc
    from concourse.bass_utils import run_bass_kernel_spmd as _run

    g = {k: np.asarray(v) for k, v in inputs.items()}
    a = {}
    a["x"] = g["x"].reshape(BATCH * TOK, D)
    ctx = g["ctx_1024"]
    padded = np.concatenate([ctx, np.repeat(ctx[:, -1:], CTXP - CTX, axis=1)], axis=1)
    a["ctx_cols"] = padded.transpose(0, 2, 1).reshape(BATCH, KD, P, CTXP).transpose(0, 2, 1, 3)
    rows = np.concatenate([ctx, np.repeat(ctx[:, -1:], CT * P - CTX, axis=1)], axis=1)
    a["ctx_rows"] = rows.reshape(BATCH, CT, P, D).transpose(0, 2, 1, 3)
    one = np.float32(1)
    pos = (np.arange(TOK, dtype=np.float32) + np.float32(0.5)) * np.float32(CTX / TOK) - np.float32(0.5)
    pos = np.clip(pos, np.float32(0), np.float32(CTX - 1))
    lo = np.floor(pos).astype(np.int32)
    hi = np.minimum(lo + 1, CTX - 1)
    share = pos - lo.astype(np.float32)
    picked = np.stack([ctx[:, lo], ctx[:, hi]], axis=1)
    a["ctx_picked"] = picked.transpose(0, 1, 3, 2).reshape(BATCH, 2, KD, P, TOK).transpose(0, 1, 3, 2, 4).reshape(
        BATCH, 2, P, KD * TOK)
    L0, L1 = "L0_xattn_", "L1_xattn_"
    a["aw0"] = np.concatenate([columns(w) for w in (
        g[L0 + "Wq_c"].T, g[L0 + "Wk_s"], g[L0 + "Wv_s"].T, g[L0 + "Wq_s"].T, g[L0 + "Wk_c"].T, g[L0 + "Wv_c"].T,
        g[L0 + "Wg"].T)], axis=1)
    a["aw1"] = np.concatenate([columns(w) for w in (
        g[L1 + "Wq"].T, g[L1 + "Wk"], g[L1 + "Wv"].T, g[L1 + "Wo"].T)], axis=1)
    a["up0"], a["down0"] = g["L0_ffn_up_w"], g["L0_ffn_down_w"]
    a["up1"], a["down1"] = g["L1_ffn_w1"], g["L1_ffn_w2"]
    a["b2"] = g["L1_ffn_b2"]

    def vec(v):
        return v.reshape(-1, P).T

    def rows_of(v):
        return np.broadcast_to(v.reshape(1, -1), (P, v.size))
    parts = {
        "bq_c": vec(g[L0 + "bq_c"]), "bv_s": vec(g[L0 + "bv_s"]), "bq_s": vec(g[L0 + "bq_s"]), "bk_c": vec(g[L0 + "bk_c"]),
        "bv_c": vec(g[L0 + "bv_c"]), "bg": vec(g[L0 + "bg"]), "bq1": vec(g[L1 + "bq"]), "bv1": vec(g[L1 + "bv"]),
        "b1": vec(g["L1_ffn_b1"]), "mixing": np.concatenate([vec(one - share), vec(share)], axis=1),
        "gates": rows_of(np.concatenate([g["g_xattn"], g["g_ffn"]])),
        "lower": rows_of(np.tril(np.ones((E, E), np.float32), -1)), "gate_b": rows_of(g["L1_ffn_gate_b"]),
        "token": (np.arange(NT, dtype=np.float32)[None, :] * P + np.arange(P, dtype=np.float32)[:, None] + 1),
        "spare": (SPARE + 1 + np.arange(BT, dtype=np.float32)[None, :] * P + np.arange(P, dtype=np.float32)[:, None]),
        "bk_s": vec(g[L0 + "bk_s"]), "bk1": vec(g[L1 + "bk"]), "router0": columns(g["L0_ffn_router_w"]),
        "router1": columns(g["L1_ffn_gate_w"]), "bo": rows_of(g[L1 + "bo"]), "ident": np.eye(P, dtype=np.float32),
    }
    a["small"] = np.concatenate([parts[n] for n, _ in _COLS], axis=1)
    a["half"] = np.concatenate([np.triu(np.ones((P, P)), 1), np.ones((P, P)), np.tile(np.arange(P), (P, 1)),
                                np.tile(np.arange(M), (P, 1))], axis=1).astype(np.float16)

    nc = _bacc.Bacc("TRN2", target_bir_lowering=False, num_devices=1)
    arrays, handles = {}, {}
    for name, v in a.items():
        v = np.ascontiguousarray(v)
        arrays[f"in_{name}"] = v
        handles[name] = nc.dram_tensor(f"in_{name}", v.shape, mybir.dt.from_np(v.dtype), kind="ExternalInput").ap()
    out = nc.dram_tensor("out_x", (ROWS, D), F32, kind="ExternalOutput").ap()
    build(nc, handles, out)
    r = _run(nc, [arrays], core_ids=[0])
    return r.results[0]["out_x"][:BATCH * TOK].reshape(BATCH, TOK, D)
```

```python
from contextlib import ExitStack

import numpy as np

import concourse.bass as bass
from concourse import mybir

F32 = mybir.dt.float32
F16 = mybir.dt.float16
I32 = mybir.dt.int32
F32R = mybir.dt.float32r
ALU = mybir.AluOpType
ACT = mybir.ActivationFunctionType
AX = mybir.AxisListType

P = 128
BATCH, TOK, D = 4, 512, 256
CTX = 1601
KD = D // P
TT = TOK // P
NT = BATCH * TT
CHUNKS = 4
CW = 2 * -(-CTX // (2 * CHUNKS))
CTXP = CHUNKS * CW
CLAST = CTX - (CHUNKS - 1) * CW
CT = -(-CTX // P)
CTX_C, CTX_R = 2 * KD, -(-CT // TT)
SLOTS = TT + 2
CREM = CTX - (CT - 1) * P
E, H = 8, 1024
HT = H // P
TOP = (4, 2)
EPS = 1e-5
SCALE = 1.0 / float(np.sqrt(np.float32(D)))
BLOCK = 256
BT = BLOCK // P
NB = BATCH * TOK // BLOCK
M = NB * BT
SPARE = BATCH * TOK
ROWS = SPARE + BLOCK
ROW = D + E
STAGE = 1024
NSTAGE = 3
CONVERT_AT = (2, 3, 6, 7)

_COLS = [
    ("bv_s", KD), ("bq_s", KD), ("bk_c", KD), ("bv_c", KD), ("bg", KD),
    ("bv1", KD), ("b1", E * HT), ("mixing", 2 * TT), ("gates", 4),
    ("lower", E * E), ("token", NT), ("spare", BT), ("gate_b", E), ("bk_s", KD), ("bk1", KD), ("bq_c", KD), ("bq1", KD), ("router0", KD * E), ("router1", KD * E),
    ("bo", D), ("ident", P),
]
COL = {}
_at = 0
for _n, _w in _COLS:
    COL[_n] = (_at, _at + _w)
    _at += _w
NCOL = _at
PAIRED = COL["bk_s"][0], COL["router1"][1]


def f32(ap):
    return ap.bitcast(F32)


class Queue:

    def __init__(self, sem):
        self.sem, self.steps, self.count = sem, [], 0

    def do(self, step, after=()):
        need = {}
        for sem, value in after:
            if value > need.get(sem.name, (None, 0))[1]:
                need[sem.name] = (sem, value)
        self.steps.append((step, list(need.values())))
        self.count += 1
        return (self.sem, self.count)

    def plain(self, step):
        self.steps.append(("plain", step))

    def only_if(self, register, above):
        self.steps.append(("if", register, above, self.count))

    def end_ifs(self):
        self.steps.append(("end", self.count))

    def last(self):
        return (self.sem, self.count)

    def emit(self, engine):
        self.at, self.registers = 0, {}
        self._emit(engine, {}, 0)

    def _emit(self, engine, passed, depth):
        while self.at < len(self.steps):
            entry = self.steps[self.at]
            if entry[0] == "end":
                return
            self.at += 1
            if entry[0] == "plain":
                entry[1](engine, self.registers)
            elif entry[0] == "if":
                _, register, above, count = entry
                with engine.If(self.registers[register] > above):
                    self._emit(engine, dict(passed), depth + 1)
                end = self.steps[self.at][1]
                if end > count:
                    with engine.Else():
                        if count:
                            engine.wait_ge(self.sem, count)
                        engine.nop().then_inc(self.sem, end - count)
                if depth:
                    return
                self.at += 1
            else:
                step, need = entry
                for sem, value in need:
                    if passed.get(sem.name, 0) < value:
                        engine.wait_ge(sem, value)
                        passed[sem.name] = value
                step(engine).then_inc(self.sem, 1)


class Loads:

    def __init__(self):
        self.steps, self.total = [], {}

    def do(self, dst, src, sem, after=()):
        self.total[sem.name] = self.total.get(sem.name, 0) + 16
        self.steps.append((dst, src, sem, list(after)))
        return (sem, self.total[sem.name])

    def emit(self, engine):
        passed = {}
        for dst, src, sem, after in self.steps:
            for s, value in after:
                if passed.get(s.name, 0) < value:
                    engine.wait_ge(s, value)
                    passed[s.name] = value
            engine.dma_start(dst, src).then_inc(sem, 16)


class Buf:

    def __init__(self, *aps):
        self.aps = aps
        self.ready, self.free = [], []

    @property
    def hi(self):
        return self.aps[0]

    @property
    def lo(self):
        return self.aps[1]

    @property
    def ap(self):
        return self.aps[0]


class Ring:
    def __init__(self, bufs):
        self.bufs, self.n = bufs, 0

    def take(self):
        b = self.bufs[self.n % len(self.bufs)]
        self.n += 1
        return b


def build(nc, t, out):
    ctx = ExitStack()
    with ctx:
        def sem(name):
            return ctx.enter_context(nc.semaphore(name))

        pe, act, dve, pool = (Queue(sem(f"{n}_steps")) for n in ("pe", "act", "dve", "pool"))
        loads = Loads()
        engines = (pe, act, dve, pool)

        def sb(name, shape, dtype=F32, stack=ctx):
            return stack.enter_context(nc.sbuf_tensor(name, shape, dtype))

        def pair(name, shape, stack=ctx):
            hi, lo = sb(name + "_hi", shape, F32R, stack), sb(name + "_lo", shape, F32R, stack)
            whole = tuple(slice(None) for _ in shape)
            return Buf(hi[whole], lo[whole])

        ps = ctx.enter_context(nc.psum_tensor("banks", [P, 8, 512], F32))

        small = sb("small", [P, NCOL])
        small_p = pair("small_pair", [P, PAIRED[1] - PAIRED[0]])
        b2 = sb("b2", [E, D])
        stage = sb("stage", [P, NSTAGE, STAGE])
        tanh_g = sb("tanh_g", [P, 4])
        half_bg = sb("half_bg", [P, KD])
        minus_half = sb("minus_half", [P, TT])
        half = sb("half_consts", [P, 3 * P + M], F16)
        before, ones, places, tiles_m = (half[:, i * P:i * P + n] for i, n in enumerate((P, P, P, M)))
        xn = Buf(sb("xn", [P, TT, ROW])[:, :, :])
        turned = pair("turned", [P, KD, TOK])
        chosen = sb("chosen", [P, NT, E], F16)
        earlier = sb("earlier", [P, NT + 1, E], F16)
        lists = sb("lists", [P, E * M])
        shared = [sb(f"onehot{i}", [P, E * P], F16) for i in range(2)]
        onehot = Ring([Buf(s[:, :].rearrange("p (e q) -> p e q", e=E)) for s in shared])
        pairwise = shared[0][:, :].bitcast(F32)
        above, same = (pairwise[:, i * TT * E * E:(i + 1) * TT * E * E].rearrange("p (t a b) -> p t a b", t=TT, a=E)
                       for i in range(2))
        logits_row = shared[1][0:E, :].bitcast(F32)
        place = sb("place", [P, TT * E])
        place3 = pairwise[:, 0:E * M]
        place_i, part_i, tile_i = (sb(f"place_i{i}", [P, TT * E], I32) for i in range(3))
        part_h, tile_h = (sb(f"place_h{i}", [P, TT, E], F16) for i in range(2))
        tokens_at = sb("tokens_at", [P, TT, E, M], F16)
        list_i = sb("list_i", [P, E * M], I32)
        counts_i = sb("counts_i", [1, E], I32)
        logits = sb("logits", [P, TT, E])
        rank = sb("rank", [P, TT, E])
        peak = sb("peak", [P, TT])
        total = sb("total", [P, TT])

        class Norm:

            def __init__(self, name):
                self.stats = sb(name + "_stats", [P, TT, 6])
                self.moments = sb(name + "_moments", [P, TT, 2])
                self.rstd = sb(name + "_rstd", [P, TT])
                self.free = []

        norm_in, norm_out = Norm("norm_in"), Norm("norm_out")
        s_small, s_b2 = sem("small_in"), sem("b2_in")
        s_half = sem("half_in")
        s_x = [sem(f"x_in{b}") for b in range(3)]
        s_rows = [sem(f"rows_out{i}") for i in range(2)]
        s_acc = [sem(f"residual_out{i}") for i in range(2)]
        slots = Ring([Buf(stage[:, i, :]) for i in range(NSTAGE)])
        for i, s in enumerate(slots.bufs):
            s.sem = sem(f"stage{i}_in")

        def col(name, i=None, n=1):
            a, b = COL[name]
            return small[:, a:b] if i is None else small[:, a + i:a + i + n]

        ident = col("ident")

        t_small = loads.do(small[:, :], t["small"], s_small)
        rows_d = [nc.dram_tensor(f"rows{i}", (ROWS, ROW), F32, kind="Internal").ap() for i in range(2)]
        acc_d = [nc.dram_tensor("residual0", (ROWS, D), F32, kind="Internal").ap(), out]
        t_half, t_b2 = (s_half, 16), (s_b2, 16)

        def later_loads():
            loads.do(half[:, :], t["half"], s_half)
            loads.do(b2[:, :], t["b2"], s_b2)
            zeros = f32(turned.hi).rearrange("p k t -> p (k t)")[:, 0:BT * ROW].rearrange("p (t d) -> p t d", t=BT)
            t_zero = dve.do(lambda e: e.memset(zeros, 0.0))
            for i in range(2):
                for d, w, q in ((rows_d[i], ROW, s_rows[i]), (acc_d[i], D, s_acc[i])):
                    turned.free.append(loads.do(d[SPARE:ROWS, :].rearrange("(t p) d -> p t d", p=P), zeros[:, :, 0:w],
                                                q, [t_zero]))

        t_mh = pool.do(lambda e: e.memset(minus_half[:, :], -0.5))
        t_tanh = act.do(lambda e: e.activation(tanh_g[:, :], col("gates"), ACT.Tanh), [t_small])
        t_bg = dve.do(lambda e: e.tensor_scalar(half_bg[:, :], col("bg"), 0.5, None, ALU.mult), [t_small])
        t_bo = dve.do(lambda e: e.tensor_scalar(col("bo"), col("bo"), tanh_g[:, 1:2], None, ALU.mult), [t_tanh])
        t_sp = dve.do(lambda e: e.tensor_copy(small_p.hi, small[:, PAIRED[0]:PAIRED[1]]), [t_small])
        t_sp = dve.do(lambda e: e.tensor_tensor(small_p.lo, small[:, PAIRED[0]:PAIRED[1]], f32(small_p.hi),
                                                ALU.subtract), [t_sp])
        small_p.ready = [t_sp]

        def pcol(name, i, n):
            a = COL[name][0] - PAIRED[0] + i
            return small_p.hi[:, a:a + n], small_p.lo[:, a:a + n]

        def fetch(src, n):
            slot = slots.take()
            slot.ready = [loads.do(slot.ap[:, :n], src, slot.sem, slot.free)]
            return slot, n

        def convert(piece, hi, lo, after, first=dve, second=pool):
            slot, n = piece
            view = slot.ap[:, :n]
            if len(hi.shape) == 3:
                view = view.rearrange("p (a b) -> p a b", a=hi.shape[1])
            copy = (lambda e: e.activation(hi, view, ACT.Copy)) if first is act else (lambda e: e.tensor_copy(hi, view))
            made = first.do(copy, [*slot.ready, *after])
            made = second.do(lambda e: e.tensor_tensor(lo, view, f32(hi), ALU.subtract), [made, *after])
            slot.free = [made]
            return made

        def bring(src, n, hi, lo, after, first=dve, second=pool):
            return convert(fetch(src, n), hi, lo, after, first, second)

        def three(e, dst, lhs, rhs, first, last):
            for n, (a, b) in enumerate(((lhs[0], rhs[0]), (lhs[0], rhs[1]), (lhs[1], rhs[0]))):
                mm = e.matmul(dst, a, b, start=first and n == 0, stop=last and n == 2, skip_group_check=True)
            return mm

        def split(src, hi, lo, after, bias=None):
            if bias is None:
                a = act.do(lambda e: e.activation(hi, src, ACT.Copy), after)
                return dve.do(lambda e: e.tensor_tensor(lo, src, f32(hi), ALU.subtract), [a, *after])
            a = act.do(lambda e: e.activation(hi, src, ACT.Identity, bias=bias), after)
            return dve.do(lambda e: e.scalar_tensor_tensor(lo, src, bias, f32(hi), ALU.add, ALU.subtract), [a, *after])

        def norm_measure(nb, x, ready):
            for i in range(TT):
                v = dve.do(lambda e, i=i: e.bn_stats(nb.stats[:, i, :], x.ap[:, i, :]), [*ready, *nb.free])
            for i in range(TT):
                v = dve.do(lambda e, i=i: e.bn_aggr(nb.moments[:, i, :], nb.stats[:, i, :]), [v])
            v = dve.do(lambda e: e.tensor_scalar(nb.rstd[:, :], nb.moments[:, :, 1], EPS, None, ALU.add), [v])
            nb.ready = [pool.do(lambda e: e.tensor_tensor(nb.rstd[:, :], nb.rstd[:, :], minus_half[:, :], ALU.pow), [v, t_mh])]

        def norm_apply(nb, x):
            for i in range(TT):
                v1 = dve.do(lambda e, i=i: e.tensor_scalar(xn.ap[:, i, 0:D], x.ap[:, i, :], nb.moments[:, i, 0:1],
                                                           nb.rstd[:, i:i + 1], ALU.subtract, ALU.mult),
                            [*nb.ready, *x.ready, *xn.free])
            xn.ready, xn.free, nb.free = [v1], [], [v1]

        def norm_turn(dst, banks):
            made = []
            for k in range(KD):
                bank = banks.take()

                def turn(e, k=k, bank=bank):
                    for i in range(TT):
                        mm = e.transpose(bank.ap[:, i * P:(i + 1) * P], xn.ap[:, i, k * P:(k + 1) * P], ident)
                    return mm
                m = pe.do(turn, [*xn.ready, *bank.free])
                bank.free = [split(bank.ap, dst.hi[:, k, :], dst.lo[:, k, :], [m, *dst.free])]
                made += bank.free
            xn.free = [m]
            dst.ready, dst.free = made, []

        def barrier():
            return [q.last() for q in engines]

        class Operands:

            def __init__(self, layer, free):
                n = f"a{layer}_"
                self.layer, self.stack = layer, ExitStack()
                self.weights = pair(n + "weights", [P, t[f"aw{layer}"].shape[1]], self.stack)
                self.ctx_c = pair(n + "ctx_cols", [P, KD, CTXP], self.stack)
                self.ctx_r = pair(n + "ctx_rows", [P, CT, D], self.stack)
                for b in (self.weights, self.ctx_c, self.ctx_r):
                    b.free = list(free)
                self.w_ready = {}
                self.first = dve if layer == 0 else act

            def fetch_weights(self, i, first=None, second=pool):
                a, b = i * STAGE, (i + 1) * STAGE
                w, piece = self.weights, fetch(t[f"aw{self.layer}"][:, i * STAGE:(i + 1) * STAGE], STAGE)

                def rest():
                    self.w_ready[i] = [convert(piece, w.hi[:, a:b], w.lo[:, a:b], w.free, first or self.first, second)]
                return rest

            def load_weights(self, i, first=None, second=pool):
                self.fetch_weights(i, first, second)()

            def context(self, b, first=None, other=pool):
                c_, r_, first = self.ctx_c, self.ctx_r, first or self.first

                def some_cols(k, h, second):
                    half = CTXP // 2
                    c = slice(h * half, (h + 1) * half)
                    piece = fetch(t["ctx_cols"][b, :, k, c], half)

                    def rest():
                        ready = convert(piece, c_.hi[:, k, c], c_.lo[:, k, c], c_.free, first, second)
                        c_.ready = [*c_.ready, ready] if (k, h) != (0, 0) else [ready]
                    return rest

                def some_rows(a, second):
                    m = min(TT, CT - a)
                    piece = fetch(t["ctx_rows"][b, :, a:a + m, :], m * D)

                    def rest():
                        ready = convert(piece, r_.hi[:, a:a + m, :], r_.lo[:, a:a + m, :], r_.free, first, second)
                        r_.ready = [*r_.ready, ready] if a else [ready]
                    return rest
                return ([lambda k=k, h=h: some_cols(k, h, (pool, other)[h]) for k in range(KD) for h in range(2)]
                        + [lambda a=a: some_rows(a, (pool, other)[a // TT % 2]) for a in range(0, CT, TT)])

        def attention(layer, ops, start, x_d, x_there):
            st = ExitStack()
            two_way = layer == 0
            n = f"a{layer}_"
            gate_col = tanh_g[:, 2 * 0 + layer:2 * 0 + layer + 1]
            weights, ctx_c, ctx_r, w_ready = ops.weights, ops.ctx_c, ops.ctx_r, ops.w_ready
            xl = pair(n + "xl", [P, KD, TOK], st)
            y = None if two_way else pair(n + "y", [P, KD, TOK], st)
            s0, s1, s3, s4 = (pair(n + f"cols{i}", [P, KD, TOK], st) for i in range(4))
            s2 = turned
            probs = Ring([Buf(sb(n + f"probs{i}", [P, CTXP], F32, st)[:, :]) for i in range(2)])
            pt = Ring([pair(n + f"probs_t{i}", [P, TOK], st) for i in range(3)])
            pt_tail = pair(n + "probs_t_tail", [P, P], st)
            mixed = Ring([Buf(sb(n + f"mixed{i}", [P, D], F32, st)[:, :]) for i in range(2)])
            work = Buf(sb(n + "work", [P, KD, TOK], F32, st)[:, :, :])
            pc = Buf(sb(n + "pc", [P, TT, TOK], F32, st)[:, :, :]) if two_way else None
            xs_ = [Buf(sb(n + f"x{i}", [P, TT, D], F32, st)[:, :, :]) for i in range(2 if two_way else 3)]
            key_pull = pair(n + "key_pull", [P, KD], st)
            offset = Buf(sb(n + "offset", [P, KD], F32, st)[:, :])
            bias_dot = sb(n + "bias_dot", [1, 1], F32, st)
            rrow = work.ap[0:1, 0, :]
            rcol = Buf(sb(n + "rcol", [P, TT], F32, st)[:, :])
            NS = 4
            cells = [[Buf(sb(n + f"cell{i}_{j}", [P, 2], F32, st)[:, :]) for j in range(NS)] for i in range(4)]
            top, nbias, sums, rinv = (Ring(c) for c in cells)
            everything = [xl, s0, s1, s3, s4, *xs_, work, rcol, *probs.bufs, *pt.bufs, pt_tail, *mixed.bufs]
            everything += [b for c in cells for b in c] + ([pc] if two_way else [y])
            for b in everything:
                b.free = list(start)
            s2.free = [*s2.free, *start]

            bank = [Buf(ps[:, i, :]) for i in range(8)]
            for b in bank:
                b.free = list(start)
            banks = Ring(bank[4:7])
            mix_bank = bank[7]
            score_banks = bank[:4]

            def wt(i, k, a=0, n=P):
                o = (i * KD + k) * D + a
                return weights.hi[:, o:o + n], weights.lo[:, o:o + n]

            def start_loads(number):
                for _ in range(number):
                    if to_load:
                        to_load.pop(0)()()

            def load_sel(b, which):
                s4.ready = [bring(t["ctx_picked"][b, which], KD * TOK, s4.hi, s4.lo, s4.free)]

            def project(w, src, dst, bias, ready=None):
                made = []
                for m in range(KD):
                    bk = banks.take()

                    def mms(e, m=m, bk=bk):
                        for k in range(KD):
                            mm = three(e, bk.ap, wt(w, k, m * P), (src.hi[:, k, :], src.lo[:, k, :]), k == 0, k == KD - 1)
                        return mm
                    p = pe.do(mms, [*w_ready[w // 2], *src.ready, *bk.free])
                    bk.free = [split(bk.ap, dst.hi[:, m, :], dst.lo[:, m, :], [p, *dst.free], bias and bias(m))]
                    made += bk.free
                src.free = [p]
                dst.ready, dst.free = made, []
                return p

            def fold_keys():
                mb, vb, cb = (banks.take() for _ in range(3))

                def mms(e):
                    for m in range(KD):
                        for k in range(KD):
                            three(e, mb.ap[:, m * D:(m + 1) * D], wt(WQ, k, m * P), wt(WK, k, 0, D),
                                  m == 0 and k == 0, k == KD - 1)
                    for i, (b_, w) in enumerate(((names[0], WK), (names[1], WQ))):
                        for k in range(KD):
                            three(e, vb.ap[0:1, i * D:(i + 1) * D], pcol(b_, k, 1), wt(w, k, 0, D),
                                  i == 0 and k == 0, k == KD - 1)
                    for k in range(KD):
                        mm = e.matmul(cb.ap[0:1, 0:1], col(names[0], k), col(names[1], k), start=k == 0, stop=k == KD - 1,
                                      skip_group_check=True)
                    return mm
                p = pe.do(mms, [*w_ready[0], *small_p.ready, *mb.free, *vb.free, *cb.free])
                o = WQ * KD * D
                made = split(mb.ap, weights.hi[:, o:o + KD * D], weights.lo[:, o:o + KD * D], [p])
                a = act.do(lambda e: e.activation(rrow, vb.ap[0:1, :], ACT.Copy), [p, *work.free])
                c = act.do(lambda e: e.activation(bias_dot[:, :], cb.ap[0:1, 0:1], ACT.Copy), [p, *start])
                mb.free, vb.free, cb.free = [made], [a], [c]
                tb = banks.take()

                def turn(e):
                    for i in range(2 * KD):
                        mm = e.transpose(tb.ap[:, i:i + 1], rrow[:, i * P:(i + 1) * P], ident[0:1, 0:1])
                    return mm
                p = pe.do(turn, [a, *tb.free])
                work.free = [p]
                v = dve.do(lambda e: e.tensor_copy(offset.ap, tb.ap[:, 0:KD]), [p, *start])
                v = dve.do(lambda e: e.tensor_copy(key_pull.hi, tb.ap[:, KD:2 * KD]), [p, *start])
                v = dve.do(lambda e: e.tensor_tensor(key_pull.lo, tb.ap[:, KD:2 * KD], f32(key_pull.hi), ALU.subtract), [v])
                tb.free = [v]
                w_ready[0] = [made, c, v]

            def query_bias(x):
                bk = banks.take()

                def mms(e):
                    for k in range(KD):
                        mm = three(e, bk.ap[0:1, :], (key_pull.hi[:, k:k + 1], key_pull.lo[:, k:k + 1]),
                                   (x.hi[:, k, :], x.lo[:, k, :]), k == 0, k == KD - 1)
                    return mm
                p = pe.do(mms, [*w_ready[0], *x.ready, *bk.free])
                x.free = [p]
                a = act.do(lambda e: e.activation(rrow, bk.ap[0:1, :], ACT.Identity, bias=bias_dot[:, :]), [p, *work.free])
                bk.free = [a]

                def rest():
                    bk2 = banks.take()

                    def turn(e):
                        for i in range(TT):
                            mm = e.transpose(bk2.ap[:, i:i + 1], rrow[:, i * P:(i + 1) * P], ident[0:1, 0:1])
                        return mm
                    p2 = pe.do(turn, [a, *bk2.free])
                    work.free = [p2]
                    v = dve.do(lambda e: e.tensor_copy(rcol.ap, bk2.ap[:, 0:TT]), [p2, *rcol.free])
                    bk2.free = [v]
                    rcol.ready, rcol.free = [v], []
                return rest

            class Tile:
                pass

            def scores(i, g):
                o = Tile()
                for c in range(CHUNKS):
                    def mms(e, c=c):
                        for k in range(KD):
                            mm = three(e, ps[:, c, 0:CW], (g.hi[:, k, i * P:(i + 1) * P], g.lo[:, k, i * P:(i + 1) * P]),
                                       (ctx_c.hi[:, k, c * CW:(c + 1) * CW], ctx_c.lo[:, k, c * CW:(c + 1) * CW]),
                                       k == 0, k == KD - 1)
                        return mm
                    p = pe.do(mms, [*g.ready, *ctx_c.ready, *score_banks[c].free])
                mx, nb, sm, ri = top.take(), nbias.take(), sums.take(), rinv.take()
                o.p, o.rinv = probs.take(), ri
                v = dve.do(lambda e: e.tensor_reduce(mx.ap[:, 0:1], ps[:, 0:CHUNKS, 0:CW], AX.XY, ALU.max), [p, *mx.free])
                r = rcol.ap[:, i:i + 1]
                v2 = dve.do(lambda e: e.tensor_tensor(mx.ap[:, 1:2], mx.ap[:, 0:1], r, ALU.add), [v, *rcol.ready])
                v3 = dve.do(lambda e: e.tensor_scalar(nb.ap[:, 0:1], r, mx.ap[:, 1:2], SCALE, ALU.subtract, ALU.mult),
                            [v2, *nb.free])
                rcol.free = [v3]
                o.peak, o.softmax = v, (i, mx, nb, sm, v3)
                o.scored = p
                return o

            def softmax(o):
                i, mx, nb, sm, v3 = o.softmax
                full = (CHUNKS - 1) * CW
                a1 = act.do(lambda e: e.activation(o.p.ap[:, 0:full].rearrange("p (c w) -> p c w", w=CW),
                                                   ps[:, 0:CHUNKS - 1, 0:CW], ACT.Exp, bias=nb.ap[:, 0:1], scale=SCALE,
                                                   accum_out=sm.ap[:, 0:1]), [v3, *o.p.free, *sm.free])
                a2 = act.do(lambda e: e.activation(o.p.ap[:, full:CTX], ps[:, CHUNKS - 1, 0:CLAST], ACT.Exp,
                                                   bias=nb.ap[:, 0:1], scale=SCALE, accum_out=sm.ap[:, 1:2]), [v3])
                mx.free, nb.free, sm.ready = [v3], [a2], [a2]
                o.sums = sm
                for bk in score_banks:
                    bk.free = [o.peak, a2]
                o.p.ready = [a1, a2]

            groups = [list(range(a, min(a + TT, CT))) for a in range(0, CT, TT)]

            def turn_probs(o):
                o.turned = []
                for kts in [groups[-1], *groups[:-1]]:
                    tail = kts[-1] == CT - 1
                    bk, dst, w = (score_banks[-1], pt_tail, CREM) if tail else (banks.take(), pt.take(), P)

                    def mms(e, kts=kts, bk=bk, w=w):
                        for j, kt in enumerate(kts):
                            mm = e.transpose(bk.ap[0:w, j * P:(j + 1) * P], o.p.ap[:, kt * P:kt * P + w], ident)
                        return mm
                    p = pe.do(mms, [*o.p.ready, *bk.free])
                    c = len(kts) * P
                    s = split(bk.ap[0:w, 0:c], dst.hi[0:w, 0:c], dst.lo[0:w, 0:c], [p, *dst.free])
                    bk.free, dst.ready, dst.free = [s], [s], []
                    o.turned.append((kts, dst, w, dst.ready))
                o.turned.append(o.turned.pop(0))
                o.p.free = [p]

            def mix(o):
                for kts, dst, w, ready in o.turned:
                    def mms(e, kts=kts, dst=dst, w=w):
                        for j, kt in enumerate(kts):
                            c = slice(j * P, (j + 1) * P)
                            mm = three(e, mix_bank.ap[:, 0:D], (dst.hi[0:w, c], dst.lo[0:w, c]),
                                       (ctx_r.hi[0:w, kt, :], ctx_r.lo[0:w, kt, :]), kt == 0, kt == CT - 1)
                        return mm
                    p = pe.do(mms, [*ready, *ctx_r.ready, *mix_bank.free])
                    dst.free = [p]
                sm, ri = o.sums, o.rinv
                v = dve.do(lambda e: e.tensor_tensor(ri.ap[:, 1:2], sm.ap[:, 0:1], sm.ap[:, 1:2], ALU.add), [*sm.ready, *ri.free])
                ri.ready = [dve.do(lambda e: e.reciprocal(ri.ap[:, 0:1], ri.ap[:, 1:2]), [v])]
                sm.free = [v]
                o.mixed = mixed.take()
                a = act.do(lambda e: e.activation(o.mixed.ap, mix_bank.ap[:, 0:D], ACT.Copy, scale=o.rinv.ap[:, 0:1]),
                           [p, *o.rinv.ready, *o.mixed.free])
                mix_bank.free = [a]
                o.rinv.free = [a]
                o.mixed.ready = [a]
                o.multiplied = p

            def turn_mixed(i, o, dst):
                bk = banks.take()

                def mms(e):
                    for k in range(KD):
                        mm = e.transpose(bk.ap[:, k * P:(k + 1) * P], o.mixed.ap[:, k * P:(k + 1) * P], ident)
                    return mm
                p = pe.do(mms, [*o.mixed.ready, *bk.free])
                c = slice(i * P, (i + 1) * P)
                s = split(bk.ap[:, 0:KD * P].rearrange("p (k q) -> p k q", k=KD), dst.hi[:, :, c], dst.lo[:, :, c],
                          [p, *(dst.free if i == 0 else [])])
                bk.free, o.mixed.free = [s], [p]
                dst.ready = [s]

            def attend(g, dst, fill, then):
                tiles = []
                for i in range(TT + 2):
                    if 1 <= i <= TT:
                        turn_probs(tiles[i - 1])
                    if i < TT:
                        tiles.append(scores(i, g))
                        ctx_c.free = g.free = [tiles[i].scored]
                    if i >= 2:
                        turn_mixed(i - 2, tiles[i - 2], dst)
                    if i < TT:
                        softmax(tiles[i])
                    fill(i)
                    if 1 <= i <= TT:
                        mix(tiles[i - 1])
                        ctx_r.free = [tiles[i - 1].multiplied]
                    then(i)
                dst.free = []

            def load_x(b):
                xb = xs_[b % len(xs_)]
                src = x_d[b * TOK:(b + 1) * TOK, :].rearrange("(t p) d -> p t d", p=P)
                xb.ready, xb.free = [loads.do(xb.ap, src, s_x[b % len(xs_)], [*xb.free, *x_there])], []
                return xb

            if two_way:
                WQ, WK, WV, WQS, WKC, WVC, WG = range(7)
                names = ("bq_c", "bk_s", "bv_s")
            else:
                WQ, WK, WV, WO = range(4)
                names = ("bq1", "bk1", "bv1")
            xls = [xl, xl] if two_way else [xl, s3]
            gs = [s1, s1] if two_way else [s1, s4]

            def project_queries(b):
                project(WQ, xls[b % 2], gs[b % 2], lambda m: offset.ap[:, m:m + 1])

            fills, thens = ([[] for _ in range(SLOTS)] for _ in range(2))
            xb = load_x(0)
            to_load = []
            norm_measure(norm_in, xb, xb.ready)
            if two_way:
                ops.load_weights(0, act, dve)
                to_load = ops.context(0, act, dve)
            norm_apply(norm_in, xb)
            start_loads(1)
            fold_keys()
            norm_turn(xl, banks)
            project_queries(0)
            start_loads(2)
            query_bias(xl)()
            if two_way:
                start_loads(1)
                ops.load_weights(WKC // 2, act, dve)
                fills[0] += [lambda: start_loads(2), lambda: start_loads(CTX_R - 2), later_loads]
                fills[1] += [lambda: ops.load_weights(WV // 2)]
                fills[2] += [lambda: ops.load_weights(WG // 2)]

            x_next = None
            for b in range(BATCH):
                more = b + 1 < BATCH
                def back_keys():
                    project(WKC, xl, s3, lambda m: col("bk_c", m))

                def back_values():
                    made = []
                    for h in range(2):
                        bk = banks.take()

                        def mms(e, h=h, bk=bk):
                            for j in range(2):
                                c = slice((2 * h + j) * P, (2 * h + j + 1) * P)
                                for k in range(KD):
                                    mm = three(e, bk.ap[:, j * D:(j + 1) * D], (xl.hi[:, k, c], xl.lo[:, k, c]),
                                               wt(WVC, k, 0, D), k == 0 and j == 0, k == KD - 1)
                            return mm
                        p = pe.do(mms, [*w_ready[WVC // 2], *xl.ready, *bk.free])
                        bk.free = [split(bk.ap, s0.hi[:, h, :], s0.lo[:, h, :], [p, *s0.free])]
                        made += bk.free
                    s0.ready, s0.free, xl.free = made, [], [p]

                def back_queries():
                    project(WQS, s4, s1, lambda m: col("bq_s", m))

                if two_way:
                    if b == 0:
                        fills[0][1:1] = [back_keys, back_values]
                    else:
                        apply, turn, find = pieces[0]
                        fills[0] = [apply, back_keys, turn, back_values, find, *fills[0]]
                    fills[2].insert(0, lambda b=b: load_sel(b, 0))
                    fills[TT + 1] += [back_queries, lambda b=b: load_sel(b, 1)]
                if more:
                    def next_x(b=b):
                        nonlocal x_next
                        x_next = load_x(b + 1)
                    fills[TT - 1 if two_way else 0].append(next_x)
                    fills[TT].append(lambda: norm_measure(norm_in, x_next, x_next.ready))
                    if two_way:
                        fills[TT + 1].append(lambda: norm_apply(norm_in, x_next))
                    if not two_way:
                        to_load += ops.context(b + 1)
                        fills[TT] += [lambda: norm_apply(norm_in, x_next), lambda: start_loads(1)]
                        thens[TT] += [lambda b=b: norm_turn(xls[(b + 1) % 2], banks)]
                        fills[TT + 1] += [lambda b=b: project_queries(b + 1), lambda: start_loads(2)]
                attend(gs[b % 2], s2, lambda i: [piece() for piece in fills[i]], lambda i: [piece() for piece in thens[i]])
                fills, thens = ([[] for _ in range(SLOTS)] for _ in range(2))
                if more and two_way:
                    to_load += ops.context(b + 1)
                if two_way:
                    for which in range(2):
                        if which:
                            back_queries()
                            start_loads(1)
                            if more:
                                norm_turn(xl, banks)
                        back = []

                        def finish(i, which=which):
                            sm, ri, pr, a = back[i]
                            v = dve.do(lambda e: e.reciprocal(ri.ap[:, 1:2], sm.ap[:, 0:1]), [a, *ri.free])
                            sm.free = [v]
                            w, dst = col("mixing", which * TT + i), pc.ap[:, i, :]
                            v = dve.do(lambda e: e.tensor_tensor(ri.ap[:, 0:1], ri.ap[:, 1:2], w, ALU.mult), [v])
                            if which == 0:
                                v = dve.do(lambda e: e.tensor_scalar(dst, dst, ri.ap[:, 0:1], None, ALU.mult), [v])
                            else:
                                v = dve.do(lambda e: e.scalar_tensor_tensor(dst, pr.ap[:, 0:TOK], ri.ap[:, 0:1], dst,
                                                                            ALU.mult, ALU.add), [v, *pc.ready])
                                pr.free = [v]
                            ri.free = [v]
                            if i % 2:
                                start_loads(1)
                            return v

                        for i in range(TT):
                            bk = score_banks[i]

                            def mms(e, i=i, bk=bk):
                                c = slice(i * P, (i + 1) * P)
                                for k in range(KD):
                                    mm = three(e, bk.ap, (s1.hi[:, k, c], s1.lo[:, k, c]),
                                               (s3.hi[:, k, :], s3.lo[:, k, :]), k == 0, k == KD - 1)
                                return mm
                            p = pe.do(mms, [*s1.ready, *s3.ready, *bk.free])
                            mx, nb, sm, ri = top.take(), nbias.take(), sums.take(), rinv.take()
                            pr = probs.take() if which else None
                            dst = pr.ap[:, 0:TOK] if which else pc.ap[:, i, :]
                            v = dve.do(lambda e, bk=bk, mx=mx: e.tensor_reduce(mx.ap[:, 0:1], bk.ap, AX.X, ALU.max),
                                       [p, *mx.free])
                            v = dve.do(lambda e, nb=nb, mx=mx: e.tensor_scalar(nb.ap[:, 0:1], mx.ap[:, 0:1], -SCALE, None,
                                                                               ALU.mult), [v, *nb.free])
                            a = act.do(lambda e, bk=bk, nb=nb, sm=sm, dst=dst: e.activation(
                                dst, bk.ap, ACT.Exp, bias=nb.ap[:, 0:1], scale=SCALE, accum_out=sm.ap[:, 0:1]),
                                [v, *(pr.free if which else pc.free), *sm.free])
                            mx.free, nb.free, bk.free = [v], [a], [a]
                            back.append((sm, ri, pr, a))
                            if i:
                                v = finish(i - 1)
                        v = finish(TT - 1)
                        pc.ready = [v]
                        s1.free = [p]
                    s3.free = [p]
                    pc.ready = [v]
                    project(WV, s2, s1, lambda m: col(names[2], m))
                    acc = score_banks[0:KD]
                    turned_pc = []

                    def turn_pc(j):
                        bk, dst = banks.take(), pt.take()

                        def mms(e):
                            for i in range(TT):
                                mm = e.transpose(bk.ap[:, i * P:(i + 1) * P], pc.ap[:, i, j * P:(j + 1) * P], ident)
                            return mm
                        p = pe.do(mms, [*pc.ready, *bk.free])
                        s = split(bk.ap, dst.hi, dst.lo, [p, *dst.free])
                        bk.free, dst.ready = [s], [s]
                        turned_pc.append((dst, p))

                    turn_pc(0)
                    turn_pc(1)
                    for j in range(TT):
                        dst = turned_pc[j][0]

                        def mms(e, j=j, dst=dst):
                            for m in range(KD):
                                o = (j % 2) * D + m * P
                                mm = three(e, acc[m].ap, (s0.hi[:, j // 2, o:o + P], s0.lo[:, j // 2, o:o + P]),
                                           (dst.hi, dst.lo), j == 0, j == TT - 1)
                            return mm
                        p = pe.do(mms, [*dst.ready, *s0.ready, *[z for q in acc for z in q.free]])
                        dst.free = [p]
                        if j + 2 < TT:
                            turn_pc(j + 2)
                            start_loads(1)
                    pc.free = [turned_pc[-1][1]]
                    s0.free = [p]
                    made = []
                    for m in range(KD):
                        acc[m].free = [split(acc[m].ap, s3.hi[:, m, :], s3.lo[:, m, :], [p, *s3.free], col("bv_c", m))]
                        made += acc[m].free
                    s3.ready, s3.free = made, []
                    diff, part = pc.ap[:, 0:KD, :], pc.ap[:, KD:2 * KD, :]
                    pr = probs.take()
                    base = pr.ap[:, 0:KD * TOK].rearrange("p (k t) -> p k t", k=KD)
                    t_base = pool.do(lambda e, base=base: e.tensor_tensor(base, f32(s3.hi), f32(s3.lo), ALU.add), [*s3.ready, *pr.free])
                    g_ = dve.do(lambda e: e.tensor_tensor(diff, f32(s1.hi), f32(s3.hi), ALU.subtract),
                                 [*s1.ready, *s3.ready, *pc.free])
                    v = dve.do(lambda e: e.tensor_tensor(part, f32(s1.lo), f32(s3.lo), ALU.subtract),
                               [*s1.ready, *s3.ready, *pc.free])
                    t_diff = dve.do(lambda e: e.tensor_tensor(diff, diff, part, ALU.add), [v, g_])
                    made = []
                    gate_banks = [banks.take() for _ in range(KD)]
                    for src, f0 in ((s1, 0), (s3, KD)):
                        for m in range(KD):
                            bk = gate_banks[m]

                            def mms(e, m=m, bk=bk, src=src, f0=f0):
                                for k in range(KD):
                                    o = (WG * KD + f0 + k) * D + m * P
                                    mm = three(e, bk.ap, (weights.hi[:, o:o + P], weights.lo[:, o:o + P]),
                                               (src.hi[:, k, :], src.lo[:, k, :]), f0 + k == 0, f0 + k == 2 * KD - 1)
                                return mm
                            p = pe.do(mms, [*w_ready[WG // 2], *src.ready, *(bk.free if f0 == 0 else [])])
                            if f0:
                                a = act.do(lambda e, m=m, bk=bk: e.activation(work.ap[:, m, :], bk.ap, ACT.Tanh,
                                                                              bias=half_bg[:, m:m + 1], scale=0.5),
                                           [p, *work.free, t_bg])
                                bk.free = [a]
                                made.append(a)
                    t_gate = p
                    v = dve.do(lambda e: e.scalar_tensor_tensor(diff, work.ap, 1.0, diff, ALU.add, ALU.mult),
                               [*made, t_diff])
                    v = dve.do(lambda e, base=base: e.scalar_tensor_tensor(work.ap, diff, 0.5, base, ALU.mult, ALU.add), [v, t_base])
                    pr.free = [v]
                    pc.free = [v]
                    s1.free = [t_gate, t_diff]
                    s3.free = [t_gate, v]
                    work.ready = [v]
                    start_loads(1)
                    if more:
                        project_queries(b + 1)
                    for h in range(2):
                        bk = banks.take()

                        def turn(e, h=h, bk=bk):
                            for j in range(2):
                                c = slice((2 * h + j) * P, (2 * h + j + 1) * P)
                                for k in range(KD):
                                    o = j * D + k * P
                                    mm = e.transpose(bk.ap[:, o:o + P], work.ap[:, k, c], ident)
                            return mm
                        p = pe.do(turn, [*work.ready, *bk.free])
                        xs = xb.ap[:, 2 * h:2 * h + 2, :].rearrange("p t d -> p (t d)")
                        v = dve.do(lambda e, bk=bk, xs=xs: e.scalar_tensor_tensor(xs, bk.ap, gate_col, xs, ALU.mult, ALU.add),
                                   [p, t_tanh, *xb.ready])
                        bk.free = [v]
                    xb.ready = [v]
                    work.free = [p]
                    if more:
                        query_bias(xl)()
                else:
                    if more:
                        bias_row = query_bias(xls[(b + 1) % 2])
                    if b:
                        for piece in last_put:
                            piece()
                    if more:
                        start_loads(1)
                        bias_row()
                    xl_b = xls[b % 2]
                    start_loads(1)
                    made = []
                    for m in range(KD):
                        bk = banks.take()

                        def mms(e, m=m, bk=bk):
                            for k in range(KD):
                                mm = three(e, bk.ap, wt(WV, k, m * P), (s2.hi[:, k, :], s2.lo[:, k, :]), k == 0, k == KD - 1)
                            return mm
                        p = pe.do(mms, [*w_ready[WV // 2], *s2.ready, *bk.free])
                        v = dve.do(lambda e, m=m, bk=bk, xl_b=xl_b: e.scalar_tensor_tensor(
                            work.ap[:, m, :], bk.ap, col(names[2], m), f32(xl_b.hi)[:, m, :], ALU.add, ALU.add),
                            [p, *work.free])
                        bk.free = [v]
                        v = dve.do(lambda e, m=m, xl_b=xl_b: e.tensor_tensor(work.ap[:, m, :], work.ap[:, m, :],
                                                                             f32(xl_b.lo)[:, m, :], ALU.add), [v])
                        made.append(split(work.ap[:, m, :], y.hi[:, m, :], y.lo[:, m, :], [v, *y.free]))
                    s2.free = [p]
                    xl_b.free = [*xl_b.free, v]
                    work.free = made
                    y.ready, y.free = made, []
                    start_loads(1)

                    def output(xb=xb):
                        for h in range(2):
                            bk = banks.take()

                            def mms(e, h=h, bk=bk):
                                for j in range(2):
                                    c = slice((2 * h + j) * P, (2 * h + j + 1) * P)
                                    for k in range(KD):
                                        mm = three(e, bk.ap[:, j * D:(j + 1) * D], (y.hi[:, k, c], y.lo[:, k, c]),
                                                   wt(WO, k, 0, D), k == 0 and j == 0, k == KD - 1)
                                return mm
                            p = pe.do(mms, [*w_ready[WO // 2], *y.ready, *bk.free])
                            xs = xb.ap[:, 2 * h:2 * h + 2, :].rearrange("p t d -> p (t d)")
                            v = dve.do(lambda e, bk=bk, xs=xs: e.scalar_tensor_tensor(xs, bk.ap, gate_col, xs, ALU.mult,
                                                                                      ALU.add), [p, t_tanh, *xb.ready])
                            bk.free = [v]
                            for j in range(2):
                                v = dve.do(lambda e, q=2 * h + j: e.tensor_tensor(xb.ap[:, q, :], xb.ap[:, q, :], col("bo"),
                                                                                  ALU.add), [v, t_bo])
                        xb.ready = [v]
                        y.free = [p]
                pieces = route(layer, b, xb, banks)
                if two_way:
                    norm_measure(norm_out, xb, xb.ready)
                    pieces[0] = [lambda xb=xb: norm_apply(norm_out, xb), *pieces[0]]
                else:
                    pieces.insert(0, [output, lambda xb=xb: norm_measure(norm_out, xb, xb.ready)])
                    pieces[1].insert(0, lambda xb=xb: norm_apply(norm_out, xb))
                if more:
                    fills[0].append(lambda: start_loads(2))
                    if two_way:
                        for i in range(1, SLOTS):
                            fills[i] += pieces[i]
                    else:
                        fills[0] += pieces[0]
                        (apply, turn, find), choose, (weigh, turn_w), put_first, put_second, put_rest = pieces[1:]
                        fills[1] += [apply]
                        thens[1] += [turn, find]
                        fills[2] += choose
                        fills[3] += [weigh]
                        thens[3] += [turn_w]
                        fills[4] += put_first
                        last_put = put_second + put_rest
                    xb = x_next
            pieces = [piece for group in pieces for piece in group]
            if not two_way:
                pieces.pop(0)()
                pieces.pop(0)()
            core_done = barrier()
            st.close()
            ops.stack.close()
            return core_done, pieces, bank, banks

        routed = []

        def route(layer, b, xb, banks):
            s = {}
            tiles = range(b * TT, (b + 1) * TT)
            ch = chosen[:, b * TT:(b + 1) * TT, :]

            def turn_tokens():
                norm_turn(turned, banks)

            def find_logits():
                bk = banks.take()

                def mms(e):
                    for k in range(KD):
                        mm = three(e, bk.ap[0:E, :], pcol(f"router{layer}", k * E, E),
                                   (turned.hi[:, k, :], turned.lo[:, k, :]), k == 0, k == KD - 1)
                    return mm
                p = pe.do(mms, [*small_p.ready, *turned.ready, *bk.free])
                turned.free = [p]
                s["logits"] = act.do(lambda e: e.activation(logits_row, bk.ap[0:E, :], ACT.Copy), [p, *routed])
                bk.free = [s["logits"]]

            def choose():
                bk = banks.take()

                def turn(e):
                    for i in range(TT):
                        mm = e.transpose(bk.ap[:, i * E:(i + 1) * E], logits_row[:, i * P:(i + 1) * P], ident[0:E, 0:E])
                    return mm
                p = pe.do(turn, [s["logits"], *bk.free])
                lg = bk.ap[:, 0:TT * E].rearrange("p (t e) -> p t e", e=E)
                if layer == 0:
                    v = dve.do(lambda e: e.tensor_copy(logits[:, :, :], lg), [p, *routed])
                else:
                    gb = col("gate_b").unsqueeze(1).to_broadcast([P, TT, E])
                    v = dve.do(lambda e: e.tensor_tensor(logits[:, :, :], lg, gb, ALU.add), [p, *routed])
                bk.free = [v]
                other = logits[:, :, :].unsqueeze(2).to_broadcast([P, TT, E, E])
                own = logits[:, :, :].unsqueeze(3).to_broadcast([P, TT, E, E])
                low = col("lower").rearrange("p (a b) -> p a b", a=E).unsqueeze(1).to_broadcast([P, TT, E, E])
                v0 = dve.do(lambda e: e.tensor_reduce(peak[:, :], logits[:, :, :], AX.X, ALU.max), [v])
                v1 = dve.do(lambda e: e.tensor_tensor(above, other, own, ALU.is_gt), [v])
                v2 = dve.do(lambda e: e.tensor_tensor(same, other, own, ALU.is_equal), [v])
                v3 = dve.do(lambda e: e.tensor_tensor(logits[:, :, :], logits[:, :, :],
                                                      peak[:, :].unsqueeze(2).to_broadcast([P, TT, E]), ALU.subtract),
                            [v0, v1, v2])
                s["exp"] = act.do(lambda e: e.activation(logits[:, :, :], logits[:, :, :], ACT.Exp), [v3])
                v = dve.do(lambda e: e.tensor_tensor(same, same, low, ALU.mult), [v2])
                v = dve.do(lambda e: e.tensor_tensor(above, above, same, ALU.add), [v1, v])
                v = dve.do(lambda e: e.tensor_reduce(rank[:, :, :], above, AX.X, ALU.add), [v])
                s["chosen"] = v = dve.do(lambda e: e.tensor_scalar(ch, rank[:, :, :], float(TOP[layer]), None, ALU.is_lt), [v])
                if b == 0:
                    v = dve.do(lambda e: e.memset(earlier[:, 0, :], 0.0), [v])
                for i in tiles:
                    v = dve.do(lambda e, i=i: e.tensor_tensor(earlier[:, i + 1, :], earlier[:, i, :], chosen[:, i, :],
                                                              ALU.add), [v])
                s["earlier"] = v

            def weigh():
                gate_col = tanh_g[:, 2 + layer:3 + layer]
                weights = xn.ap[:, :, D:ROW]
                v = dve.do(lambda e: e.tensor_tensor(logits[:, :, :], logits[:, :, :], ch, ALU.mult), [s["chosen"], s["exp"]])
                v = dve.do(lambda e: e.tensor_reduce(total[:, :], logits[:, :, :], AX.X, ALU.add), [v])
                v = dve.do(lambda e: e.reciprocal(total[:, :], total[:, :]), [v])
                s["weights"] = dve.do(lambda e: e.scalar_tensor_tensor(
                    weights, logits[:, :, :], gate_col, total[:, :].unsqueeze(2).to_broadcast([P, TT, E]),
                    ALU.mult, ALU.mult), [v, t_tanh, *xn.ready])
                dst = rows_d[layer][b * TOK:(b + 1) * TOK, :].rearrange("(t p) d -> p t d", p=P)
                xn.free = [*xn.free, loads.do(dst, xn.ap, s_rows[layer], [s["weights"], *xn.ready])]
                if layer == 0:
                    send_residual()
                bk = banks.take()

                def mms(e):
                    i = b * TT
                    e.matmul(bk.ap[:, 0:TT * E], before, chosen[:, i:i + TT, :].rearrange("p t e -> p (t e)"), start=True,
                             stop=False, skip_group_check=True)
                    return e.matmul(bk.ap[:, 0:TT * E], ones, earlier[:, i:i + TT, :].rearrange("p t e -> p (t e)"),
                                    start=False, stop=True, skip_group_check=True)
                p = pe.do(mms, [s["earlier"], t_half, *bk.free])
                v = dve.do(lambda e: e.scalar_tensor_tensor(place[:, :], bk.ap[:, 0:TT * E], 1.0,
                                                            ch.rearrange("p t e -> p (t e)"), ALU.add, ALU.mult), [p, *routed])
                bk.free = [v]
                v = dve.do(lambda e: e.tensor_scalar(place_i[:, :], place[:, :], -1.0, None, ALU.add), [v])
                shift = P.bit_length() - 1
                v1 = dve.do(lambda e: e.tensor_scalar(tile_i[:, :], place_i[:, :], shift, None, ALU.arith_shift_right), [v])
                v2 = dve.do(lambda e: e.tensor_scalar(part_i[:, :], place_i[:, :], P - 1, None, ALU.bitwise_and), [v])
                v1 = dve.do(lambda e: e.tensor_copy(tile_h[:, :, :].rearrange("p t e -> p (t e)"), tile_i[:, :]), [v1])
                v2 = dve.do(lambda e: e.tensor_copy(part_h[:, :, :].rearrange("p t e -> p (t e)"), part_i[:, :]), [v2])
                s["part"] = v2
                v1 = dve.do(lambda e: e.tensor_tensor(
                    tokens_at[:, :, :, :].rearrange("p t e m -> p (t e) m"), tiles_m.unsqueeze(1).to_broadcast([P, TT * E, M]),
                    tile_h[:, :, :].rearrange("p t e -> p (t e)").unsqueeze(2).to_broadcast([P, TT * E, M]),
                    ALU.is_equal), [v1, t_half, *routed])
                flat = tokens_at[:, :, :, :].rearrange("p t e m -> p t (e m)")
                s["at"] = dve.do(lambda e: e.tensor_tensor(
                    flat, flat, col("token")[:, b * TT:(b + 1) * TT].unsqueeze(2).to_broadcast([P, TT, E * M]), ALU.mult), [v1])

            def send_residual():
                dst = acc_d[layer][b * TOK:(b + 1) * TOK, :].rearrange("(t p) d -> p t d", p=P)
                xb.free = [loads.do(dst, xb.ap, s_acc[layer], xb.ready)]

            def turn_weights():
                bk = banks.take()

                def turn(e):
                    for i in range(TT):
                        mm = e.transpose(bk.ap[0:E, i * P:(i + 1) * P], xn.ap[:, i, D:ROW], ident)
                    return mm
                p = pe.do(turn, [s["weights"], *bk.free])
                xn.free.append(p)
                s["turned"] = act.do(lambda e: e.activation(logits_row, bk.ap[0:E, :], ACT.Copy), [p, *routed])
                bk.free = [s["turned"]]

            def add_biases():
                for h in range(2):
                    bk = banks.take()

                    def mms(e, h=h, bk=bk):
                        for j in range(2):
                            c = slice((2 * h + j) * P, (2 * h + j + 1) * P)
                            mm = e.matmul(bk.ap[:, j * D:(j + 1) * D], logits_row[:, c], b2[:, :],
                                          start=j == 0, stop=True, skip_group_check=True)
                        return mm
                    p = pe.do(mms, [s["turned"], t_b2, *bk.free])
                    xs = xb.ap[:, 2 * h:2 * h + 2, :].rearrange("p t d -> p (t d)")
                    v = dve.do(lambda e, bk=bk, xs=xs: e.tensor_tensor(xs, xs, bk.ap, ALU.add), [p, *xb.ready])
                    bk.free = [v]
                xb.ready = [v]
                send_residual()

            def mark(i):
                oh = onehot.take()
                oh.ready = [dve.do(lambda e: e.tensor_tensor(
                    oh.ap, places.unsqueeze(1).to_broadcast([P, E, P]),
                    part_h[:, i, :].unsqueeze(2).to_broadcast([P, E, P]), ALU.is_equal), [s["part"], *xb.ready, *oh.free])]
                s[i] = oh

            def put(i):
                oh, bk = s[i], banks.take()

                def mms(e):
                    for x_ in range(E):
                        mm = e.matmul(bk.ap[:, x_ * M:(x_ + 1) * M], oh.ap[:, x_, :], tokens_at[:, i, x_, :],
                                      start=x_ == 0, stop=x_ == E - 1, skip_group_check=True)
                    return mm
                p = pe.do(mms, [s["at"], *oh.ready, *bk.free])
                before_ = [s["listed"]] if "listed" in s else routed
                if b == 0 and i == 0:
                    v = dve.do(lambda e: e.tensor_copy(lists[:, :], bk.ap[:, 0:E * M]), [p, *before_])
                else:
                    v = dve.do(lambda e: e.tensor_tensor(lists[:, :], lists[:, :], bk.ap[:, 0:E * M], ALU.add),
                               [p, *before_])
                oh.free, bk.free, s["listed"] = [p], [v], v
                if i == TT - 1:
                    routed[:] = [v, p]

            def weigh_and_place():
                weigh()
                mark(0)

            def put_first():
                if layer == 1:
                    add_biases()
                put(0)
                mark(1)

            def put_second():
                put(1)
                mark(2)
                mark(3)

            def put_rest():
                put(2)
                put(3)

            assert TT == 4
            weighing = [weigh_and_place] if layer == 0 else [weigh_and_place, turn_weights]
            return [[turn_tokens, find_logits], [choose], weighing, [put_first], [put_second], [put_rest]]

        def finish_lists(banks):
            bk = banks.take()
            p = pe.do(lambda e: e.matmul(bk.ap[:, 0:E], ones, earlier[:, NT, :], start=True, stop=True,
                                         skip_group_check=True), [*routed, *bk.free])
            c = dve.do(lambda e: e.tensor_copy(counts_i[:, :], bk.ap[0:1, 0:E]), [p, *routed])
            bk.free = [c]
            spare = col("spare").unsqueeze(1).to_broadcast([P, E * NB, BT])
            ls = lists[:, :].rearrange("p (a t) -> p a t", t=BT)
            t_ = place3.rearrange("p (a t) -> p a t", t=BT)
            v = dve.do(lambda e: e.scalar_tensor_tensor(t_, ls, 0.0, spare, ALU.is_equal, ALU.mult), [*routed])
            v = dve.do(lambda e: e.scalar_tensor_tensor(list_i[:, :], lists[:, :], -1.0, place3, ALU.add, ALU.add), [v])
            return [v], [c]

        def experts(layer, start, pieces, bank, banks, prefetch):
            st = ExitStack()
            n = f"m{layer}_"
            gelu = (ACT.Gelu_apprx_tanh, ACT.Gelu)[layer]
            up_d, down_d = t[f"up{layer}"], t[f"down{layer}"]
            ups = [pair(n + f"up{i}", [P, KD, H], st) for i in range(2)]
            downs = [pair(n + f"down{i}", [P, HT, D], st) for i in range(2)]
            firsts, others = ([Buf(sb(n + f"{w}{i}", [P, BT, ROW], F32, st)[:, :, :]) for i in range(2)]
                              for w in ("first_block", "other_block"))
            for i in range(2):
                firsts[i].sem, others[i].sem = sem(n + f"first_in{i}"), sem(n + f"other_in{i}")
                firsts[i].count = 0
            xt = pair(n + "xt", [P, KD, BLOCK], st)
            act_out = Ring([Buf(sb(n + f"act_out{i}", [P, BLOCK], F32, st)[:, :]) for i in range(3)])
            hidden = [pair(n + f"hidden{f}", [P, BLOCK], st) for f in range(HT)]
            y = Buf(sb(n + "y", [P, BT, D], F32, st)[:, :, :])
            w_now, w_prev = (Buf(sb(n + f"w{i}", [P, BT], F32, st)[:, :]) for i in range(2))
            i_now, i_prev, i_out = (Buf(sb(n + f"i{i}", [P, BT], I32, st)[:, :]) for i in range(3))
            more_slots = [Buf(sb(n + f"stage{i}", [P, STAGE], F32, st)[:, :]) for i in range(1 if prefetch else 3)]
            for i, b in enumerate(more_slots):
                b.sem = sem(n + f"stage{i}_in")

            def free_memory(*bufs):
                for b in bufs:
                    b.free = list(start)

            free_memory(*ups, *downs)
            def fetch_expert(e_, piece):
                h = HT // 2
                if piece < KD:
                    return fetch(up_d[e_].rearrange("(k p) f -> p k f", p=P)[:, piece, :], H)
                a = (piece - KD) * h
                return fetch(down_d[e_].rearrange("(f p) d -> p f d", p=P)[:, a:a + h, :], h * D)

            def convert_expert(e_, piece, fetched, first=dve, second=pool):
                u, d, h = ups[e_ % 2], downs[e_ % 2], HT // 2
                if piece < KD:
                    u.ready = [convert(fetched, u.hi[:, piece, :], u.lo[:, piece, :], u.free, first, pool)]
                else:
                    a = (piece - KD) * h
                    d.ready = [convert(fetched, d.hi[:, a:a + h, :], d.lo[:, a:a + h, :], d.free, first, second)]

            quarters = [fetch_expert(0, piece) for piece in range(NSTAGE)]
            for piece in range(4):
                convert_expert(0, piece, quarters[piece], act, pool)
                if len(quarters) < 4:
                    quarters.append(fetch_expert(0, len(quarters)))
                pieces.pop(0)()
            while pieces:
                pieces.pop(0)()
            list_ready, counts_ready = finish_lists(banks)
            s_add = sem(n + "added")
            rows_ready = (s_rows[layer], loads.total[s_rows[layer].name])
            acc_ready = (s_acc[layer], loads.total[s_acc[layer].name])
            start = [*start, *barrier(), rows_ready, acc_ready]
            own_slots, slots.bufs = slots.bufs, slots.bufs + more_slots
            free_memory(*more_slots, *firsts, *others, xt, *act_out.bufs, *hidden, y, w_now, w_prev, i_now, i_prev, i_out)
            up_banks = Ring(bank[0:5])
            x_bank, y_bank = bank[5], bank[6]
            for b in bank:
                b.free = [*b.free, *start]

            def counters(e, r):
                for key in ("adds", "others0", "others1"):
                    r[key] = e.alloc_register(n + key)
                    e.reg_mov(r[key], 0)
            pool.plain(counters)

            def others_in(i):
                def step(e):
                    e.wait_ge(others[i].sem, e.snap(pool.registers[f"others{i}"]))
                    e.wait_ge(pool.sem, before_step)
                    return e.nop()
                before_step = pool.count
                return pool.do(step)

            def gather_done(e_, j):
                g = others[j % 2] if j else firsts[e_ % 2]
                g.ready = [others_in(j % 2) if j else (g.sem, g.count)]

            def gather(e_, j):
                g = others[j % 2] if j else firsts[e_ % 2]
                rows = [list_i[:, e_ * M + j * BT + i:e_ * M + j * BT + i + 1] for i in range(BT)]

                def step(e):
                    for i in range(BT):
                        e.indirect_dma_start(out=g.ap[:, i, :], out_offset=None, in_=rows_d[layer],
                                             in_offset=bass.IndirectOffsetOnAxis(ap=rows[i], axis=0)).then_inc(g.sem, 16)
                    if j:
                        r = pool.registers[f"others{j % 2}"]
                        e.reg_add(r, r, 16 * BT)
                    e.wait_ge(pool.sem, before_step)
                    return e.nop()
                before_step = pool.count
                pool.do(step, [*list_ready, rows_ready, *g.free])
                if j == 0:
                    g.count += 16 * BT

            def add_done():
                def step(e):
                    e.wait_ge(s_add, e.snap(pool.registers["adds"]))
                    e.wait_ge(pool.sem, before_step)
                    return e.nop()
                before_step = pool.count
                return pool.do(step)

            def add():
                def step(e):
                    for i in range(BT):
                        e.indirect_dma_start(out=acc_d[layer], out_offset=bass.IndirectOffsetOnAxis(ap=i_out.ap[:, i:i + 1], axis=0),
                                             in_=y.ap[:, i, :], in_offset=None, compute_op=ALU.add).then_inc(s_add, 16)
                    e.reg_add(pool.registers["adds"], pool.registers["adds"], 16 * BT)
                    e.wait_ge(pool.sem, before_step)
                    return e.nop()
                before_step = pool.count
                pool.do(step, [acc_ready, *y.ready, *i_out.ready])

            def now_is_before():
                w_prev.ready = [dve.do(lambda e: e.tensor_copy(w_prev.ap, w_now.ap), [*w_prev.free, *w_now.ready])]
                i_prev.ready = [dve.do(lambda e: e.tensor_copy(i_prev.ap, i_now.ap), [*i_prev.free, *i_now.ready])]

            def block_in(e_, j, g):
                now_is_before()
                v = dve.do(lambda e: e.tensor_copy(w_now.ap, g.ap[:, :, D + e_]), [*w_prev.ready, *g.ready])
                w_now.ready = [v]
                o = e_ * M + j * BT
                v2 = dve.do(lambda e: e.tensor_copy(i_now.ap, list_i[:, o:o + BT]), [*i_prev.ready, *list_ready])
                i_now.ready = [v2]

                def turn(e):
                    for i in range(BT):
                        for k in range(KD):
                            c = k * BLOCK + i * P
                            mm = e.transpose(x_bank.ap[:, c:c + P], g.ap[:, i, k * P:(k + 1) * P], ident)
                    return mm
                p = pe.do(turn, [*g.ready, *x_bank.free])
                g.free = [v, p]
                src = x_bank.ap.rearrange("p (k t) -> p k t", k=KD)
                x_bank.free = [split(src, xt.hi, xt.lo, [p, *xt.free])]
                xt.ready = x_bank.free

            def up(e_, f):
                u, bk, a_, hb = ups[e_ % 2], up_banks.take(), act_out.take(), hidden[f]
                fs = slice(f * P, (f + 1) * P)
                dst = bk.ap[:, 0:BLOCK]

                def mms(e):
                    for k in range(KD):
                        mm = three(e, dst, (u.hi[:, k, fs], u.lo[:, k, fs]), (xt.hi[:, k, :], xt.lo[:, k, :]),
                                   k == 0, k == KD - 1)
                    return mm
                p = pe.do(mms, [*u.ready, *xt.ready, *bk.free])
                bias = {} if layer == 0 else {"bias": col("b1", e_ * HT + f)}
                a = act.do(lambda e: e.activation(a_.ap, dst, gelu, **bias), [p, *a_.free])
                bk.free = [a]
                a2 = act.do(lambda e: e.activation(hb.hi, a_.ap, ACT.Copy), [a, *hb.free])
                v = dve.do(lambda e: e.tensor_tensor(hb.lo, a_.ap, f32(hb.hi), ALU.subtract), [a2, *hb.free])
                a_.free, hb.ready, xt.free, u.free = [v], [v], [p], [p]

            def down(e_, f):
                d, hb = downs[e_ % 2], hidden[f]

                def mms(e):
                    for i in range(BT):
                        mm = three(e, y_bank.ap[:, i * D:(i + 1) * D], (hb.hi[:, i * P:(i + 1) * P], hb.lo[:, i * P:(i + 1) * P]),
                                   (d.hi[:, f, :], d.lo[:, f, :]), f == 0 and i == 0, f == HT - 1)
                    return mm
                p = pe.do(mms, [*d.ready, *hb.ready, *y_bank.free])
                hb.free = d.free = y_bank.ready = [p]

            def block_out():
                for i in range(BT):
                    a = act.do(lambda e, i=i: e.activation(y.ap[:, i, :], y_bank.ap[:, i * D:(i + 1) * D], ACT.Copy,
                                                           scale=w_prev.ap[:, i:i + 1]),
                               [*y_bank.ready, *w_prev.ready, *y.free])
                v = dve.do(lambda e: e.tensor_copy(i_out.ap, i_prev.ap), [*i_prev.ready, *y.free])
                y_bank.free, w_prev.free, i_prev.free, y.ready, i_out.ready = [a], [a], [v], [a], [v]

            spare = col("spare")
            for b in (i_out, i_now):
                b.ready = [dve.do(lambda e, b=b: e.tensor_scalar(b.ap, spare, -1.0, None, ALU.add), [t_small, *b.free])]
            w_now.ready = [dve.do(lambda e: e.memset(w_now.ap, 0.0), w_now.free)]
            def get_counts(e, r):
                for sem_, value in counts_ready:
                    e.wait_ge(sem_, value)
                for e_ in range(E):
                    r[e_] = e.snap(e.value_load(counts_i[0:1, e_:e_ + 1], min_val=0, max_val=BATCH * TOK))
            for q in (pe, act, dve):
                q.plain(get_counts)
            gather(0, 0)
            y.ready = [pool.do(lambda e: e.memset(y.ap, 0.0), y.free)]
            add()
            gather(0, 1)
            pool.plain(get_counts)

            fetched = []
            for e_ in range(E):
                for j in range(NB):
                    first = e_ == 0 and j == 0
                    if j:
                        for q in engines:
                            q.only_if(e_, BLOCK * j)
                    g = others[j % 2] if j else firsts[e_ % 2]
                    if j == 0:
                        gather_done(e_, 0)
                    if j + 1 < NB and not first:
                        gather(e_, j + 1)
                    if j == 0 and e_ + 1 < E:
                        gather(e_ + 1, 0)
                    y.free = [add_done()]
                    block_in(e_, j, g)
                    if j + 1 < NB:
                        gather_done(e_, j + 1)
                    downs_ = [] if first else list(range(HT))
                    before_e = e_ if j else e_ - 1
                    next_weights = j == 0 and e_ + 1 < E
                    if next_weights:
                        quarters = [fetch_expert(e_ + 1, piece) for piece in range(2)]
                    for f in downs_[:3]:
                        down(before_e, f)
                    downs_ = downs_[3:]
                    for f in range(HT):
                        up(e_, f)
                        if downs_:
                            down(before_e, downs_.pop(0))
                            if not downs_:
                                block_out()
                        if j == 0 and f < 2 and fetched:
                            fetched.pop(0)()
                        if next_weights:
                            if 0 < f <= 2:
                                quarters.append(fetch_expert(e_ + 1, f + 1))
                            if f in CONVERT_AT:
                                piece = CONVERT_AT.index(f)
                                convert_expert(e_ + 1, piece, quarters[piece])
                            if f == HT - 1:
                                fetched = [prefetch.pop(0)() for _ in range(min(2, len(prefetch)))]
                    if not first:
                        add()
                for q in engines:
                    q.end_ifs()
            y.free = [add_done()]
            now_is_before()
            for f in range(HT):
                down(E - 1, f)
            block_out()
            add()
            t_done = add_done()
            routed[:] = [t_done, t_done]
            assert not prefetch
            slots.bufs = own_slots
            st.close()
            return t_done

        routed_0 = attention(0, Operands(0, []), [], t["x"], [])
        ops_1 = Operands(1, routed_0[0])
        ahead = [lambda i=i: ops_1.fetch_weights(i, dve, dve) for i in range(t["aw1"].shape[1] // STAGE)]
        done = experts(0, *routed_0, [*ahead, *ops_1.context(0, dve, dve)])
        routed_1 = attention(1, ops_1, barrier(), acc_d[0], [done])
        done = experts(1, *routed_1, [])

        block = ctx.enter_context(nc.Block())

        @block.sync
        def _(e):
            loads.emit(e)
            e.wait_ge(*done)

        @block.tensor
        def _(e):
            pe.emit(e)

        @block.scalar
        def _(e):
            act.emit(e)

        @block.vector
        def _(e):
            dve.emit(e)

        @block.gpsimd
        def _(e):
            pool.emit(e)


def columns(w):
    a, b = w.shape
    return w.reshape(a // P, P, b).transpose(1, 0, 2).reshape(P, -1)


def kernel(**inputs):
    import concourse.bacc as _bacc
    from concourse.bass_utils import run_bass_kernel_spmd as _run

    g = {k: np.asarray(v) for k, v in inputs.items()}
    a = {}
    a["x"] = g["x"].reshape(BATCH * TOK, D)
    ctx = g["ctx_1024"]
    padded = np.concatenate([ctx, np.repeat(ctx[:, -1:], CTXP - CTX, axis=1)], axis=1)
    a["ctx_cols"] = padded.transpose(0, 2, 1).reshape(BATCH, KD, P, CTXP).transpose(0, 2, 1, 3)
    rows = np.concatenate([ctx, np.repeat(ctx[:, -1:], CT * P - CTX, axis=1)], axis=1)
    a["ctx_rows"] = rows.reshape(BATCH, CT, P, D).transpose(0, 2, 1, 3)
    one = np.float32(1)
    pos = (np.arange(TOK, dtype=np.float32) + np.float32(0.5)) * np.float32(CTX / TOK) - np.float32(0.5)
    pos = np.clip(pos, np.float32(0), np.float32(CTX - 1))
    lo = np.floor(pos).astype(np.int32)
    hi = np.minimum(lo + 1, CTX - 1)
    share = pos - lo.astype(np.float32)
    picked = np.stack([ctx[:, lo], ctx[:, hi]], axis=1)
    a["ctx_picked"] = picked.transpose(0, 1, 3, 2).reshape(BATCH, 2, KD, P, TOK).transpose(0, 1, 3, 2, 4).reshape(
        BATCH, 2, P, KD * TOK)
    L0, L1 = "L0_xattn_", "L1_xattn_"
    a["aw0"] = np.concatenate([columns(w) for w in (
        g[L0 + "Wq_c"], g[L0 + "Wk_s"], g[L0 + "Wv_s"].T, g[L0 + "Wq_s"].T, g[L0 + "Wk_c"].T, g[L0 + "Wv_c"].T,
        g[L0 + "Wg"].T)], axis=1)
    a["aw1"] = np.concatenate([columns(w) for w in (
        g[L1 + "Wq"], g[L1 + "Wk"], g[L1 + "Wv"].T, g[L1 + "Wo"].T)], axis=1)
    a["up0"], a["down0"] = g["L0_ffn_up_w"], g["L0_ffn_down_w"]
    a["up1"], a["down1"] = g["L1_ffn_w1"], g["L1_ffn_w2"]
    a["b2"] = g["L1_ffn_b2"]

    def vec(v):
        return v.reshape(-1, P).T

    def rows_of(v):
        return np.broadcast_to(v.reshape(1, -1), (P, v.size))
    parts = {
        "bq_c": vec(g[L0 + "bq_c"]), "bv_s": vec(g[L0 + "bv_s"]), "bq_s": vec(g[L0 + "bq_s"]), "bk_c": vec(g[L0 + "bk_c"]),
        "bv_c": vec(g[L0 + "bv_c"]), "bg": vec(g[L0 + "bg"]), "bq1": vec(g[L1 + "bq"]), "bv1": vec(g[L1 + "bv"]),
        "b1": vec(g["L1_ffn_b1"]), "mixing": np.concatenate([vec(one - share), vec(share)], axis=1),
        "gates": rows_of(np.concatenate([g["g_xattn"], g["g_ffn"]])),
        "lower": rows_of(np.tril(np.ones((E, E), np.float32), -1)), "gate_b": rows_of(g["L1_ffn_gate_b"]),
        "token": (np.arange(NT, dtype=np.float32)[None, :] * P + np.arange(P, dtype=np.float32)[:, None] + 1),
        "spare": (SPARE + 1 + np.arange(BT, dtype=np.float32)[None, :] * P + np.arange(P, dtype=np.float32)[:, None]),
        "bk_s": vec(g[L0 + "bk_s"]), "bk1": vec(g[L1 + "bk"]), "router0": columns(g["L0_ffn_router_w"]),
        "router1": columns(g["L1_ffn_gate_w"]), "bo": rows_of(g[L1 + "bo"]), "ident": np.eye(P, dtype=np.float32),
    }
    a["small"] = np.concatenate([parts[n] for n, _ in _COLS], axis=1)
    a["half"] = np.concatenate([np.triu(np.ones((P, P)), 1), np.ones((P, P)), np.tile(np.arange(P), (P, 1)),
                                np.tile(np.arange(M), (P, 1))], axis=1).astype(np.float16)

    nc = _bacc.Bacc("TRN2", target_bir_lowering=False, num_devices=1)
    arrays, handles = {}, {}
    for name, v in a.items():
        v = np.ascontiguousarray(v)
        arrays[f"in_{name}"] = v
        handles[name] = nc.dram_tensor(f"in_{name}", v.shape, mybir.dt.from_np(v.dtype), kind="ExternalInput").ap()
    out = nc.dram_tensor("out_x", (ROWS, D), F32, kind="ExternalOutput").ap()
    build(nc, handles, out)
    r = _run(nc, [arrays], core_ids=[0])
    return r.results[0]["out_x"][:BATCH * TOK].reshape(BATCH, TOK, D)
```
